# Optimizing a Trainium2 kernel written in Bass

```python
import numpy as np
import jax
import jax.numpy as jnp

def _softmax(x, axis=-1):
    return jax.nn.softmax(x, axis=axis)

def _gelu(x):
    return jax.nn.gelu(x, approximate=True)

def _silu(x):
    return jax.nn.silu(x)

def _sigmoid(x):
    return jax.nn.sigmoid(x)

def _layernorm(x, axis=-1, eps=1e-05):
    m = jnp.mean(x, axis=axis, keepdims=True)
    v = jnp.var(x, axis=axis, keepdims=True)
    return (x - m) / jnp.sqrt(v + eps)

def _scatter_add(tgt, idx, src, axis=0):
    return tgt.at[idx].add(src)

def _segment_sum(src, seg, n):
    return jax.ops.segment_sum(src, seg, n)
kernel_name = 'mk_adaln_d4_jaxref_r8_0e7e2c'

def setup_inputs(seed: int=0):
    np.random.seed(seed)
    _w = jnp.asarray

    def _L0_attn_setup():
        import jax, jax.numpy as jnp
        import numpy as np
        import math
        N_EMBD = 128
        N_LAYER = 24
        LAYER_ID = 12
        B, T = (8, 256)

        def _init_params():
            C = N_EMBD
            ratio_0_to_1 = LAYER_ID / (N_LAYER - 1)
            ratio_1_to_almost0 = 1.0 - LAYER_ID / N_LAYER
            h = np.arange(C, dtype=np.float64)
            decay_speed = -5.0 + 8.0 * (h / (C - 1)) ** (0.7 + 1.3 * ratio_0_to_1)
            zigzag = ((np.arange(C) + 1) % 3 - 1) * 0.5
            time_first = np.ones(C) * math.log(0.3) + zigzag
            xline = (np.arange(C, dtype=np.float64) / C).reshape(1, 1, C)
            time_mix_k = xline ** ratio_1_to_almost0
            time_mix_v = xline ** ratio_1_to_almost0 + 0.3 * ratio_0_to_1
            time_mix_r = xline ** (0.5 * ratio_1_to_almost0)
            f32 = lambda a: jnp.asarray(a, dtype=jnp.float32)
            return (f32(decay_speed), f32(time_first), f32(time_mix_k), f32(time_mix_v), f32(time_mix_r))

        def _wkv(w, u, k, v):
            kT = jnp.swapaxes(k, 0, 1)
            vT = jnp.swapaxes(v, 0, 1)

            def step(carry, kv_t):
                p, q, o = carry
                kt, vt = kv_t
                no = jnp.maximum(o, u + kt)
                A = jnp.exp(o - no)
                Bc = jnp.exp(u + kt - no)
                y = (A * p + Bc * vt) / (A * q + Bc)
                no2 = jnp.maximum(w + o, kt)
                A2 = jnp.exp(w + o - no2)
                B2 = jnp.exp(kt - no2)
                return ((A2 * p + B2 * vt, A2 * q + B2, no2), y)
            z = jnp.zeros(k.shape[::2], dtype=k.dtype)
            init = (z, z, jnp.full_like(z, -1e+38))
            _, yT = jax.lax.scan(step, init, (kT, vT))
            return jnp.swapaxes(yT, 0, 1)
        key = jax.random.key(seed)
        kx, kk, kv, kr, ko = jax.random.split(key, 5)
        C = N_EMBD
        scale = 1.0 / np.sqrt(C)
        time_decay, time_first, tmk, tmv, tmr = _init_params()
        return {'x': jax.random.normal(kx, (B, T, C), dtype=jnp.float32), 'time_decay': time_decay, 'time_first': time_first, 'time_mix_k': tmk, 'time_mix_v': tmv, 'time_mix_r': tmr, 'W_key': jax.random.uniform(kk, (C, C), jnp.float32, -scale, scale), 'W_value': jax.random.uniform(kv, (C, C), jnp.float32, -scale, scale), 'W_receptance': jax.random.uniform(kr, (C, C), jnp.float32, -scale, scale), 'W_output': jax.random.uniform(ko, (C, C), jnp.float32, -scale, scale)}
    _L0_attn_in = _L0_attn_setup()

    def _L0_ffn_setup():
        import jax, jax.numpy as jnp
        import numpy as np
        LN_EPS = 1e-05

        def layer_norm(x, g, b):
            mu = jnp.mean(x, axis=-1, keepdims=True)
            var = jnp.mean(jnp.square(x - mu), axis=-1, keepdims=True)
            return (x - mu) * jax.lax.rsqrt(var + LN_EPS) * g + b

        def ternary_quant(w):
            scale = 1.0 / jnp.clip(jnp.mean(jnp.abs(w)), 1e-05)
            wq = jnp.clip(jnp.round(w * scale), -1.0, 1.0) / scale
            return w + jax.lax.stop_gradient(wq - w)
        key = jax.random.key(seed)
        ks = jax.random.split(key, 3)
        dim, hidden = (128, 512)
        B, S = (8, 128)
        x = jax.random.normal(ks[0], (B, S, dim), dtype=jnp.float32)
        w1 = jax.random.normal(ks[1], (hidden, dim), dtype=jnp.float32) * 0.02
        w2 = jax.random.normal(ks[2], (dim, hidden), dtype=jnp.float32) * 0.02
        return {'x': x, 'ln1_g': jnp.ones((dim,), jnp.float32), 'ln1_b': jnp.zeros((dim,), jnp.float32), 'w1': w1, 'b1': jnp.zeros((hidden,), jnp.float32), 'ln2_g': jnp.ones((hidden,), jnp.float32), 'ln2_b': jnp.zeros((hidden,), jnp.float32), 'w2': w2, 'b2': jnp.zeros((dim,), jnp.float32)}
    _L0_ffn_in = _L0_ffn_setup()
    _L0_c = _w((lambda *s: np.random.randn(*s).astype(np.float32) * 0.05)(2, 128))
    _L0_wmod = _w((lambda *s: np.random.randn(*s).astype(np.float32) * 0.05)(128, 6 * 128) * 128 ** (-0.5))

    def _L1_attn_setup():
        import jax, jax.numpy as jnp
        import numpy as np
        D_MODEL = 128
        NHEAD = 16
        HEAD_DIM = D_MODEL // NHEAD
        LN_EPS = 1e-05

        def _retention_scan(v, lam_h):
            B, L, H, DH = v.shape
            a = jnp.broadcast_to(lam_h[None, None, :, None], v.shape)

            def combine(x, y):
                a1, b1 = x
                a2, b2 = y
                return (a1 * a2, a2 * b1 + b2)
            _, states = jax.lax.associative_scan(combine, (a, v), axis=1)
            return states
        key = jax.random.key(seed)
        ks = jax.random.split(key, 6)
        B, L, D = (4, 512, D_MODEL)
        s = 1.0 / np.sqrt(D)
        return {'x': jax.random.normal(ks[0], (B, L, D), jnp.float32), 'Wq': jax.random.normal(ks[1], (D, D), jnp.float32) * s, 'Wv': jax.random.normal(ks[2], (D, D), jnp.float32) * s, 'Wg': jax.random.normal(ks[3], (D, D), jnp.float32) * s, 'Wo': jax.random.normal(ks[4], (D, D), jnp.float32) * s, 'beta': jnp.full((NHEAD,), -0.2, jnp.float32), 'ln_gamma': jnp.ones((D_MODEL,), jnp.float32), 'ln_beta': jnp.zeros((D_MODEL,), jnp.float32)}
    _L1_attn_in = _L1_attn_setup()

    def _L1_ffn_setup():
        import jax, jax.numpy as jnp
        import numpy as np
        B, S, D, E = (2, 256, 128, 8)
        key = jax.random.key(seed)
        ks = jax.random.split(key, 5)
        x = jax.random.normal(ks[0], (B, S, D), dtype=jnp.float32)
        router_w = jax.random.normal(ks[1], (E, D), dtype=jnp.float32) * 0.02
        router_b = jnp.zeros((E,), dtype=jnp.float32)
        expert_w = jax.random.normal(ks[2], (E, D, D), dtype=jnp.float32) * 0.02
        expert_b = jnp.zeros((E, D), dtype=jnp.float32)
        return {'x': x, 'router_w': router_w, 'router_b': router_b, 'expert_w': expert_w, 'expert_b': expert_b}
    _L1_ffn_in = _L1_ffn_setup()
    _L1_c = _w((lambda *s: np.random.randn(*s).astype(np.float32) * 0.05)(2, 128))
    _L1_wmod = _w((lambda *s: np.random.randn(*s).astype(np.float32) * 0.05)(128, 6 * 128) * 128 ** (-0.5))

    def _L2_attn_setup():
        import jax, jax.numpy as jnp
        import numpy as np
        NUM_HEADS = 16
        N_EMBD = 128

        def alibi_bias(num_heads: int, seq_len: int) -> jnp.ndarray:
            pos = jnp.arange(seq_len, dtype=jnp.float32)
            dgrid = pos[None, :] - pos[:, None]
            slopes = 2.0 ** (-8.0 / num_heads * (jnp.arange(num_heads, dtype=jnp.float32) + 1.0))
            bias = slopes[:, None, None] * dgrid[None, :, :]
            return jnp.where(dgrid[None, :, :] > 0, -jnp.inf, bias)
        key = jax.random.key(seed)
        k1, k2, k3 = jax.random.split(key, 3)
        B, L, E = (2, 256, N_EMBD)
        x = jax.random.normal(k1, (B, L, E), dtype=jnp.float32)
        w_in = jax.random.normal(k2, (3 * E, E), dtype=jnp.float32) * 0.02
        w_out = jax.random.normal(k3, (E, E), dtype=jnp.float32) * 0.02
        return {'x': x, 'w_in': w_in, 'w_out': w_out}
    _L2_attn_in = _L2_attn_setup()

    def _L2_ffn_setup():
        import jax, jax.numpy as jnp
        import numpy as np
        B, S, D = (4, 128, 128)
        E, K = (8, 2)
        H = 2 * D
        key = jax.random.key(seed)
        ks = jax.random.split(key, 5)
        x = jax.random.normal(ks[0], (B, S, D), dtype=jnp.float32)
        Wg = jax.random.normal(ks[1], (E, D), dtype=jnp.float32) * 0.02
        W1 = jax.random.normal(ks[2], (E, H, D), dtype=jnp.float32) * 0.02
        W2 = jax.random.normal(ks[3], (E, H, D), dtype=jnp.float32) * 0.02
        W3 = jax.random.normal(ks[4], (E, D, H), dtype=jnp.float32) * 0.02
        return {'x': x, 'Wg': Wg, 'W1': W1, 'W2': W2, 'W3': W3}
    _L2_ffn_in = _L2_ffn_setup()
    _L2_c = _w((lambda *s: np.random.randn(*s).astype(np.float32) * 0.05)(2, 128))
    _L2_wmod = _w((lambda *s: np.random.randn(*s).astype(np.float32) * 0.05)(128, 6 * 128) * 128 ** (-0.5))

    def _L3_attn_setup():
        import jax, jax.numpy as jnp
        import numpy as np
        NUM_HEADS = 16
        DEPTH = 0

        def rotate_half(x):
            x1, x2 = jnp.split(x, 2, axis=-1)
            return jnp.concatenate((-x2, x1), axis=-1)

        def rotary_tables(seq_len, rot_dim, dtype):
            inv_freq = 1.0 / 10000.0 ** (jnp.arange(0, rot_dim, 2, dtype=jnp.float32) / rot_dim)
            freqs = jnp.arange(seq_len, dtype=jnp.float32)[:, None] * inv_freq[None, :]
            emb = jnp.concatenate((freqs, freqs), axis=-1)
            return (emb.astype(dtype), jnp.cos(emb).astype(dtype), jnp.sin(emb).astype(dtype))
        key = jax.random.key(seed)
        ks = jax.random.split(key, 7)
        B, N, C = (1, 256, 128)
        hd = C // NUM_HEADS
        std_qkv = (1.0 / C) ** 0.5
        std_proj = (1.0 / (2 * C)) ** 0.5
        return {'x': jax.random.normal(ks[0], (B, N, C), dtype=jnp.float32), 'W_qkv': jax.random.normal(ks[1], (6 * C, C), dtype=jnp.float32) * std_qkv, 'W_proj': jax.random.normal(ks[2], (C, 2 * C), dtype=jnp.float32) * std_proj, 'lambda_q1': jax.random.normal(ks[3], (hd,), dtype=jnp.float32) * 0.1, 'lambda_q2': jax.random.normal(ks[4], (hd,), dtype=jnp.float32) * 0.1, 'lambda_k1': jax.random.normal(ks[5], (hd,), dtype=jnp.float32) * 0.1, 'lambda_k2': jax.random.normal(ks[6], (hd,), dtype=jnp.float32) * 0.1}
    _L3_attn_in = _L3_attn_setup()

    def _L3_ffn_setup():
        import jax, jax.numpy as jnp
        import numpy as np
        DIM = 128

        def _reference_tuple_inner(x, W_r, W_k, W_v, mu_r, mu_k):
            B, T, C = x.shape
            x_prev = jnp.concatenate([jnp.zeros((B, 1, C), x.dtype), x[:, :-1, :]], axis=1)
            xr = mu_r * x + (1.0 - mu_r) * x_prev
            xk = mu_k * x + (1.0 - mu_k) * x_prev
            r = jax.nn.sigmoid(jnp.einsum('btc,dc->btd', xr, W_r))
            k = jnp.einsum('btc,dc->btd', xk, W_k)
            k_act = jnp.square(jax.nn.relu(k))
            out = r * jnp.einsum('btc,dc->btd', k_act, W_v)
            new_state = x[:, -1, :]
            return (out, new_state)
        key = jax.random.key(seed)
        ks = jax.random.split(key, 6)
        B, T, C = (8, 256, DIM)
        x = jax.random.normal(ks[0], (B, T, C), dtype=jnp.float32)
        s = 1.0 / np.sqrt(C)
        W_r = jax.random.uniform(ks[1], (C, C), jnp.float32, -s, s)
        W_k = jax.random.uniform(ks[2], (C, C), jnp.float32, -s, s)
        W_v = jax.random.uniform(ks[3], (C, C), jnp.float32, -s, s)
        mu_r = jax.random.uniform(ks[4], (C,), jnp.float32)
        mu_k = jax.random.uniform(ks[5], (C,), jnp.float32)
        return {'x': x, 'W_r': W_r, 'W_k': W_k, 'W_v': W_v, 'mu_r': mu_r, 'mu_k': mu_k}
    _L3_ffn_in = _L3_ffn_setup()
    _L3_c = _w((lambda *s: np.random.randn(*s).astype(np.float32) * 0.05)(2, 128))
    _L3_wmod = _w((lambda *s: np.random.randn(*s).astype(np.float32) * 0.05)(128, 6 * 128) * 128 ** (-0.5))
    _d = {'L0_attn_x': _L0_attn_in['x'], 'L0_attn_time_decay': _L0_attn_in['time_decay'], 'L0_attn_time_first': _L0_attn_in['time_first'], 'L0_attn_time_mix_k': _L0_attn_in['time_mix_k'], 'L0_attn_time_mix_v': _L0_attn_in['time_mix_v'], 'L0_attn_time_mix_r': _L0_attn_in['time_mix_r'], 'L0_attn_W_key': _L0_attn_in['W_key'], 'L0_attn_W_value': _L0_attn_in['W_value'], 'L0_attn_W_receptance': _L0_attn_in['W_receptance'], 'L0_attn_W_output': _L0_attn_in['W_output'], 'L0_ffn_ln1_g': _L0_ffn_in['ln1_g'], 'L0_ffn_ln1_b': _L0_ffn_in['ln1_b'], 'L0_ffn_w1': _L0_ffn_in['w1'], 'L0_ffn_b1': _L0_ffn_in['b1'], 'L0_ffn_ln2_g': _L0_ffn_in['ln2_g'], 'L0_ffn_ln2_b': _L0_ffn_in['ln2_b'], 'L0_ffn_w2': _L0_ffn_in['w2'], 'L0_ffn_b2': _L0_ffn_in['b2'], 'L0_c': _L0_c, 'L0_wmod': _L0_wmod, 'L1_attn_Wq': _L1_attn_in['Wq'], 'L1_attn_Wv': _L1_attn_in['Wv'], 'L1_attn_Wg': _L1_attn_in['Wg'], 'L1_attn_Wo': _L1_attn_in['Wo'], 'L1_attn_beta': _L1_attn_in['beta'], 'L1_attn_ln_gamma': _L1_attn_in['ln_gamma'], 'L1_attn_ln_beta': _L1_attn_in['ln_beta'], 'L1_ffn_router_w': _L1_ffn_in['router_w'], 'L1_ffn_router_b': _L1_ffn_in['router_b'], 'L1_ffn_expert_w': _L1_ffn_in['expert_w'], 'L1_ffn_expert_b': _L1_ffn_in['expert_b'], 'L1_c': _L1_c, 'L1_wmod': _L1_wmod, 'L2_attn_w_in': _L2_attn_in['w_in'], 'L2_attn_w_out': _L2_attn_in['w_out'], 'L2_ffn_Wg': _L2_ffn_in['Wg'], 'L2_ffn_W1': _L2_ffn_in['W1'], 'L2_ffn_W2': _L2_ffn_in['W2'], 'L2_ffn_W3': _L2_ffn_in['W3'], 'L2_c': _L2_c, 'L2_wmod': _L2_wmod, 'L3_attn_W_qkv': _L3_attn_in['W_qkv'], 'L3_attn_W_proj': _L3_attn_in['W_proj'], 'L3_attn_lambda_q1': _L3_attn_in['lambda_q1'], 'L3_attn_lambda_q2': _L3_attn_in['lambda_q2'], 'L3_attn_lambda_k1': _L3_attn_in['lambda_k1'], 'L3_attn_lambda_k2': _L3_attn_in['lambda_k2'], 'L3_ffn_W_r': _L3_ffn_in['W_r'], 'L3_ffn_W_k': _L3_ffn_in['W_k'], 'L3_ffn_W_v': _L3_ffn_in['W_v'], 'L3_ffn_mu_r': _L3_ffn_in['mu_r'], 'L3_ffn_mu_k': _L3_ffn_in['mu_k'], 'L3_c': _L3_c, 'L3_wmod': _L3_wmod}
    _x0 = _d['L0_attn_x']
    _d['L0_attn_x'] = jax.random.normal(jax.random.fold_in(jax.random.key(seed), 1), (2, 1024, 128), dtype=_x0.dtype)
    del _x0
    return _d

def reference(L0_attn_x, L0_attn_time_decay, L0_attn_time_first, L0_attn_time_mix_k, L0_attn_time_mix_v, L0_attn_time_mix_r, L0_attn_W_key, L0_attn_W_value, L0_attn_W_receptance, L0_attn_W_output, L0_ffn_ln1_g, L0_ffn_ln1_b, L0_ffn_w1, L0_ffn_b1, L0_ffn_ln2_g, L0_ffn_ln2_b, L0_ffn_w2, L0_ffn_b2, L0_c, L0_wmod, L1_attn_Wq, L1_attn_Wv, L1_attn_Wg, L1_attn_Wo, L1_attn_beta, L1_attn_ln_gamma, L1_attn_ln_beta, L1_ffn_router_w, L1_ffn_router_b, L1_ffn_expert_w, L1_ffn_expert_b, L1_c, L1_wmod, L2_attn_w_in, L2_attn_w_out, L2_ffn_Wg, L2_ffn_W1, L2_ffn_W2, L2_ffn_W3, L2_c, L2_wmod, L3_attn_W_qkv, L3_attn_W_proj, L3_attn_lambda_q1, L3_attn_lambda_q2, L3_attn_lambda_k1, L3_attn_lambda_k2, L3_ffn_W_r, L3_ffn_W_k, L3_ffn_W_v, L3_ffn_mu_r, L3_ffn_mu_k, L3_c, L3_wmod):

    def _L0_attn_ref(x, time_decay, time_first, time_mix_k, time_mix_v, time_mix_r, W_key, W_value, W_receptance, W_output):
        import jax, jax.numpy as jnp
        import numpy as np
        import math
        N_EMBD = 128
        N_LAYER = 24
        LAYER_ID = 12
        B, T = (8, 256)

        def _init_params():
            C = N_EMBD
            ratio_0_to_1 = LAYER_ID / (N_LAYER - 1)
            ratio_1_to_almost0 = 1.0 - LAYER_ID / N_LAYER
            h = np.arange(C, dtype=np.float64)
            decay_speed = -5.0 + 8.0 * (h / (C - 1)) ** (0.7 + 1.3 * ratio_0_to_1)
            zigzag = ((np.arange(C) + 1) % 3 - 1) * 0.5
            time_first = np.ones(C) * math.log(0.3) + zigzag
            xline = (np.arange(C, dtype=np.float64) / C).reshape(1, 1, C)
            time_mix_k = xline ** ratio_1_to_almost0
            time_mix_v = xline ** ratio_1_to_almost0 + 0.3 * ratio_0_to_1
            time_mix_r = xline ** (0.5 * ratio_1_to_almost0)
            f32 = lambda a: jnp.asarray(a, dtype=jnp.float32)
            return (f32(decay_speed), f32(time_first), f32(time_mix_k), f32(time_mix_v), f32(time_mix_r))

        def _wkv(w, u, k, v):
            kT = jnp.swapaxes(k, 0, 1)
            vT = jnp.swapaxes(v, 0, 1)

            def step(carry, kv_t):
                p, q, o = carry
                kt, vt = kv_t
                no = jnp.maximum(o, u + kt)
                A = jnp.exp(o - no)
                Bc = jnp.exp(u + kt - no)
                y = (A * p + Bc * vt) / (A * q + Bc)
                no2 = jnp.maximum(w + o, kt)
                A2 = jnp.exp(w + o - no2)
                B2 = jnp.exp(kt - no2)
                return ((A2 * p + B2 * vt, A2 * q + B2, no2), y)
            z = jnp.zeros(k.shape[::2], dtype=k.dtype)
            init = (z, z, jnp.full_like(z, -1e+38))
            _, yT = jax.lax.scan(step, init, (kT, vT))
            return jnp.swapaxes(yT, 0, 1)
        xx = jnp.concatenate([jnp.zeros_like(x[:, :1]), x[:, :-1]], axis=1)
        xk = x * time_mix_k + xx * (1.0 - time_mix_k)
        xv = x * time_mix_v + xx * (1.0 - time_mix_v)
        xr = x * time_mix_r + xx * (1.0 - time_mix_r)
        k = jnp.einsum('btc,dc->btd', xk, W_key)
        v = jnp.einsum('btc,dc->btd', xv, W_value)
        r = jnp.einsum('btc,dc->btd', xr, W_receptance)
        sr = jax.nn.sigmoid(r)
        w = -jnp.exp(time_decay)
        wkv = _wkv(w, time_first, k, v)
        return jnp.einsum('btc,dc->btd', sr * wkv, W_output)

    def _L0_ffn_ref(x, ln1_g, ln1_b, w1, b1, ln2_g, ln2_b, w2, b2):
        import jax, jax.numpy as jnp
        import numpy as np
        LN_EPS = 1e-05

        def layer_norm(x, g, b):
            mu = jnp.mean(x, axis=-1, keepdims=True)
            var = jnp.mean(jnp.square(x - mu), axis=-1, keepdims=True)
            return (x - mu) * jax.lax.rsqrt(var + LN_EPS) * g + b

        def ternary_quant(w):
            scale = 1.0 / jnp.clip(jnp.mean(jnp.abs(w)), 1e-05)
            wq = jnp.clip(jnp.round(w * scale), -1.0, 1.0) / scale
            return w + jax.lax.stop_gradient(wq - w)
        h = layer_norm(x, ln1_g, ln1_b)
        h = jnp.einsum('bsd,hd->bsh', h, ternary_quant(w1)) + b1
        h = jax.nn.gelu(h, approximate=False)
        h = layer_norm(h, ln2_g, ln2_b)
        out = jnp.einsum('bsh,dh->bsd', h, ternary_quant(w2)) + b2
        return out

    def _L1_attn_ref(x, Wq, Wv, Wg, Wo, beta, ln_gamma, ln_beta):
        import jax, jax.numpy as jnp
        import numpy as np
        D_MODEL = 128
        NHEAD = 16
        HEAD_DIM = D_MODEL // NHEAD
        LN_EPS = 1e-05

        def _retention_scan(v, lam_h):
            B, L, H, DH = v.shape
            a = jnp.broadcast_to(lam_h[None, None, :, None], v.shape)

            def combine(x, y):
                a1, b1 = x
                a2, b2 = y
                return (a1 * a2, a2 * b1 + b2)
            _, states = jax.lax.associative_scan(combine, (a, v), axis=1)
            return states
        B, L, D = x.shape
        H, DH = (NHEAD, HEAD_DIM)
        q = (x @ Wq.T).reshape(B, L, H, DH)
        v = (x @ Wv.T).reshape(B, L, H, DH)
        lam_h = jax.nn.sigmoid(beta)
        state = _retention_scan(v, lam_h)
        y = (q * state).reshape(B, L, D)
        mu = jnp.mean(y, axis=-1, keepdims=True)
        var = jnp.mean((y - mu) ** 2, axis=-1, keepdims=True)
        y = (y - mu) * jax.lax.rsqrt(var + LN_EPS) * ln_gamma + ln_beta
        gate = jax.nn.silu(x @ Wg.T)
        y = y * gate
        return y @ Wo.T

    def _L1_ffn_ref(x, router_w, router_b, expert_w, expert_b):
        import jax, jax.numpy as jnp
        import numpy as np
        B, S, D, E = (2, 256, 128, 8)
        logits = jnp.einsum('bsd,ed->bse', x, router_w) + router_b
        probs = jax.nn.softmax(logits, axis=-1)
        weights = jnp.max(probs, axis=-1)
        top1 = jnp.argmax(probs, axis=-1)
        y_all = jnp.einsum('bsd,eod->bseo', x, expert_w) + expert_b
        y = jnp.take_along_axis(y_all, top1[:, :, None, None], axis=2)[:, :, 0, :]
        out = y * weights[:, :, None]
        return out

    def _L2_attn_ref(x, w_in, w_out):
        import jax, jax.numpy as jnp
        import numpy as np
        NUM_HEADS = 16
        N_EMBD = 128

        def alibi_bias(num_heads: int, seq_len: int) -> jnp.ndarray:
            pos = jnp.arange(seq_len, dtype=jnp.float32)
            dgrid = pos[None, :] - pos[:, None]
            slopes = 2.0 ** (-8.0 / num_heads * (jnp.arange(num_heads, dtype=jnp.float32) + 1.0))
            bias = slopes[:, None, None] * dgrid[None, :, :]
            return jnp.where(dgrid[None, :, :] > 0, -jnp.inf, bias)
        B, L, E = x.shape
        H = NUM_HEADS
        D = E // H
        qkv = jnp.einsum('ble,fe->blf', x, w_in)
        q, k, v = jnp.split(qkv, 3, axis=-1)

        def to_heads(t):
            return t.reshape(B, L, H, D).transpose(0, 2, 1, 3)
        q, k, v = (to_heads(q), to_heads(k), to_heads(v))
        scale = 1.0 / jnp.sqrt(jnp.asarray(D, dtype=x.dtype))
        scores = jnp.einsum('bhqd,bhkd->bhqk', q, k) * scale
        scores = scores + alibi_bias(H, L)[None]
        attn = jax.nn.softmax(scores, axis=-1)
        ctx = jnp.einsum('bhqk,bhkd->bhqd', attn, v)
        ctx = ctx.transpose(0, 2, 1, 3).reshape(B, L, E)
        return jnp.einsum('ble,fe->blf', ctx, w_out)

    def _L2_ffn_ref(x, Wg, W1, W2, W3):
        import jax, jax.numpy as jnp
        import numpy as np
        B, S, D = (4, 128, 128)
        E, K = (8, 2)
        H = 2 * D
        gate_out = jnp.einsum('bsd,ed->bse', x, Wg)
        top_v, top_i = jax.lax.top_k(gate_out, K)
        probs = jax.nn.softmax(top_v, axis=-1)
        out = jnp.zeros_like(x)
        for e in range(E):
            w_e = jnp.sum(probs * (top_i == e), axis=-1)
            h1 = jnp.einsum('bsd,hd->bsh', x, W1[e])
            h2 = jnp.einsum('bsd,hd->bsh', x, W2[e])
            g = h1 * jax.nn.sigmoid(h1) * h2
            y = jnp.einsum('bsh,dh->bsd', g, W3[e])
            out = out + y * w_e[..., None]
        return out

    def _L3_attn_ref(x, W_qkv, W_proj, lambda_q1, lambda_q2, lambda_k1, lambda_k2):
        import jax, jax.numpy as jnp
        import numpy as np
        NUM_HEADS = 16
        DEPTH = 0

        def rotate_half(x):
            x1, x2 = jnp.split(x, 2, axis=-1)
            return jnp.concatenate((-x2, x1), axis=-1)

        def rotary_tables(seq_len, rot_dim, dtype):
            inv_freq = 1.0 / 10000.0 ** (jnp.arange(0, rot_dim, 2, dtype=jnp.float32) / rot_dim)
            freqs = jnp.arange(seq_len, dtype=jnp.float32)[:, None] * inv_freq[None, :]
            emb = jnp.concatenate((freqs, freqs), axis=-1)
            return (emb.astype(dtype), jnp.cos(emb).astype(dtype), jnp.sin(emb).astype(dtype))
        B, N, C = x.shape
        H = NUM_HEADS
        hd = C // H
        scale = hd ** (-0.5)
        lambda_init = 0.8 - 0.6 * np.exp(-0.3 * DEPTH)
        qkv = jnp.einsum('bnc,dc->bnd', x, W_qkv)
        qkv = qkv.reshape(B, N, 6, H, hd).transpose(2, 0, 3, 1, 4)
        q = jnp.concatenate((qkv[0], qkv[1]), axis=-1)
        k = jnp.concatenate((qkv[2], qkv[3]), axis=-1)
        v = jnp.concatenate((qkv[4], qkv[5]), axis=-1)
        _, cos, sin = rotary_tables(N, 2 * hd, x.dtype)
        q = q * cos + rotate_half(q) * sin
        k = k * cos + rotate_half(k) * sin
        q1, q2 = jnp.split(q, 2, axis=-1)
        k1, k2 = jnp.split(k, 2, axis=-1)
        attn1 = jnp.einsum('bhid,bhjd->bhij', q1, k1) * scale
        attn2 = jnp.einsum('bhid,bhjd->bhij', q2, k2) * scale
        lam1 = jnp.exp(jnp.sum(lambda_q1 * lambda_k1))
        lam2 = jnp.exp(jnp.sum(lambda_q2 * lambda_k2))
        lam = (lam1 - lam2 + lambda_init).astype(x.dtype)
        probs = jax.nn.softmax(attn1, axis=-1) - lam * jax.nn.softmax(attn2, axis=-1)
        out = jnp.einsum('bhij,bhjd->bhid', probs, v)
        out = out.transpose(0, 2, 1, 3).reshape(B, N, 2 * C)
        out = jnp.einsum('bnd,cd->bnc', out, W_proj)
        return out

    def _L3_ffn_ref(x, W_r, W_k, W_v, mu_r, mu_k):
        import jax, jax.numpy as jnp
        import numpy as np
        DIM = 128

        def _reference_tuple_inner(x, W_r, W_k, W_v, mu_r, mu_k):
            B, T, C = x.shape
            x_prev = jnp.concatenate([jnp.zeros((B, 1, C), x.dtype), x[:, :-1, :]], axis=1)
            xr = mu_r * x + (1.0 - mu_r) * x_prev
            xk = mu_k * x + (1.0 - mu_k) * x_prev
            r = jax.nn.sigmoid(jnp.einsum('btc,dc->btd', xr, W_r))
            k = jnp.einsum('btc,dc->btd', xk, W_k)
            k_act = jnp.square(jax.nn.relu(k))
            out = r * jnp.einsum('btc,dc->btd', k_act, W_v)
            new_state = x[:, -1, :]
            return (out, new_state)
        return _reference_tuple_inner(x, W_r, W_k, W_v, mu_r, mu_k)[0]
    x = L0_attn_x
    mod = (_silu(L0_c) @ L0_wmod).reshape(L0_c.shape[0], 6, 1, -1)
    sa, ca, ga, sb, cb, gb = (mod[:, 0], mod[:, 1], mod[:, 2], mod[:, 3], mod[:, 4], mod[:, 5])
    ga = (2 * (ga >= 0) - 1) * jnp.maximum(jnp.abs(ga), 0.25)
    gb = (2 * (gb >= 0) - 1) * jnp.maximum(jnp.abs(gb), 0.25)
    h = _layernorm(x, axis=-1) * (1 + ca) + sa
    x = x + ga * _L0_attn_ref(h, L0_attn_time_decay, L0_attn_time_first, L0_attn_time_mix_k, L0_attn_time_mix_v, L0_attn_time_mix_r, L0_attn_W_key, L0_attn_W_value, L0_attn_W_receptance, L0_attn_W_output)
    h = _layernorm(x, axis=-1) * (1 + cb) + sb
    x = x + gb * _L0_ffn_ref(h, L0_ffn_ln1_g, L0_ffn_ln1_b, L0_ffn_w1, L0_ffn_b1, L0_ffn_ln2_g, L0_ffn_ln2_b, L0_ffn_w2, L0_ffn_b2)
    mod = (_silu(L1_c) @ L1_wmod).reshape(L1_c.shape[0], 6, 1, -1)
    sa, ca, ga, sb, cb, gb = (mod[:, 0], mod[:, 1], mod[:, 2], mod[:, 3], mod[:, 4], mod[:, 5])
    ga = (2 * (ga >= 0) - 1) * jnp.maximum(jnp.abs(ga), 0.25)
    gb = (2 * (gb >= 0) - 1) * jnp.maximum(jnp.abs(gb), 0.25)
    h = _layernorm(x, axis=-1) * (1 + ca) + sa
    x = x + ga * _L1_attn_ref(h, L1_attn_Wq, L1_attn_Wv, L1_attn_Wg, L1_attn_Wo, L1_attn_beta, L1_attn_ln_gamma, L1_attn_ln_beta)
    h = _layernorm(x, axis=-1) * (1 + cb) + sb
    x = x + gb * _L1_ffn_ref(h, L1_ffn_router_w, L1_ffn_router_b, L1_ffn_expert_w, L1_ffn_expert_b)
    mod = (_silu(L2_c) @ L2_wmod).reshape(L2_c.shape[0], 6, 1, -1)
    sa, ca, ga, sb, cb, gb = (mod[:, 0], mod[:, 1], mod[:, 2], mod[:, 3], mod[:, 4], mod[:, 5])
    ga = (2 * (ga >= 0) - 1) * jnp.maximum(jnp.abs(ga), 0.25)
    gb = (2 * (gb >= 0) - 1) * jnp.maximum(jnp.abs(gb), 0.25)
    h = _layernorm(x, axis=-1) * (1 + ca) + sa
    x = x + ga * _L2_attn_ref(h, L2_attn_w_in, L2_attn_w_out)
    h = _layernorm(x, axis=-1) * (1 + cb) + sb
    x = x + gb * _L2_ffn_ref(h, L2_ffn_Wg, L2_ffn_W1, L2_ffn_W2, L2_ffn_W3)
    mod = (_silu(L3_c) @ L3_wmod).reshape(L3_c.shape[0], 6, 1, -1)
    sa, ca, ga, sb, cb, gb = (mod[:, 0], mod[:, 1], mod[:, 2], mod[:, 3], mod[:, 4], mod[:, 5])
    ga = (2 * (ga >= 0) - 1) * jnp.maximum(jnp.abs(ga), 0.25)
    gb = (2 * (gb >= 0) - 1) * jnp.maximum(jnp.abs(gb), 0.25)
    h = _layernorm(x, axis=-1) * (1 + ca) + sa
    x = x + ga * _L3_attn_ref(h, L3_attn_W_qkv, L3_attn_W_proj, L3_attn_lambda_q1, L3_attn_lambda_q2, L3_attn_lambda_k1, L3_attn_lambda_k2)
    h = _layernorm(x, axis=-1) * (1 + cb) + sb
    x = x + gb * _L3_ffn_ref(h, L3_ffn_W_r, L3_ffn_W_k, L3_ffn_W_v, L3_ffn_mu_r, L3_ffn_mu_k)
    return x

_drawn_inputs = setup_inputs


def setup_inputs(seed=0):
    import zlib

    import numpy as np

    out = dict(_drawn_inputs(seed))
    spreads = {'L0_ffn_ln1_g': (1.0, 0.6),
     'L0_ffn_ln1_b': (0.0, 0.8),
     'L0_ffn_b1': (0.0, 0.1),
     'L0_ffn_ln2_g': (1.0, 0.6),
     'L0_ffn_ln2_b': (0.0, 0.8),
     'L0_ffn_b2': (0.0, 0.301),
     'L1_attn_beta': (-0.20000000298023224, 0.6),
     'L1_attn_ln_gamma': (1.0, 0.574),
     'L1_attn_ln_beta': (0.0, 0.525),
     'L1_ffn_router_b': (0.0, 0.8),
     'L1_ffn_expert_b': (0.0, 0.8)}
    factors = {'L0_attn_time_decay': 3.32,
     'L0_attn_time_first': 8.0,
     'L0_attn_time_mix_k': 8.0,
     'L0_attn_time_mix_v': 8.0,
     'L0_attn_time_mix_r': 8.0,
     'L0_attn_W_key': 8.0,
     'L0_attn_W_value': 2.802,
     'L0_attn_W_receptance': 8.0,
     'L0_attn_W_output': 2.801,
     'L1_ffn_router_w': 5.62,
     'L1_ffn_expert_w': 5.539,
     'L2_attn_w_in': 8.0,
     'L2_attn_w_out': 8.0,
     'L2_ffn_Wg': 8.0,
     'L2_ffn_W1': 8.0,
     'L2_ffn_W2': 8.0,
     'L2_ffn_W3': 8.0,
     'L2_c': 8.0,
     'L2_wmod': 8.0,
     'L3_attn_lambda_q1': 8.0,
     'L3_attn_lambda_q2': 47.096,
     'L3_attn_lambda_k1': 30.746,
     'L3_attn_lambda_k2': 8.0,
     'L3_ffn_W_r': 8.0,
     'L3_ffn_W_k': 3.006,
     'L3_ffn_W_v': 2.795,
     'L3_ffn_mu_r': 8.0,
     'L3_ffn_mu_k': 4.725,
     'L3_attn_W_qkv': 3.045,
     'L3_attn_W_proj': 3.091}
    for name, (base, spread) in spreads.items():
        noise = np.random.default_rng([zlib.crc32(name.encode()), seed]).standard_normal(out[name].shape)
        drawn = base * np.exp(spread * noise) if base else spread * noise
        out[name] = jnp.asarray(drawn.astype(out[name].dtype))
    for name, factor in factors.items():
        out[name] = (out[name] * factor).astype(out[name].dtype)
    return out
```

```python
from contextlib import ExitStack

import numpy as np

import concourse.bass as bass
from concourse import mybir

F32 = mybir.dt.float32
BF16 = mybir.dt.bfloat16
ALU = mybir.AluOpType
ACT = mybir.ActivationFunctionType
AX = mybir.AxisListType

P = 128
B, SEQ, C = 2, 1024, 128
TOK = B * SEQ
NT = TOK // P
CH = 512
NCH = TOK // CH
TPC = CH // P
CPB = SEQ // CH
E = 8
H1 = 512
HE = 2 * C
HEADS, HD = 16, 8
EPS = 1e-5
LOWEST = -1e38
ROUND = 12582912.0
MASKED = -1e30
LAMBDA_INIT = 0.8 - 0.6 * float(np.exp(-0.3 * 0))

WEIGHTS = {
    0: [("wmod", 6 * C), ("key", C), ("value", C), ("recept", C), ("out", C), ("w1", H1), ("w2", H1)],
    1: [("wmod", 6 * C), ("q", C), ("v", C), ("g", C), ("out", C), ("router", E), ("expert", E * C)],
    2: [("wmod", 6 * C), ("q", C), ("k", C), ("v", C), ("out", C), ("router", E),
        ("w1", E * HE), ("w2", E * HE), ("w3", E * HE)],
    3: [("wmod", 6 * C), ("q0", C), ("q1", C), ("k0", C), ("k1", C), ("v", 2 * C), ("out", 2 * C),
        ("wr", C), ("wk", C), ("wv", C)],
}
COLUMNS = [("c", 8), ("decay", 1), ("first", 1), ("mix_k", 1), ("mix_v", 1), ("mix_r", 1), ("ln1_g", 1),
           ("ln1_b", 1), ("ln2_g", 4), ("ln2_b", 4), ("b2", 1), ("beta", 1), ("gamma", 1), ("lnb", 1),
           ("mu_r", 1), ("mu_k", 1)]


def places(items):
    at, out = 0, {}
    for name, width in items:
        out[name] = (at, width)
        at += width
    return out, at


PAIRS_Q = [0, 1, 2, 0, 1, 0]
PAIRS_K = [0, 0, 0, 1, 1, 2]
ROWS = HD * len(PAIRS_Q)
HALF = 64
SLOTS = 4
SETS = 2 * SLOTS
QT = SEQ // P


class Attention:

    def __init__(self, name, heads, width, causal, groups):
        self.name, self.heads, self.width, self.causal, self.groups = name, heads, width, causal, groups
        self.max_rows = ROWS + (3 if causal else 0)
        self.all_rows = self.max_rows + 3
        self.batches = []
        for qc in range(CPB):
            for i in range(2):
                for kt in range(0, TPC * (qc + 1) if causal else QT, 2):
                    first = max(0, kt - TPC * qc) * P if causal else 0
                    self.batches.append((qc, i, kt, first))
        self.nbatch = len(self.batches)
        self.nsteps = SLOTS * self.nbatch
        self.pieces = []
        for qt in range(QT):
            for s in range(SLOTS):
                for i in (1, 0):
                    keys = P * (qt + 1) if causal else SEQ
                    for pc in range(-(-keys // CH)):
                        self.pieces.append((i, s, qt, pc, min(CH, keys - pc * CH)))
        self.npieces = len(self.pieces)


A2 = Attention("a2", 8, HD, True, 4)
A3 = Attention("a3", 4, 2 * HD, False, 8)


def adaln_stack(nc, x_in, w_in, columns_in, rows_in, expertb_in, ident_in, rope_in, masks_in, alibi_in,
                ones_in, out):
    wplace = {layer: places(items)[0] for layer, items in WEIGHTS.items()}
    wwidth = {layer: places(items)[1] - 6 * C for layer, items in WEIGHTS.items()}
    col_at, ncols = places(COLUMNS)

    with ExitStack() as ctx:
        def sb(name, shape, dt=F32):
            return ctx.enter_context(nc.sbuf_tensor(name, shape, dt))

        def sem(name):
            return ctx.enter_context(nc.semaphore(name))

        x_tok = sb("x_tok", [P, NT, C])
        xn = sb("xn", [P, NT, C])
        hT = sb("hT", [P, B, SEQ + 1])
        hF = hT[:].rearrange("p b s -> p (b s)")[:, 0:TOK]
        work = sb("work", [P, 12 * TOK])
        w02 = sb("w02", [P, wwidth[2]])
        w13 = sb("w13", [P, wwidth[1] + wwidth[3]])
        cols = sb("cols", [P, ncols])
        rowc = sb("rowc", [P, H1 + 2 * E + 4 * HD])
        expertb = sb("expertb", [E, C])
        ident = sb("ident", [P, P])
        ident16 = sb("ident16", [P, P], BF16)
        mask16 = sb("mask16", [P, 3 * P], BF16)
        ones = sb("ones", [P, P])
        mod = sb("mod", [P, 4, 6, B])
        modx = sb("modx", [P, 4, 2, B])
        silc = sb("silc", [P, 8])
        stats = sb("stats", [P, NT, 6])
        mv = sb("mv", [P, NT, 2])
        var = sb("var", [P, NT])
        rstd = sb("rstd", [P, NT])
        mhalf = sb("mhalf", [P, NT])
        small = sb("small", [P, 64])
        route = sb("route", [P, 8, NT * E])
        rone = sb("rone", [P, 6, NT])
        mcol = sb("mcol", [P, SETS * QT, 2])
        negm = sb("negm", [P, P])
        mrest = sb("mrest", [SETS * QT, P])
        mpart = sb("mpart", [SETS * QT, 3, P], BF16)
        rz = sb("rz", [P, TPC * SLOTS])
        qs = sb("qs", [P, 2, SLOTS, SEQ], BF16)
        ks = sb("ks", [P, 2, SLOTS, SEQ], BF16)
        ps = ctx.enter_context(nc.psum_tensor("ps", [P, 8, CH], F32))

        def arr(n):
            return work[:, n * TOK:(n + 1) * TOK]

        def w(layer, name):
            at, width = wplace[layer][name]
            at -= 6 * C
            if layer in (0, 2):
                return w02[:, at:at + width]
            at += wwidth[1] if layer == 3 else 0
            return w13[:, at:at + width]

        def col(name, j=0):
            at = col_at[name][0] + j
            return cols[:, at:at + 1]

        b1_row = rowc[:, 0:H1]
        routerb_row = rowc[:, H1:H1 + E]
        tie_row = rowc[:, H1 + E:H1 + 2 * E]
        lam_rows = rowc[:, H1 + 2 * E:]

        def dram(name, shape, dt=F32):
            return nc.dram_tensor(name, shape, dt, kind="Internal").ap()

        gates1 = dram("gates1", [NT, E, P])
        gates2 = dram("gates2", [NT, E, P])
        qd2 = dram("qd2", [1, A2.groups, 3, A2.heads * HD, SEQ], BF16)
        kd2 = dram("kd2", [1, A2.groups, 3, A2.heads * HD, SEQ], BF16)
        qd3 = dram("qd3", [2, A3.groups, 3, A3.heads * HD, SEQ], BF16)
        kd3 = dram("kd3", [2, A3.groups, 3, A3.heads * HD, SEQ], BF16)

        S = {}

        def s(name):
            if name not in S:
                S[name] = sem(name)
            return S[name]

        wmod = work[:, 0:4 * 6 * C].rearrange("p (l n) -> p l n", l=4)
        pslots = work[:, 0:8 * 2 * CH].rearrange("p (n k q) -> p n k q", n=8, k=2)
        vall = work[:, 4 * TOK:8 * TOK]
        vgrp = work[:, 8 * TOK:10 * TOK].rearrange("p (u n) -> p u n", u=2)
        otok = work[:, 10 * TOK:12 * TOK]

        def group_v(a):
            n = SETS if a.causal else SLOTS
            return (vall.rearrange("p (g k n d) -> p g k n d", g=a.groups, k=QT, n=n),
                    [vgrp[:, u, 0:QT * n * 32].rearrange("p (k n d) -> p k n d", k=QT, n=n) for u in range(2)])

        LN = {"a0": 0, "b0": 1, "in0": 2, "a1": 3, "y1": 4, "b1": 5, "a2": 6, "b2": 7, "a3": 8, "b3": 9}
        OUT = {"a0": 0, "b0": 1, "a1": 2, "b1": 3, "a2": 4, "b2": 5, "a3": 6, "b3": 7}
        OUT_MM = {"a0": 0, "b0": 1, "a1": 2, "b1": 3, "a2": 4, "a3": 5, "b3": 6}

        def hid(n):
            return work[:, TOK + (n % 8) * H1:TOK + (n % 8 + 1) * H1]

        def hid_T(c):
            return arr(3 + c % 2).rearrange("p (j t) -> p j t", j=4)

        def parts_ring(slot):
            return arr(2 + slot // 2)[:, (slot % 2) * 1024:(slot % 2) * 1024 + 768].bitcast(BF16).rearrange(
                "p (n t) -> p n t", n=3)

        def side(k):
            return xn[:].rearrange("p t c -> p (t c)")[:, k * CH:(k + 1) * CH]

        def o_tile(a, t, hf):
            at = ((t // QT * halves_of(a) + hf) * QT + t % QT) * P
            return otok[:, at:at + P]

        def halves_of(a):
            return 1 if a.causal else 2

        def wkv_temp(b, k):
            n = 4 * b + k
            if n < 4:
                return work[:, 9 * TOK + n * SEQ:9 * TOK + (n + 1) * SEQ]
            if n < 6:
                return xn[:].rearrange("p t c -> p (t c)")[:, (n - 4) * SEQ:(n - 3) * SEQ]
            return work[:, 768:768 + SEQ] if n == 6 else work[:, 9 * TOK - SEQ:9 * TOK]

        def wkv_state(k):
            at = 5 * TOK + k * B * (SEQ + 1)
            return work[:, at:at + B * (SEQ + 1)].rearrange("p (b s) -> p b s", b=B)

        def roped(unit):
            return arr(1)[:, (unit % 4) * CH:(unit % 4 + 1) * CH]

        def rest(unit):
            return arr(11)[:, (unit % 2) * CH:(unit % 2 + 1) * CH]

        block = ctx.enter_context(nc.Block())

        def tok(c):
            return slice(c * CH, (c + 1) * CH)

        def h_chunk(c, shift=0):
            b, o = c // CPB, (c % CPB) * CH
            return hT[:, b, 1 + o - shift:1 + o - shift + CH]

        def attention_transfers(sp, a, qd, kd):
            n = a.name
            narr = 1 if a.causal else 2
            per_b = a.groups // B
            rows = a.heads * HD
            units = [(ar, c) for c in range(NCH) for ar in range(2 * narr)]
            for unit, (ar, c) in enumerate(units):
                b, o = c // CPB, (c % CPB) * CH
                dst = (qd, kd)[ar // narr]
                sp.wait_ge(s(n + "_parts"), unit + 1)
                for hg in range(per_b):
                    sp.dma_start(dst[ar % narr, per_b * b + hg, :, :, o:o + CH].rearrange("p r t -> r p t"),
                                 parts_ring(unit % 4)[rows * hg:rows * (hg + 1)]).then_inc(s(f"{n}_st{unit % 4}"), 16)
            for slot in range(4):
                sp.wait_ge(s(f"{n}_st{slot}"), 16 * per_b * (len(units) // 4))
            for u in range(2):
                for i in range(2):
                    r = HALF * i + ROWS
                    if a.causal:
                        sp.dma_start(qs[r:r + 3, u].rearrange("p n t -> p (n t)"), ones_in).then_inc(s(n + "_ones"), 16)
                        sp.dma_start(ks[r + 3:r + 6, u].rearrange("p n t -> p (n t)"), ones_in).then_inc(s(n + "_ones"), 16)
                    else:
                        sp.dma_start(ks[r:r + 3, u].rearrange("p n t -> p (n t)"), ones_in).then_inc(s(n + "_ones"), 16)
            va, vg = group_v(a)
            vflat = va.rearrange("p g k n d -> p g (k n d)")

            def load(g, u):
                for i in range(2):
                    r = HALF * i
                    half, first = (0, SLOTS * HD * i) if a.causal else (i, 0)
                    for stack, src, pairs in ((qs, qd, PAIRS_Q), (ks, kd, PAIRS_K)):
                        for j, part in enumerate(pairs):
                            sp.dma_start(stack[r + HD * j:r + HD * (j + 1), u],
                                         src[half, bass.ds(g, 1), part, first:first + SLOTS * HD, :].rearrange(
                                             "g (n d) t -> (g d) n t", d=HD)).then_inc(s(f"{n}_ld{u}"), 16)
                    if a.causal:
                        hg = g % 2
                        sp.dma_start(ks[r + ROWS:r + ROWS + 3, u],
                                     alibi_in[:, a.heads * hg + SLOTS * i:a.heads * hg + SLOTS * (i + 1), :]
                                     ).then_inc(s(f"{n}_ld{u}"), 16)
                sp.dma_start(vg[u].rearrange("p k n d -> p (k n d)"), vflat[:, bass.ds(g, 1)].rearrange("p g n -> p (g n)")
                             ).then_inc(s(f"{n}_ld{u}"), 16)

            def load_max(g, u):
                sp.wait_ge(s(n + "_msplit"), g + 1)
                for i in range(2):
                    for p in range(3):
                        sp.dma_start(qs[HALF * i + a.max_rows + p:HALF * i + a.max_rows + p + 1, u].rearrange("r n (q t) -> r (n q) t", t=P),
                                     mpart[32 * i:32 * i + 32, p, :]).then_inc(s(n + "_mld"), 16)

            sp.wait_ge(s(n + "_v"), NT)
            load(0, 0)
            load(1, 1)
            load_max(0, 0)

            def pair(g, last):
                load_max(g + 1, 1)
                if not last:
                    sp.wait_ge(s(n + "_pv"), (g + 1) * a.nbatch + 2)
                    load(g + 2, 0)
                    load_max(g + 2, 0)
                    sp.wait_ge(s(n + "_pv"), (g + 2) * a.nbatch + 2)
                    load(g + 3, 1)

            if a.groups > 4:
                with sp.Fori(0, a.groups // 2 - 1) as it:
                    pair(it * 2, False)
            else:
                pair(0, False)
            pair(a.groups - 2, True)

        @block.sync
        def _(sp):
            sp.dma_start(cols[:], columns_in).then_inc(s("ld_first"), 16)
            sp.dma_start(wmod[:], w_in["wmod"].rearrange("l p n -> p l n")).then_inc(s("ld_first"), 16)
            sp.dma_start(ident[:], ident_in).then_inc(s("ld_first"), 16)
            for c in range(NCH):
                sp.dma_start(x_tok[:, TPC * c:TPC * c + TPC, :],
                             x_in.rearrange("b s d -> (b s) d")[tok(c), :].rearrange("(t p) d -> p t d", p=P)
                             ).then_inc(s("ld_x"), 16)
            sp.dma_start(w02[:, 0:wwidth[0]], w_in[0]).then_inc(s("ld_w0"), 16)
            sp.dma_start(rowc[:], rows_in.to_broadcast([P, H1 + 2 * E + 4 * HD])).then_inc(s("ld_w0"), 16)
            sp.dma_start(w13[:, 0:wwidth[1]], w_in[1]).then_inc(s("ld_w13"), 16)
            sp.dma_start(w13[:, wwidth[1]:], w_in[3]).then_inc(s("ld_w13"), 16)
            sp.dma_start(expertb[:], expertb_in).then_inc(s("ld_w13"), 16)
            sp.dma_start(mask16[:], masks_in).then_inc(s("ld_const"), 16)
            sp.wait_ge(s("out_mm"), NCH * (OUT_MM["b0"] + 1))
            sp.dma_start(w02[:, 0:wwidth[2]], w_in[2]).then_inc(s("ld_w2"), 16)
            sp.wait_ge(s("gate_rows"), 1)
            sp.dma_start(gates1.rearrange("t e p -> (t e) p"), route[:, 7, :]).then_inc(s("st_gate"), 16)
            sp.wait_ge(s("st_gate"), 16)
            for e in range(E):
                sp.dma_start(arr(e).rearrange("p (t k) -> p t k", k=P),
                             gates1[:, e, :].rearrange("t (u k) -> u t k", u=1).to_broadcast([P, NT, P])
                             ).then_inc(s(f"ld_gate{e}"), 16)
            sp.dma_start(arr(9)[0:E, :].rearrange("e (t k) -> e t k", k=P), gates1.rearrange("t e k -> e t k")).then_inc(s("ld_gater"), 16)

            attention_transfers(sp, A2, qd2, kd2)
            sp.wait_ge(s("gate_rows"), 2)
            sp.dma_start(gates2.rearrange("t e p -> (t e) p"), route[:, 7, :]).then_inc(s("st_gate"), 16)
            sp.wait_ge(s("st_gate"), 32)
            for e in range(E):
                sp.dma_start(arr(e).rearrange("p (t k) -> p t k", k=P),
                             gates2[:, e, :].rearrange("t (u k) -> u t k", u=1).to_broadcast([P, NT, P])
                             ).then_inc(s(f"ld_gate{e}"), 16)
            sp.wait_ge(s("x_upd"), NCH * (OUT["b2"] + 1))
            sp.dma_start(arr(10), rope_in).then_inc(s("ld_rope"), 16)
            attention_transfers(sp, A3, qd3, kd3)
            for c in range(NCH):
                sp.wait_ge(s("x_upd"), NCH * OUT["b3"] + c + 1)
                sp.dma_start(out.rearrange("b s d -> (b s) d")[tok(c), :].rearrange("(t p) d -> p t d", p=P),
                             x_tok[:, TPC * c:TPC * c + TPC, :]).then_inc(s("st_out"), 16)
            sp.wait_ge(s("st_out"), 16 * NCH)

        def value_products(pe, a, wv, width):
            if not a.causal:
                pe.wait_ge(s("rope_read"), 2 * NCH)
            for t in range(NT):
                if t >= 2:
                    pe.wait_ge(s(a.name + "_v"), t - 1)
                pe.matmul(ps[:, 6 + t % 2, 0:width], hF[:, t * P:(t + 1) * P], wv, start=True,
                          stop=True).then_inc(s(a.name + "_vmm"), 1)

        def attention_products(pe, a):
            n = a.name
            _, vg = group_v(a)
            nb, ns, np_ = a.nbatch, a.nsteps, a.npieces
            begin, end = ns // 8, ns * 13 // 16
            at = [0 if k < begin else min(np_, (k - begin) * np_ // (end - begin)) for k in range(ns + 1)]

            def piece(g, u, m):
                i, sl, qt, pc, keys = a.pieces[m]
                lo = HALF * i
                bank = ps[:, 4 + m % 2, 0:keys]
                pe.wait_ge(s(n + "_mx"), g * np_ + m + 1)
                diag = a.causal and (pc + 1) * CH >= P * (qt + 1)
                last = pe.matmul(bank, qs[lo:lo + a.max_rows, u, sl, qt * P:(qt + 1) * P],
                                 ks[lo:lo + a.max_rows, u, sl, pc * CH:pc * CH + keys], start=True, stop=not diag)
                if diag:
                    last = pe.matmul(ps[:, 4 + m % 2, keys - P:keys], ident16[:], mask16[:, 2 * P:3 * P],
                                     start=False, stop=True)
                last.then_inc(s(n + "_mxmm"), 1)

            def turn_max(g):
                pe.wait_ge(s(n + "_neg"), g + 1)
                pe.transpose(ps[:, 4, 0:P], negm[:], ident[:]).then_inc(s(n + "_mturn"), 1)

            def scores(g, u, beta, sl):
                qc, i, kt, f = a.batches[beta]
                k = SLOTS * beta + sl
                lo = HALF * i
                pe.wait_ge(s(n + "_exp"), g * ns + k + 1)
                for h in range(2):
                    bank = 2 * (k % 2) + h
                    diag = a.causal and kt >= TPC * qc
                    last = pe.matmul(ps[:, bank, f:CH], ks[lo:lo + a.all_rows, u, sl, (kt + h) * P:(kt + h + 1) * P],
                                     qs[lo:lo + a.all_rows, u, sl, qc * CH + f:(qc + 1) * CH], start=True, stop=not diag)
                    if diag and h == 0:
                        last = pe.matmul(ps[:, bank, f:f + P], ident16[:], mask16[:, P:2 * P], start=False, stop=True)
                    if diag and h == 1:
                        last = pe.matmul(ps[:, bank, f:f + 2 * P], ident16[:], mask16[:, 0:2 * P], start=False, stop=True)
                last.then_inc(s(n + "_sc"), 1)

            def weighted(g, u, beta):
                qc, i, kt, f = a.batches[beta]
                pe.wait_ge(s(n + "_exp"), g * ns + SLOTS * (beta + 1) + 2)
                last_kt = (TPC * (qc + 1) if a.causal else QT) - 2
                if kt == 0:
                    pe.wait_ge(s(n + "_ocopy"), g * 4 + 2 * qc + i + 1)
                for h in range(2):
                    g0 = f + (P * h if a.causal and kt >= TPC * qc else 0)
                    for sl in range(SLOTS):
                        k = SLOTS * beta + sl
                        v = vg[u][:, kt + h, (SLOTS * i if a.causal else 0) + sl, :]
                        last = pe.matmul(ps[32 * sl:32 * sl + 32, 6, g0:CH], v, pslots[:, k % 8, h, g0:CH],
                                         start=(kt == 0 and h == 0), stop=(kt == last_kt and h == 1), skip_group_check=True)
                last.then_inc(s(n + "_pv"), 1)
                return kt == last_kt

            def turn_out(g, j):
                pe.wait_ge(s(n + "_ocopy"), g * 4 + j + 2)
                pe.wait_ge(s(n + "_oread"), g * 4 + j + 1)
                for t in range(TPC):
                    last = pe.transpose(ps[:, 7, t * P:(t + 1) * P], side(j % 2)[:, t * P:(t + 1) * P], ident[:])
                last.then_inc(s(n + "_oturn"), 1)

            def main(g, u, following):
                if following:
                    turned = False
                waiting, j = False, 0
                pe.wait_ge(s(n + "_mld"), 96 * (g + 1))
                for beta in range(nb):
                    for sl in range(SLOTS):
                        k = SLOTS * beta + sl
                        scores(g, u, beta, sl)
                        if following:
                            for m in range(at[k], at[k + 1]):
                                if m == 0:
                                    wait_loaded(g + 1, 1 - u)
                                    pe.wait_ge(s(n + "_msplit"), g + 1)
                                piece(g + 1, 1 - u, m)
                    if waiting:
                        turn_out(g, j)
                        j += 1
                        waiting = False
                    if beta >= 1:
                        waiting = weighted(g, u, beta - 1)
                    if following and SLOTS * (beta + 1) >= end + SLOTS and not turned:
                        turn_max(g + 1)
                        turned = True
                if waiting:
                    turn_out(g, j)
                    j += 1
                weighted(g, u, nb - 1)
                turn_out(g, 3)

            nld = 2 * (12 + (1 if a.causal else 0)) + 1

            def wait_loaded(g, u):
                if isinstance(g, int):
                    pe.wait_ge(s(f"{n}_ld{u}"), 16 * nld * (g // 2 + 1))
                else:
                    pe.wait_ge(s(f"{n}_ld{u}"), g * (8 * nld) + (16 - 8 * u) * nld)

            pe.sem_inc(s(n + "_pv"), 2)
            pe.sem_inc(s(n + "_oturn"), 2)
            pe.wait_ge(s(n + "_ones"), 16 * (8 if a.causal else 4))
            wait_loaded(0, 0)
            for m in range(np_):
                piece(0, 0, m)
            turn_max(0)

            def pair(g, last):
                main(g, 0, True)
                main(g + 1, 1, not last)

            if a.groups > 4:
                with pe.Fori(0, a.groups // 2 - 1) as it:
                    pair(it * 2, False)
            else:
                pair(0, False)
            pair(a.groups - 2, True)

        def attention_turns(pe, a):
            n = a.name
            halves = 1 if a.causal else 2
            pe.wait_ge(s(n + "_oread"), 4 * a.groups + 1)
            if not a.causal:
                pe.wait_ge(s("a3_odone"), 2 * a.groups)
            for c in range(NCH):
                for hf in range(halves):
                    k = halves * c + hf
                    if k >= 2:
                        pe.wait_ge(s(n + "_ctx"), k - 1)
                    for t in range(TPC):
                        last = pe.transpose(ps[:, 4 + k % 2, t * P:(t + 1) * P], o_tile(a, TPC * c + t, hf), ident[:])
                    last.then_inc(s(n + "_cturn"), 1)

        @block.tensor
        def _(pe):
            def layernorm(name):
                n = LN[name]
                for c in range(NCH):
                    pe.wait_ge(s("ln_normed"), NCH * n + c + 1)
                    for t in range(TPC):
                        last = pe.transpose(ps[:, c, t * P:(t + 1) * P], xn[:, TPC * c + t, :], ident[:])
                    last.then_inc(s("ln_turned"), 1)

            def to_tokens(src, name, ready, base):
                for c in range(NCH):
                    pe.wait_ge(ready, base + c + 1)
                    for t in range(TPC):
                        last = pe.transpose(ps[:, 4 + c, t * P:(t + 1) * P], src(c)[:, t * P:(t + 1) * P], ident[:])
                    last.then_inc(s("tok_turned"), 1)

            def block_out(name, c):
                n = OUT[name]
                pe.wait_ge(s("out_scaled"), NCH * n + c + 1)
                if c >= 2:
                    pe.wait_ge(s("x_upd"), NCH * n + c - 1)
                for t in range(TPC):
                    last = pe.transpose(ps[:, 2 + c % 2, t * P:(t + 1) * P],
                                        arr(11)[:, c * CH + t * P:c * CH + (t + 1) * P], ident[:])
                last.then_inc(s("out_turned"), 1)

            def outputs(name, products):
                for c in range(NCH):
                    if c >= 2:
                        pe.wait_ge(s("out_scaled"), NCH * OUT[name] + c - 1)
                    products(c, ps[:, c % 2, :]).then_inc(s("out_mm"), 1)
                    if c >= 1:
                        block_out(name, c - 1)
                block_out(name, NCH - 1)

            pe.wait_ge(s("ld_first"), 48)
            pe.wait_ge(s("silu_c"), 1)
            for layer in range(4):
                for j in range(6):
                    at = (layer * 6 + j) * B
                    last = pe.matmul(ps[:, 7, at:at + B], wmod[:, layer, j * C:(j + 1) * C],
                                     silc[:, B * layer:B * layer + B], start=True, stop=True)
            last.then_inc(s("mod_mm"), 1)

            layernorm("a0")
            pe.wait_ge(s("abs_sum"), 2)
            pe.matmul(ps[:, 6, 0:2], ones[:], small[:, 0:2], start=True, stop=True).then_inc(s("abs_mm"), 1)
            pe.wait_ge(s("w0_mixed"), 6)
            for c in range(NCH):
                pe.wait_ge(s("hT"), NCH * LN["a0"] + c + 1)
                for j, name in enumerate(("key", "value", "recept")):
                    n = 3 * c + j
                    pe.wait_ge(s("mod_ready"), 1)
                    pe.wait_ge(s("abs_read"), 1)
                    if n >= 4:
                        pe.wait_ge(s("kvr_read"), n - 3)
                    bank = ps[:, 4 + n % 4, :]
                    pe.matmul(bank, arr(0)[:, (2 * j) * C:(2 * j + 1) * C], h_chunk(c), start=True, stop=False)
                    pe.matmul(bank, arr(0)[:, (2 * j + 1) * C:(2 * j + 2) * C], h_chunk(c, 1), start=False,
                              stop=True).then_inc(s("kvr_mm"), 1)

            def out_a0(c, bank):
                pe.wait_ge(s("wkv"), c // CPB + 1)
                return pe.matmul(bank, w(0, "out"), arr(1)[:, tok(c)], start=True, stop=True)
            outputs("a0", out_a0)

            layernorm("b0")
            to_tokens(h_chunk, "in0", s("hT"), NCH * LN["b0"])
            layernorm("in0")
            pe.wait_ge(s("ternary"), 2)
            pe.wait_ge(s("hT"), NCH * (LN["in0"] + 1))
            for j in range(4):
                last = pe.matmul(ps[:, 3, 0:1], w(0, "w2")[:, j * C:(j + 1) * C], col("ln2_b", j),
                                 start=(j == 0), stop=(j == 3))
            last.then_inc(s("b2_mm"), 1)
            pe.wait_ge(s("w2_scaled"), 1)

            def hidden(c):
                for t in range(TPC):
                    n = TPC * c + t
                    if n >= 2:
                        pe.wait_ge(s("hid_read"), n - 1)
                    pe.matmul(ps[:, 4 + n % 2, :], hT[:, c // CPB, 1 + (c % CPB) * CH + t * P:1 + (c % CPB) * CH + (t + 1) * P],
                              w(0, "w1"), start=True, stop=True).then_inc(s("hid_mm"), 1)

            def out_b0(c, bank):
                hidden(c + 1) if c + 1 < NCH else None
                for t in range(TPC):
                    n = TPC * c + t
                    pe.wait_ge(s("hid_normed"), n + 1)
                    if n >= 2:
                        pe.wait_ge(s("hidT"), n - 1)
                    for j in range(4):
                        last = pe.transpose(ps[:, 6 + n % 2, j * P:(j + 1) * P], hid(n)[:, j * P:(j + 1) * P], ident[:])
                    last.then_inc(s("hid_turned"), 1)
                pe.wait_ge(s("hidT"), TPC * (c + 1))
                for j in range(4):
                    last = pe.matmul(bank, arr(0)[:, j * C:(j + 1) * C], hid_T(c)[:, j, :], start=(j == 0), stop=(j == 3))
                return last
            hidden(0)
            outputs("b0", out_b0)

            layernorm("a1")
            for c in range(NCH):
                pe.wait_ge(s("hT"), NCH * LN["a1"] + c + 1)
                if c == 0:
                    pe.wait_ge(s("ld_w13"), 48)
                for j, name in enumerate(("v", "q", "g")):
                    n = 3 * c + j
                    if n >= 4:
                        for which in range(3):
                            if (n - 4) % 3 == which:
                                pe.wait_ge(s(("l1_state", "l1_y", "l1_gate")[which]), (n - 4) // 3 + 1)
                    pe.matmul(ps[:, 4 + n % 4, :], w(1, name), hF[:, tok(c)], start=True, stop=True).then_inc(s("vqg_mm"), 1)
            pe.wait_ge(s("l1_gate"), NCH)
            pe.wait_ge(s("l1_y"), NCH)
            to_tokens(lambda c: arr(2)[:, tok(c)], "y1", s("l1_y"), 0)
            layernorm("y1")

            def out_a1(c, bank):
                pe.wait_ge(s("l1_gated"), c + 1)
                return pe.matmul(bank, w(1, "out"), arr(4)[:, tok(c)], start=True, stop=True)
            outputs("a1", out_a1)

            def router(layer, n):
                for t in range(NT):
                    pe.wait_ge(s("hT"), NCH * LN[f"b{layer}"] + t // TPC + 1)
                    last = pe.matmul(ps[:, 4, t * E:(t + 1) * E], hF[:, t * P:(t + 1) * P], w(layer, "router"),
                                     start=True, stop=True)
                last.then_inc(s("router_mm"), 1)
                pe.wait_ge(s("gates"), n + 1)
                pe.transpose(ps[:, 5, 0:P], route[:, 6, :], ident[:]).then_inc(s("gates_turned"), 1)

            layernorm("b1")
            router(1, 0)

            def out_b1(c, bank):
                for e in range(E):
                    n = E * c + e
                    pe.wait_ge(s("picked"), n + 1)
                    pe.matmul(bank, w(1, "expert")[:, e * C:(e + 1) * C], arr(8)[:, (n % 4) * CH:(n % 4 + 1) * CH],
                              start=(e == 0), stop=False).then_inc(s("expert_mm"), 1)
                if c == 0:
                    pe.wait_ge(s("ld_gater"), 16)
                return pe.matmul(bank, expertb[:], arr(9)[0:E, tok(c)], start=False, stop=True)
            outputs("b1", out_b1)

            layernorm("a2")
            pe.wait_ge(s("ld_w2"), 16)
            pe.wait_ge(s("hT"), NCH * (LN["a2"] + 1))
            for c in range(NCH):
                for j, name in enumerate(("q", "k")):
                    n = 2 * c + j
                    if n >= 2:
                        pe.wait_ge(s("a2_rest"), n - 1)
                    pe.matmul(ps[:, 4 + n % 2, :], w(2, name), hF[:, tok(c)], start=True, stop=True).then_inc(s("qk2_mm"), 1)
            value_products(pe, A2, w(2, "v"), C)
            pe.wait_ge(s("ident16"), 1)
            attention_products(pe, A2)
            attention_turns(pe, A2)

            def out_a2(c, bank):
                pe.wait_ge(s("a2_ctx"), c + 1)
                return pe.matmul(bank, w(2, "out"), arr(0)[:, tok(c)], start=True, stop=True)
            outputs("a2", out_a2)

            layernorm("b2")
            router(2, 1)

            pe.wait_ge(s("gate_rows"), 2)

            def expert_hidden(cc, m):
                k = cc * 2 * E + m
                pe.wait_ge(s("silu2"), k + 1)
                pe.wait_ge(s("swiglu"), k + 1)
                rhs = hF[:, bass.ds(cc * CH, CH)]
                pe.matmul(ps[:, 4 + 2 * (m % 2), :], w(2, "w1")[:, m * P:(m + 1) * P], rhs, start=True,
                          stop=True).then_inc(s("h1_mm"), 1)
                pe.matmul(ps[:, 5 + 2 * (m % 2), :], w(2, "w2")[:, m * P:(m + 1) * P], rhs, start=True,
                          stop=True).then_inc(s("h2_mm"), 1)

            pe.sem_inc(s("g_used"), 2)
            with pe.Fori(0, NCH) as cc:
                pe.wait_ge(s("out_scaled"), NCH * OUT["b2"] + cc)
                for m in range(2 * E):
                    expert_hidden(cc, m)
                    if m >= 1:
                        pe.wait_ge(s("gated2"), cc * (2 * E) + m)
                        pe.matmul(ps[:, 0, :], w(2, "w3")[:, (m - 1) * C:m * C], arr(8)[:, ((m - 1) % 2) * CH:((m - 1) % 2 + 1) * CH],
                                  start=(m == 1), stop=False).then_inc(s("g_used"), 1)
                m = 2 * E
                pe.wait_ge(s("gated2"), cc * (2 * E) + m)
                pe.matmul(ps[:, 0, :], w(2, "w3")[:, (m - 1) * C:m * C], arr(8)[:, ((m - 1) % 2) * CH:((m - 1) % 2 + 1) * CH],
                          start=False, stop=True).then_inc(s("g_used"), 1)
            for c in range(NCH):
                block_out("b2", c)

            layernorm("a3")
            pe.wait_ge(s("hT"), NCH * (LN["a3"] + 1))
            for c in range(NCH):
                for j in range(2):
                    n = 2 * c + j
                    if n >= 2:
                        pe.wait_ge(s("rope_read"), n - 1)
                    for i in range(2):
                        pe.matmul(ps[:, 4 + 2 * (n % 2) + i, :], w(3, "qk"[j] + str(i)), hF[:, tok(c)], start=True,
                                  stop=True).then_inc(s("qk3_mm"), 1)
            value_products(pe, A3, w(3, "v"), 2 * C)
            attention_products(pe, A3)
            attention_turns(pe, A3)

            def out_a3(c, bank):
                pe.wait_ge(s("a3_ctx"), 2 * c + 2)
                pe.matmul(bank, w(3, "out")[:, 0:C], arr(0)[:, tok(c)], start=True, stop=False)
                return pe.matmul(bank, w(3, "out")[:, C:2 * C], arr(1)[:, tok(c)], start=False, stop=True)
            outputs("a3", out_a3)

            layernorm("b3")
            pe.wait_ge(s("w3_mixed"), 4)
            for c in range(NCH):
                pe.wait_ge(s("hT"), NCH * LN["b3"] + c + 1)
                for j in range(2):
                    n = 2 * c + j
                    if n >= 4:
                        pe.wait_ge(s(("cm_k", "cm_r")[j]), c - 1)
                    pe.matmul(ps[:, 4 + n % 4, :], arr(4)[:, 2 * j * C:(2 * j + 1) * C], h_chunk(c), start=True, stop=False)
                    pe.matmul(ps[:, 4 + n % 4, :], arr(4)[:, (2 * j + 1) * C:(2 * j + 2) * C], h_chunk(c, 1), start=False,
                              stop=True).then_inc(s("cm_mm"), 1)

            def out_b3(c, bank):
                pe.wait_ge(s("cm_sq"), c + 1)
                return pe.matmul(bank, w(3, "wv"), arr(2)[:, tok(c)], start=True, stop=True)
            outputs("b3", out_b3)

        def first_part(act, a, unit, src, scale, _):
            n = a.name
            if unit >= 4:
                act.wait_ge(s(f"{n}_st{unit % 4}"), 16 * (a.groups // B) * (unit // 4))
            act.activation(parts_ring(unit % 4)[:, 0, :], src, ACT.Copy, scale=scale).then_inc(s(n + "_p1"), 1)

        def values(act, a):
            n = a.name
            per_b = a.groups // B
            va, _ = group_v(a)
            act.wait_ge(s(n + "_vzero"), 2)
            for t in range(NT):
                act.wait_ge(s(n + "_vmm"), t + 1)
                b, kt = t // QT, t % QT
                for i in range(halves_of(a)):
                    last = act.activation(va[:, per_b * b:per_b * (b + 1), kt, :, HD * i:HD * (i + 1)],
                                          ps[:, 6 + t % 2, i * C:(i + 1) * C].rearrange("p (g n d) -> p g n d", g=per_b, d=HD),
                                          ACT.Copy)
                last.then_inc(s(n + "_v"), 1)

        def exponentials(act, a):
            n = a.name
            nb, ns = a.nbatch, a.nsteps

            def copy_out(g, j, beta):
                act.wait_ge(s(n + "_pv"), g * nb + beta + 3)
                act.wait_ge(s(n + "_oturn"), g * 4 + j + 1)
                act.activation(side(j % 2), ps[:, 6, :], ACT.Copy).then_inc(s(n + "_ocopy"), 1)

            def main(g):
                j = 0
                for beta, (qc, i, kt, f) in enumerate(a.batches):
                    for sl in range(SLOTS):
                        k = SLOTS * beta + sl
                        act.wait_ge(s(n + "_sc"), g * ns + k + 1)
                        act.wait_ge(s(n + "_pv"), g * nb + beta + 1)
                        act.activation(pslots[:, k % 8, :, f:CH], ps[:, 2 * (k % 2):2 * (k % 2) + 2, f:CH], ACT.Exp
                                       ).then_inc(s(n + "_exp"), 1)
                    if beta >= 1 and a.batches[beta][0:2] != a.batches[beta - 1][0:2]:
                        copy_out(g, j, beta - 1)
                        j += 1
                copy_out(g, 3, nb - 1)

            act.sem_inc(s(n + "_exp"), 2)
            act.sem_inc(s(n + "_ocopy"), 1)
            for slot in range(4):
                act.wait_ge(s(f"{n}_st{slot}"), 16 * (a.groups // B) * halves_of(a) * 2)
            if a.groups > 4:
                with act.Fori(0, a.groups // 2) as it:
                    main(it * 2)
                    main(it * 2 + 1)
            else:
                for g in range(a.groups):
                    main(g)

        def contexts(act, a):
            n = a.name
            for k in range(halves_of(a) * NCH):
                c, hf = k // halves_of(a), k % halves_of(a)
                act.wait_ge(s(n + "_cturn"), k + 1)
                act.activation(arr(hf)[:, tok(c)], ps[:, 4 + k % 2, :], ACT.Copy).then_inc(s(n + "_ctx"), 1)

        @block.scalar
        def _(act):
            def features(name, scale, bias, dst):
                n = LN[name]
                for c in range(NCH):
                    act.wait_ge(s("ln_turned"), NCH * n + c + 1)
                    act.activation(dst(c), ps[:, c, :], ACT.Identity, bias=bias(c // CPB), scale=scale(c // CPB)
                                   ).then_inc(s("hT"), 1)

            def modulated(layer, which, dst):
                j = 0 if which == "a" else 3
                features(f"{which}{layer}", lambda b: mod[:, layer, j + 1, b:b + 1], lambda b: mod[:, layer, j, b:b + 1], dst)

            def flat(c):
                return hF[:, tok(c)]

            def scaled(name, c, bias=0.0):
                layer, j = int(name[1]), 2 if name[0] == "a" else 5
                act.wait_ge(s("out_mm"), NCH * OUT_MM[name] + c + 1)
                b = c // CPB
                act.activation(arr(11)[:, tok(c)], ps[:, c % 2, :], ACT.Identity, bias=bias,
                               scale=mod[:, layer, j, b:b + 1]).then_inc(s("out_scaled"), 1)

            act.wait_ge(s("ld_first"), 48)
            act.activation(silc[:], cols[:, 0:8], ACT.Silu).then_inc(s("silu_c"), 1)
            act.activation(small[:, 18:19], col("beta"), ACT.Sigmoid).then_inc(s("lam1"), 1)
            act.activation(small[:, 16:17], col("decay"), ACT.Exp).then_inc(s("decay_exp"), 1)

            act.wait_ge(s("mod_ready"), 1)
            modulated(0, "a", h_chunk)
            for n in range(3 * NCH):
                c, j = n // 3, n % 3
                act.wait_ge(s("kvr_mm"), n + 1)
                act.activation(arr(2 + j)[:, tok(c)], ps[:, 4 + n % 4, :], (ACT.Copy, ACT.Copy, ACT.Sigmoid)[j]
                               ).then_inc(s("kvr_read"), 1)
            for b in range(B):
                for k, ready in enumerate(("wkv_a2", "wkv_b2", "wkv_bc", "wkv_a")):
                    act.wait_ge(s(ready), b + 1)
                    x = wkv_temp(b, (0, 1, 3, 2)[k])
                    act.activation(x, x, ACT.Exp).then_inc(s("wkv_exp"), 1)
            for c in range(NCH):
                scaled("a0", c)

            modulated(0, "b", h_chunk)
            features("in0", lambda b: col("ln1_g"), lambda b: col("ln1_b"), h_chunk)

            def gelus(c):
                for n in range(TPC * c, TPC * c + TPC):
                    act.wait_ge(s("hid_read"), n + 1)
                    act.activation(hid(n), hid(n), ACT.Gelu).then_inc(s("gelu"), 1)
            gelus(0)
            for c in range(NCH):
                if c + 1 < NCH:
                    gelus(c + 1)
                for t in range(TPC):
                    n = TPC * c + t
                    act.wait_ge(s("hid_turned"), n + 1)
                    if c >= 2 and t == 0:
                        act.wait_ge(s("out_mm"), NCH * OUT_MM["b0"] + c - 1)
                    act.activation(hid_T(c)[:, :, t * P:(t + 1) * P],
                                   ps[:, 6 + n % 2, :].rearrange("p (j t) -> p j t", j=4), ACT.Copy
                                   ).then_inc(s("hidT"), 1)
                if c == 0:
                    act.wait_ge(s("b2_ready"), 1)
                scaled("b0", c, bias=small[:, 9 + c // CPB:10 + c // CPB])

            modulated(1, "a", flat)
            for c in range(NCH):
                act.wait_ge(s("vqg_mm"), 3 * c + 3)
                act.activation(arr(3)[:, tok(c)], ps[:, 4 + (3 * c + 2) % 4, :], ACT.Silu).then_inc(s("l1_gate"), 1)
            features("y1", lambda b: col("gamma"), lambda b: col("lnb"), flat)
            for c in range(NCH):
                scaled("a1", c)

            modulated(1, "b", flat)
            act.wait_ge(s("route_in"), 1)
            act.activation(route[:, 3, :], route[:, 3, :], ACT.Exp).then_inc(s("route_exp"), 1)
            for c in range(NCH):
                scaled("b1", c)

            modulated(2, "a", flat)
            for n in range(2 * NCH):
                act.wait_ge(s("qk2_mm"), n + 1)
                first_part(act, A2, n, ps[:, 4 + n % 2, :], HD ** -0.5 if n % 2 == 0 else 1.0, 2)
            values(act, A2)
            exponentials(act, A2)
            contexts(act, A2)
            for c in range(NCH):
                scaled("a2", c)

            modulated(2, "b", flat)
            act.wait_ge(s("route_in"), 2)
            act.activation(rone[:, 3, :], rone[:, 3, :], ACT.Exp).then_inc(s("route_exp"), 1)
            act.sem_inc(s("silu2"), 2)
            with act.Fori(0, NCH) as cc:
                for m in range(2 * E):
                    k = cc * (2 * E) + m
                    act.wait_ge(s("h1_mm"), k + 1)
                    act.wait_ge(s("swiglu"), k + 1)
                    act.activation(arr(9)[:, (m % 2) * CH:(m % 2 + 1) * CH], ps[:, 4 + 2 * (m % 2), :], ACT.Silu
                                   ).then_inc(s("silu2"), 1)
                act.wait_ge(s("g_used"), (cc + 1) * (2 * E) + 2)
                act.activation(arr(11)[:, bass.ds(cc * CH, CH)], ps[:, 0, :], ACT.Copy, scale=small[:, bass.ds(cc + 28, 1)]
                               ).then_inc(s("out_scaled"), 1)

            modulated(3, "a", flat)
            act.wait_ge(s("lam_sum"), 1)
            act.activation(small[:, 22:24], small[:, 20:22], ACT.Exp).then_inc(s("lam_exp"), 1)
            for n in range(2 * NCH):
                for i in range(2):
                    act.wait_ge(s("roped"), 2 * n + i + 1)
                    first_part(act, A3, 2 * n + i, roped(2 * n + i), HD ** -0.5 if n % 2 == 0 else 1.0, 4)
            values(act, A3)
            exponentials(act, A3)
            contexts(act, A3)
            for c in range(NCH):
                scaled("a3", c)

            modulated(3, "b", h_chunk)
            for c in range(NCH):
                act.wait_ge(s("cm_mm"), 2 * c + 1)
                act.activation(arr(1)[:, tok(c)], ps[:, 4 + (2 * c) % 4, :], ACT.Relu).then_inc(s("cm_k"), 1)
                act.wait_ge(s("cm_mm"), 2 * c + 2)
                act.activation(arr(0)[:, tok(c)], ps[:, 4 + (2 * c + 1) % 4, :], ACT.Sigmoid).then_inc(s("cm_r"), 1)

        def gate_out(dve, c):
            dve.wait_ge(s("out_mm"), NCH * OUT_MM["b3"] + c + 1)
            dve.wait_ge(s("cm_r"), c + 1)
            dve.scalar_tensor_tensor(out=arr(11)[:, tok(c)], in0=ps[:, c % 2, :], scalar=mod[:, 3, 5, c // CPB:c // CPB + 1],
                                     in1=arr(0)[:, tok(c)], op0=ALU.mult, op1=ALU.mult).then_inc(s("out_scaled"), 1)

        def other_parts(dve, a, unit, src, scale):
            n = a.name
            ring = parts_ring(unit % 4)
            dve.wait_ge(s(n + "_p1"), unit + 1)
            dve.scalar_tensor_tensor(out=rest(unit), in0=src, scalar=scale, in1=ring[:, 0, :], op0=ALU.mult, op1=ALU.subtract
                                     ).then_inc(s(n + "_rest"), 1)
            dve.wait_ge(s(n + "_rest"), unit + 1)
            dve.tensor_copy(ring[:, 1, :], rest(unit)).then_inc(s(n + "_p2"), 1)
            dve.wait_ge(s(n + "_p2"), unit + 1)
            dve.tensor_tensor(ring[:, 2, :], rest(unit), ring[:, 1, :], ALU.subtract).then_inc(s(n + "_parts"), 1)

        def maxima(dve, a):
            n = a.name
            nb, ns, np_ = a.nbatch, a.nsteps, a.npieces
            begin, end = ns // 8, ns * 13 // 16
            at = [0 if k < begin else min(np_, (k - begin) * np_ // (end - begin)) for k in range(ns + 1)]

            def piece(g, m):
                i, sl, qt, pc, keys = a.pieces[m]
                dve.wait_ge(s(n + "_mxmm"), g * np_ + m + 1)
                row = (i * SLOTS + sl) * QT + qt
                dve.tensor_reduce(mcol[:, row, pc:pc + 1], ps[:, 4 + m % 2, 0:keys], AX.X, ALU.max).then_inc(s(n + "_mx"), 1)
                if m == np_ - 1:
                    dve.wait_ge(s(n + "_mx"), (g + 1) * np_ + 2)
                    dve.tensor_reduce(negm[:, 0:SETS * QT], mcol[:], AX.X, ALU.max, negate=True).then_inc(s(n + "_neg"), 1)

            def split_max(g):
                dve.wait_ge(s(n + "_mturn"), g + 1)
                if not (isinstance(g, int) and g == 0):
                    dve.wait_ge(s(n + "_mld"), g * 96)
                src = ps[0:SETS * QT, 4, 0:P]
                dve.tensor_copy(mpart[:, 0, :], src).then_inc(s(n + "_mstep"), 1)
                dve.wait_ge(s(n + "_mstep"), g * 3 + 1)
                dve.tensor_tensor(mrest[:], src, mpart[:, 0, :], ALU.subtract).then_inc(s(n + "_mstep"), 1)
                dve.wait_ge(s(n + "_mstep"), g * 3 + 2)
                dve.tensor_copy(mpart[:, 1, :], mrest[:]).then_inc(s(n + "_mstep"), 1)
                dve.wait_ge(s(n + "_mstep"), g * 3 + 3)
                dve.tensor_tensor(mpart[:, 2, :], mrest[:], mpart[:, 1, :], ALU.subtract).then_inc(s(n + "_msplit"), 1)

            placed = otok[:, 0:a.groups // 2 * QT * P].rearrange("p (g q u f) -> p g q u f", q=QT, u=2, f=P // 2)

            def output(pair, u, j):
                g, (qc, i), w_ = pair * 2 + u, divmod(j, 2), a.width
                src = ps[:, 7, :].rearrange("p (t n d) -> p (t n) d", t=TPC, d=32)
                dve.wait_ge(s(n + "_oturn"), g * 4 + j + 3)
                dve.reciprocal(rz[:].unsqueeze(2), src[:, :, w_:w_ + 1]).then_inc(s(n + "_orz"), 1)
                dve.wait_ge(s(n + "_orz"), g * 4 + j + 1)
                rb = rz[:].unsqueeze(2).to_broadcast([P, TPC * SLOTS, w_])
                if a.causal:
                    dst = placed[:, bass.ds(pair, 1), TPC * qc:TPC * (qc + 1), u, 32 * i:32 * i + 32].rearrange(
                        "p g q (n d) -> p (g q) n d", d=w_)
                    dve.tensor_tensor(dst, src[:, :, 0:w_].rearrange("p (t n) d -> p t n d", t=TPC),
                                      rb.rearrange("p (t n) d -> p t n d", t=TPC), ALU.mult).then_inc(s(n + "_oread"), 1)
                    return
                half = xn[:].rearrange("p t c -> p (t c)")[:, 2 * CH + i * 256:2 * CH + (i + 1) * 256]
                dve.tensor_tensor(half.rearrange("p (x d) -> p x d", d=w_), src[:, :, 0:w_], rb, ALU.mult).then_inc(s(n + "_oread"), 1)
                if i == 1:
                    dst = placed[:, bass.ds(pair, 1), TPC * qc:TPC * (qc + 1), u, :].rearrange("p g q f -> p (g q) f")
                    dve.wait_ge(s(n + "_oread"), g * 4 + j + 2)
                    dve.scalar_tensor_tensor(out=dst, in0=half.rearrange("p (q f) -> p q f", q=TPC), scalar=small[:, 25:26],
                                             in1=xn[:].rearrange("p t c -> p (t c)")[:, 2 * CH:2 * CH + 256].rearrange(
                                                 "p (q f) -> p q f", q=TPC),
                                             op0=ALU.mult, op1=ALU.add).then_inc(s(n + "_odone"), 1)

            def main(pair, u, following):
                g, waiting, j, turned = pair * 2 + u, False, 0, False
                for beta in range(nb):
                    if following:
                        for k in range(SLOTS * beta, SLOTS * (beta + 1)):
                            for m in range(at[k], at[k + 1]):
                                piece(g + 1, m)
                    if waiting:
                        output(pair, u, j)
                        j += 1
                    waiting = beta >= 1 and a.batches[beta][0:2] != a.batches[beta - 1][0:2]
                    if following and SLOTS * (beta + 1) >= end + SLOTS and not turned:
                        split_max(g + 1)
                        turned = True
                if waiting:
                    output(pair, u, j)
                    j += 1
                output(pair, u, 3)

            dve.sem_inc(s(n + "_mx"), 2)
            dve.sem_inc(s(n + "_oread"), 1)
            for m in range(np_):
                piece(0, m)
            split_max(0)
            if a.groups > 4:
                with dve.Fori(0, a.groups // 2 - 1) as it:
                    main(it, 0, True)
                    main(it, 1, True)
            else:
                main(0, 0, True)
                main(0, 1, True)
            main(a.groups // 2 - 1, 0, True)
            main(a.groups // 2 - 1, 1, False)

        @block.vector
        def _(dve):
            chain = [0]

            def link(ins):
                chain[0] += 1
                ins.then_inc(s("dve_chain"), 1)
                dve.wait_ge(s("dve_chain"), chain[0])

            def bc(ap, n):
                return ap.unsqueeze(2).to_broadcast([P, NT, n])

            def layernorm(name, feature_major=False):
                n = LN[name]
                if name != "a0" and not feature_major:
                    dve.wait_ge(s("x_upd"), NCH * (n - {"b0": 0, "a1": 1, "b1": 2, "a2": 2, "b2": 2, "a3": 2, "b3": 2}[name]))

                def src(t):
                    if feature_major:
                        return ps[:, 4 + t // TPC, (t % TPC) * P:(t % TPC + 1) * P]
                    return x_tok[:, t, :]
                for t in range(NT):
                    if t % TPC == 0:
                        if feature_major:
                            dve.wait_ge(s("tok_turned"), NCH * (0 if name == "in0" else 1) + t // TPC + 1)
                        elif name == "a0":
                            if t == 0:
                                dve.wait_ge(s("ld_x"), 16 * NCH)
                    dve.bn_stats(stats[:, t, :], src(t)).then_inc(s("ln_stats"), 1)
                for t in range(NT):
                    dve.wait_ge(s("ln_stats"), NT * n + t + 1)
                    dve.bn_aggr(mv[:, t, :], stats[:, t, :]).then_inc(s("ln_aggr"), 1)
                dve.wait_ge(s("ln_aggr"), NT * (n + 1))
                dve.tensor_scalar(var[:], mv[:, :, 1], EPS, None, ALU.add).then_inc(s("ln_var"), 1)
                dve.wait_ge(s("ln_rstd"), n + 1)
                for t in range(NT):
                    last = dve.tensor_scalar(xn[:, t, :], src(t), mv[:, t, 0:1], rstd[:, t:t + 1], ALU.subtract, ALU.mult)
                    if t % TPC == TPC - 1:
                        last.then_inc(s("ln_normed"), 1)

            def add_to_x(name, c):
                dve.wait_ge(s("out_turned"), NCH * OUT[name] + c + 1)
                xs = x_tok[:, TPC * c:TPC * (c + 1), :].rearrange("p t c -> p (t c)")
                dve.tensor_tensor(xs, xs, ps[:, 2 + c % 2, :], ALU.add).then_inc(s("x_upd"), 1)

            dve.memset(hT[:, :, 0:1], 0.0)
            dve.memset(mcol[:], LOWEST)
            dve.memset(negm[:], 0.0)
            link(dve.memset(ones[:], 1.0))
            dve.wait_ge(s("mod_mm"), 1)
            link(dve.tensor_copy(mod[:].rearrange("p l j b -> p (l j b)"), ps[:, 7, 0:8 * 6]))
            for k, j in enumerate((2, 5)):
                dve.tensor_scalar(modx[:, :, k, :], mod[:, :, j, :], 0.0, 2.0, ALU.is_ge, ALU.mult)
            for j in (1, 4):
                dve.tensor_scalar(mod[:, :, j, :], mod[:, :, j, :], 1.0, None, ALU.add)
            for j in (2, 5):
                last = dve.scalar_tensor_tensor(out=mod[:, :, j, :], in0=mod[:, :, j, :], scalar=-1.0, in1=mod[:, :, j, :],
                                                op0=ALU.mult, op1=ALU.max)
            link(last)
            for j in (2, 5):
                last = dve.tensor_scalar(mod[:, :, j, :], mod[:, :, j, :], 0.25, None, ALU.max)
            link(last)
            for k, j in enumerate((2, 5)):
                last = dve.scalar_tensor_tensor(out=mod[:, :, j, :], in0=modx[:, :, k, :], scalar=-1.0, in1=mod[:, :, j, :],
                                                op0=ALU.add, op1=ALU.mult)
            last.then_inc(s("mod_ready"), 1)
            layernorm("a0")

            dve.wait_ge(s("ld_w0"), 32)
            for j, name in enumerate(("mix_k", "mix_v", "mix_r")):
                last = dve.tensor_scalar(small[:, 12 + j:13 + j], col(name), -1.0, 1.0, ALU.mult, ALU.add)
            link(last)
            for j, (name, mix) in enumerate((("key", "mix_k"), ("value", "mix_v"), ("recept", "mix_r"))):
                dve.tensor_scalar(arr(0)[:, 2 * j * C:(2 * j + 1) * C], w(0, name), col(mix), None, ALU.mult).then_inc(s("w0_mixed"), 1)
                dve.tensor_scalar(arr(0)[:, (2 * j + 1) * C:(2 * j + 2) * C], w(0, name), small[:, 12 + j:13 + j], None,
                                  ALU.mult).then_inc(s("w0_mixed"), 1)
            for k, name in enumerate(("w1", "w2")):
                dve.tensor_reduce(small[:, k:k + 1], w(0, name), AX.X, ALU.add, apply_absolute_value=True).then_inc(s("abs_sum"), 1)
            dve.wait_ge(s("decay_exp"), 1)
            dve.tensor_scalar(small[:, 17:18], small[:, 16:17], -1.0, None, ALU.mult)
            dve.wait_ge(s("abs_mm"), 1)
            dve.tensor_scalar(small[:, 2:4], ps[:, 6, 0:2], 1.0 / (H1 * C), 1e-5, ALU.mult, ALU.max).then_inc(s("abs_read"), 1)

            o_, p_, q_ = wkv_state(0), wkv_state(1), wkv_state(2)
            dve.memset(o_[:, :, 0:1], LOWEST)
            dve.memset(p_[:, :, 0:1], 0.0)
            link(dve.memset(q_[:, :, 0:1], 0.0))
            wdecay, u = small[:, 17:18], col("first")
            for b in range(B):
                bt = slice(b * SEQ, (b + 1) * SEQ)
                k, v = arr(2)[:, bt], arr(3)[:, bt]
                dve.wait_ge(s("kvr_read"), 6 * b + 6)
                link(dve.tensor_tensor_scan(o_[:, b, 1:], wdecay.to_broadcast([P, SEQ]), k, LOWEST, ALU.add, ALU.max))
                before = o_[:, b, 0:SEQ]
                dve.scalar_tensor_tensor(out=wkv_temp(b, 0), in0=before, scalar=wdecay, in1=o_[:, b, 1:], op0=ALU.add,
                                         op1=ALU.subtract).then_inc(s("wkv_a2"), 1)
                dve.tensor_tensor(wkv_temp(b, 1), k, o_[:, b, 1:], ALU.subtract).then_inc(s("wkv_b2"), 1)
                link(dve.scalar_tensor_tensor(out=wkv_temp(b, 2), in0=k, scalar=u, in1=before, op0=ALU.add, op1=ALU.max))
                link(dve.scalar_tensor_tensor(out=wkv_temp(b, 3), in0=k, scalar=u, in1=wkv_temp(b, 2), op0=ALU.add,
                                              op1=ALU.subtract))
                dve.nop().then_inc(s("wkv_bc"), 1)
                dve.tensor_tensor(wkv_temp(b, 2), before, wkv_temp(b, 2), ALU.subtract).then_inc(s("wkv_a"), 1)
            for b in range(B):
                bt = slice(b * SEQ, (b + 1) * SEQ)
                v, y = arr(3)[:, bt], arr(1)[:, bt]
                t0, t1, t2, t3 = (wkv_temp(b, k) for k in range(4))
                dve.wait_ge(s("wkv_exp"), 4 * b + 4)
                link(dve.tensor_tensor(y, t1, v, ALU.mult))
                dve.tensor_tensor_scan(p_[:, b, 1:], t0, y, 0.0, ALU.mult, ALU.add)
                link(dve.tensor_tensor_scan(q_[:, b, 1:], t0, t1, 0.0, ALU.mult, ALU.add))
                dve.tensor_tensor(t0, t2, p_[:, b, 0:SEQ], ALU.mult)
                dve.tensor_tensor(t1, t3, v, ALU.mult)
                link(dve.tensor_tensor(t2, t2, q_[:, b, 0:SEQ], ALU.mult))
                dve.tensor_tensor(t0, t0, t1, ALU.add)
                link(dve.tensor_tensor(t2, t2, t3, ALU.add))
                link(dve.reciprocal(t1, t2))
                link(dve.tensor_tensor(t0, t0, t1, ALU.mult))
                dve.tensor_tensor(y, t0, arr(4)[:, bt], ALU.mult).then_inc(s("wkv"), 1)

            dve.wait_ge(s("abs_read"), 1)
            link(dve.reciprocal(small[:, 4:6], small[:, 2:4]))
            link(dve.reciprocal(small[:, 6:8], small[:, 4:6]))
            for k, name in enumerate(("w1", "w2")):
                x = w(0, name)
                link(dve.tensor_scalar(x, x, small[:, 4 + k:5 + k], ROUND, ALU.mult, ALU.add))
                link(dve.tensor_scalar(x, x, -ROUND, 1.0, ALU.add, ALU.min))
                dve.tensor_scalar(x, x, -1.0, small[:, 6 + k:7 + k], ALU.max, ALU.mult).then_inc(s("ternary"), 1)
            for c in range(NCH):
                add_to_x("a0", c)

            dve.wait_ge(s("ternary"), 2)
            for j in range(4):
                last = dve.tensor_scalar(arr(0)[:, j * C:(j + 1) * C], w(0, "w2")[:, j * C:(j + 1) * C], col("ln2_g", j), None, ALU.mult)
            last.then_inc(s("w2_scaled"), 1)
            layernorm("b0")
            layernorm("in0", True)
            dve.wait_ge(s("b2_mm"), 1)
            link(dve.tensor_scalar(small[:, 8:9], ps[:, 3, 0:1], col("b2"), None, ALU.add))
            for b in range(B):
                last = dve.tensor_scalar(small[:, 9 + b:10 + b], small[:, 8:9], mod[:, 0, 5, b:b + 1], None, ALU.mult)
            last.then_inc(s("b2_ready"), 1)

            def hidden(c):
                for t in range(TPC):
                    n = TPC * c + t
                    dve.wait_ge(s("hid_mm"), n + 1)
                    if c >= 2 and t == 0:
                        dve.wait_ge(s("hid_turned"), TPC * (c - 1))
                    dve.tensor_tensor(hid(n), ps[:, 4 + n % 2, :], b1_row, ALU.add).then_inc(s("hid_read"), 1)
                for t in range(TPC):
                    dve.wait_ge(s("gelu"), TPC * c + t + 1)
                    last = dve.bn_stats(stats[:, t, :], hid(TPC * c + t))
                link(last)
                for t in range(TPC):
                    last = dve.bn_aggr(mv[:, t, :], stats[:, t, :])
                link(last)
                dve.tensor_scalar(var[:, 0:TPC], mv[:, 0:TPC, 1], EPS, None, ALU.add).then_inc(s("hid_var"), 1)
                dve.wait_ge(s("hid_rstd"), c + 1)
                for t in range(TPC):
                    x = hid(TPC * c + t)
                    dve.tensor_scalar(x, x, mv[:, t, 0:1], rstd[:, t:t + 1], ALU.subtract, ALU.mult).then_inc(s("hid_normed"), 1)
            hidden(0)
            for c in range(NCH):
                if c + 1 < NCH:
                    hidden(c + 1)
                if c >= 1:
                    add_to_x("b0", c - 1)
            add_to_x("b0", NCH - 1)

            layernorm("a1")
            dve.wait_ge(s("lam1"), 1)
            lam = small[:, 18:19].to_broadcast([P, CH])
            for c in range(NCH):
                dve.wait_ge(s("vqg_mm"), 3 * c + 1)
                x = arr(1)[:, tok(c)]
                if c % CPB:
                    dve.wait_ge(s("l1_state"), c)
                dve.tensor_tensor_scan(x, lam, ps[:, 4 + (3 * c) % 4, :], arr(1)[:, c * CH - 1:c * CH] if c % CPB else 0.0,
                                       ALU.mult, ALU.add).then_inc(s("l1_state"), 1)
                dve.wait_ge(s("vqg_mm"), 3 * c + 2)
                dve.wait_ge(s("l1_state"), c + 1)
                dve.tensor_tensor(arr(2)[:, tok(c)], x, ps[:, 4 + (3 * c + 1) % 4, :], ALU.mult).then_inc(s("l1_y"), 1)
            layernorm("y1", True)
            dve.wait_ge(s("l1_gate"), NCH)
            for c in range(NCH):
                dve.wait_ge(s("hT"), NCH * LN["y1"] + c + 1)
                dve.tensor_tensor(arr(4)[:, tok(c)], hF[:, tok(c)], arr(3)[:, tok(c)], ALU.mult).then_inc(s("l1_gated"), 1)
            for c in range(NCH):
                add_to_x("a1", c)

            def r3(k):
                return route[:, k, :].rearrange("p (t e) -> p t e", e=E)

            def rf(k):
                return rone[:, k, :]
            ties = tie_row.unsqueeze(1).to_broadcast([P, NT, E])

            def first_max(logits, biggest, pick, tmp):
                link(dve.tensor_reduce(biggest, logits, AX.X, ALU.max))
                link(dve.tensor_tensor(tmp, logits, bc(biggest, E), ALU.is_equal))
                link(dve.tensor_tensor(tmp, tmp, ties, ALU.mult))
                link(dve.tensor_reduce(rf(5), tmp, AX.X, ALU.max))
                link(dve.tensor_tensor(pick, tmp, bc(rf(5), E), ALU.is_equal))

            def rows_of_gates(n):
                dve.wait_ge(s("gates_turned"), n + 1)
                dve.tensor_copy(route[:, 7, :], ps[:, 5, 0:P]).then_inc(s("gate_rows"), 1)

            layernorm("b1")
            dve.wait_ge(s("router_mm"), 1)
            link(dve.tensor_tensor(r3(0), ps[:, 4, 0:P].rearrange("p (t e) -> p t e", e=E),
                                   routerb_row.unsqueeze(1).to_broadcast([P, NT, E]), ALU.add))
            first_max(r3(0), rf(0), r3(2), r3(1))
            dve.tensor_tensor(r3(3), r3(0), bc(rf(0), E), ALU.subtract).then_inc(s("route_in"), 1)
            dve.wait_ge(s("route_exp"), 1)
            link(dve.tensor_reduce(rf(1), r3(3), AX.X, ALU.add))
            link(dve.reciprocal(rf(2), rf(1)))
            dve.tensor_tensor(r3(6), r3(2), bc(rf(2), E), ALU.mult).then_inc(s("gates"), 1)
            rows_of_gates(0)
            for c in range(NCH):
                for e in range(E):
                    n = E * c + e
                    if c == 0:
                        dve.wait_ge(s(f"ld_gate{e}"), 16)
                    if n >= 4:
                        dve.wait_ge(s("expert_mm"), n - 3)
                    dve.tensor_tensor(arr(8)[:, (n % 4) * CH:(n % 4 + 1) * CH], hF[:, tok(c)], arr(e)[:, tok(c)],
                                      ALU.mult).then_inc(s("picked"), 1)
                if c >= 1:
                    add_to_x("b1", c - 1)
            add_to_x("b1", NCH - 1)

            layernorm("a2")
            dve.wait_ge(s("ld_const"), 16)
            dve.wait_ge(s("ld_first"), 48)
            dve.tensor_copy(ident16[:], ident[:]).then_inc(s("ident16"), 1)
            for n in range(2 * NCH):
                other_parts(dve, A2, n, ps[:, 4 + n % 2, :], HD ** -0.5 if n % 2 == 0 else 1.0)
            maxima(dve, A2)
            for c in range(NCH):
                add_to_x("a2", c)

            for c in range(NCH):
                dve.tensor_copy(small[:, 28 + c:29 + c], mod[:, 2, 5, c // CPB:c // CPB + 1])
            layernorm("b2")
            dve.wait_ge(s("router_mm"), 2)
            link(dve.tensor_copy(r3(0), ps[:, 4, 0:P].rearrange("p (t e) -> p t e", e=E)))
            first_max(r3(0), rf(0), r3(2), r3(1))
            link(dve.scalar_tensor_tensor(out=route[:, 3, :], in0=route[:, 2, :], scalar=MASKED, in1=route[:, 0, :],
                                          op0=ALU.mult, op1=ALU.add))
            first_max(r3(3), rf(1), r3(4), r3(1))
            dve.tensor_tensor(rf(3), rf(1), rf(0), ALU.subtract).then_inc(s("route_in"), 1)
            dve.wait_ge(s("route_exp"), 2)
            link(dve.tensor_scalar(rf(2), rf(3), 1.0, None, ALU.add))
            link(dve.reciprocal(rf(4), rf(2)))
            link(dve.tensor_tensor(rf(3), rf(3), rf(4), ALU.mult))
            dve.tensor_tensor(r3(5), r3(2), bc(rf(4), E), ALU.mult)
            link(dve.tensor_tensor(r3(1), r3(4), bc(rf(3), E), ALU.mult))
            dve.tensor_tensor(r3(6), r3(5), r3(1), ALU.add).then_inc(s("gates"), 1)
            rows_of_gates(1)
            dve.sem_inc(s("swiglu"), 2)
            for e in range(E):
                dve.wait_ge(s(f"ld_gate{e}"), 32)
            with dve.Fori(0, NCH) as cc:
                for m in range(2 * E):
                    k = cc * (2 * E) + m
                    dve.wait_ge(s("h2_mm"), k + 1)
                    dve.wait_ge(s("silu2"), k + 3)
                    dve.tensor_tensor(arr(9)[:, (2 + m % 2) * CH:(3 + m % 2) * CH], arr(9)[:, (m % 2) * CH:(m % 2 + 1) * CH],
                                      ps[:, 5 + 2 * (m % 2), :], ALU.mult).then_inc(s("swiglu"), 1)
                    dve.wait_ge(s("g_used"), k + 1)
                    dve.wait_ge(s("swiglu"), k + 3)
                    dve.tensor_tensor(arr(8)[:, (m % 2) * CH:(m % 2 + 1) * CH], arr(9)[:, (2 + m % 2) * CH:(3 + m % 2) * CH],
                                      arr(m // 2)[:, bass.ds(cc * CH, CH)], ALU.mult).then_inc(s("gated2"), 1)
            for c in range(NCH):
                add_to_x("b2", c)

            link(dve.tensor_tensor(small[:, 32:48], lam_rows[:, 0:16], lam_rows[:, 16:32], ALU.mult))
            dve.tensor_reduce(small[:, 20:22], small[:, 32:48].rearrange("p (a d) -> p a d", a=2), AX.X, ALU.add
                              ).then_inc(s("lam_sum"), 1)
            layernorm("a3")
            dve.wait_ge(s("ld_rope"), 16)
            for n in range(2 * NCH + 1):
                if n < 2 * NCH:
                    o = (n // 2 % CPB) * CH
                    cos, sin = arr(10)[:, o:o + CH], arr(10)[:, SEQ + o:SEQ + o + CH]
                    x0, x1 = ps[:, 4 + 2 * (n % 2), :], ps[:, 5 + 2 * (n % 2), :]
                    dve.wait_ge(s("qk3_mm"), 2 * n + 2)
                    if n >= 1:
                        dve.wait_ge(s("roped"), 2 * n)
                    for k, (x, y) in enumerate(((x0, cos), (x1, sin), (x1, cos), (x0, sin))):
                        last = dve.tensor_tensor(arr(0)[:, k * CH:(k + 1) * CH], y, x, ALU.mult)
                    last.then_inc(s("rope_read"), 1)
                if n >= 1:
                    for i in range(2):
                        unit = 2 * (n - 1) + i
                        dve.wait_ge(s("roped"), unit + 1)
                        other_parts(dve, A3, unit, roped(unit), HD ** -0.5 if (n - 1) % 2 == 0 else 1.0)
            dve.wait_ge(s("lam_exp"), 1)
            link(dve.tensor_tensor(small[:, 24:25], small[:, 23:24], small[:, 22:23], ALU.subtract))
            link(dve.tensor_scalar(small[:, 25:26], small[:, 24:25], -LAMBDA_INIT, None, ALU.add))
            maxima(dve, A3)
            for c in range(NCH):
                add_to_x("a3", c)

            dve.memset(hT[:, :, 0:1], 0.0)
            for j, name in enumerate(("mu_k", "mu_r")):
                last = dve.tensor_scalar(small[:, 26 + j:27 + j], col(name), -1.0, 1.0, ALU.mult, ALU.add)
            link(last)
            for j, (name, mu) in enumerate((("wk", "mu_k"), ("wr", "mu_r"))):
                dve.tensor_scalar(arr(4)[:, 2 * j * C:(2 * j + 1) * C], w(3, name), col(mu), None, ALU.mult).then_inc(s("w3_mixed"), 1)
                dve.tensor_scalar(arr(4)[:, (2 * j + 1) * C:(2 * j + 2) * C], w(3, name), small[:, 26 + j:27 + j], None,
                                  ALU.mult).then_inc(s("w3_mixed"), 1)
            layernorm("b3")
            for c in range(NCH):
                dve.wait_ge(s("cm_k"), c + 1)
                dve.tensor_tensor(arr(2)[:, tok(c)], arr(1)[:, tok(c)], arr(1)[:, tok(c)], ALU.mult).then_inc(s("cm_sq"), 1)
                if c >= 1:
                    gate_out(dve, c - 1)
                    if c >= 2:
                        add_to_x("b3", c - 2)
            gate_out(dve, NCH - 1)
            add_to_x("b3", NCH - 2)
            add_to_x("b3", NCH - 1)

        @block.gpsimd
        def _(pool):
            pool.memset(mhalf[:], -0.5).then_inc(s("mhalf"), 1)
            pool.wait_ge(s("mhalf"), 1)

            def rsqrt(n):
                pool.wait_ge(s("ln_var"), n + 1)
                pool.tensor_tensor(rstd[:], var[:], mhalf[:], ALU.pow).then_inc(s("ln_rstd"), 1)

            def zero_v(a):
                va, _ = group_v(a)
                pool.memset(vall, 0.0).then_inc(s(a.name + "_vzero"), 1)
                pool.wait_ge(s(a.name + "_vzero"), 1)
                pool.memset(va.rearrange("p g k n d -> p (g k n) d")[:, :, a.width:a.width + 1], 1.0).then_inc(s(a.name + "_vzero"), 1)

            for n in range(3):
                rsqrt(n)
            for c in range(NCH):
                pool.wait_ge(s("hid_var"), c + 1)
                pool.tensor_tensor(rstd[:, 0:TPC], var[:, 0:TPC], mhalf[:, 0:TPC], ALU.pow).then_inc(s("hid_rstd"), 1)
            for n in range(3, 7):
                rsqrt(n)
            zero_v(A2)
            rsqrt(7)
            rsqrt(8)
            zero_v(A3)
            for n in range(2 * NCH):
                pool.wait_ge(s("rope_read"), n + 1)
                for i, op in enumerate((ALU.subtract, ALU.add)):
                    if n >= 2:
                        pool.wait_ge(s("a3_rest"), 2 * n + i - 3)
                    pool.tensor_tensor(roped(2 * n + i), arr(0)[:, 2 * i * CH:(2 * i + 1) * CH],
                                       arr(0)[:, (2 * i + 1) * CH:(2 * i + 2) * CH], op).then_inc(s("roped"), 1)
            rsqrt(9)


def kernel(**inputs):
    import ml_dtypes
    import concourse.bacc as bacc
    from concourse.bass_utils import run_bass_kernel_spmd

    def a(name):
        return np.asarray(inputs[name])

    def cat(parts):
        return np.ascontiguousarray(np.concatenate(parts, axis=1))

    def down(m):
        return m.reshape(-1, P, m.shape[1]).transpose(1, 0, 2).reshape(P, -1)

    arrays = {
        "x": a("L0_attn_x"),
        "wmod": np.ascontiguousarray(np.stack([a(f"L{i}_wmod") for i in range(4)])),
        "w0": cat([a("L0_attn_W_key").T, a("L0_attn_W_value").T, a("L0_attn_W_receptance").T, a("L0_attn_W_output").T,
                   a("L0_ffn_w1").T, down(a("L0_ffn_w2").T)]),
        "w1": cat([a("L1_attn_Wq").T, a("L1_attn_Wv").T, a("L1_attn_Wg").T, a("L1_attn_Wo").T, a("L1_ffn_router_w").T,
                   a("L1_ffn_expert_w").transpose(2, 0, 1).reshape(C, -1)]),
        "w2": cat([a("L2_attn_w_in").T, a("L2_attn_w_out").T, a("L2_ffn_Wg").T, a("L2_ffn_W1").transpose(2, 0, 1).reshape(C, -1),
                   a("L2_ffn_W2").transpose(2, 0, 1).reshape(C, -1), down(a("L2_ffn_W3").transpose(0, 2, 1).reshape(-1, C))]),
        "w3": cat([a("L3_attn_W_qkv").T, down(a("L3_attn_W_proj").T), a("L3_ffn_W_r").T, a("L3_ffn_W_k").T, a("L3_ffn_W_v").T]),
    }
    vectors = {
        "c": np.concatenate([a(f"L{i}_c").T for i in range(4)], axis=1), "decay": a("L0_attn_time_decay"),
        "first": a("L0_attn_time_first"), "mix_k": a("L0_attn_time_mix_k"), "mix_v": a("L0_attn_time_mix_v"),
        "mix_r": a("L0_attn_time_mix_r"), "ln1_g": a("L0_ffn_ln1_g"), "ln1_b": a("L0_ffn_ln1_b"),
        "ln2_g": a("L0_ffn_ln2_g").reshape(4, P).T, "ln2_b": a("L0_ffn_ln2_b").reshape(4, P).T, "b2": a("L0_ffn_b2"),
        "beta": np.repeat(a("L1_attn_beta"), HD), "gamma": a("L1_attn_ln_gamma"), "lnb": a("L1_attn_ln_beta"),
        "mu_r": a("L3_ffn_mu_r"), "mu_k": a("L3_ffn_mu_k"),
    }
    arrays["columns"] = cat([vectors[name].reshape(P, width) for name, width in COLUMNS])
    arrays["rows"] = cat([v.reshape(1, -1) for v in (
        a("L0_ffn_b1"), a("L1_ffn_router_b"), np.arange(E, 0, -1, dtype=np.float32), a("L3_attn_lambda_q1"),
        a("L3_attn_lambda_q2"), a("L3_attn_lambda_k1"), a("L3_attn_lambda_k2"))])
    arrays["expert_b"] = a("L1_ffn_expert_b")

    arrays["ident"] = np.eye(P, dtype=np.float32)
    inv = (1.0 / np.float32(10000.0) ** (np.arange(0, 2 * HD, 2, dtype=np.float32) / np.float32(2 * HD))).astype(np.float32)
    angle = np.tile(np.arange(SEQ, dtype=np.float32)[None, :] * inv[:, None], (HEADS, 1))
    arrays["rope"] = np.concatenate([np.cos(angle), np.sin(angle)], axis=1).astype(np.float32)
    key, query = np.arange(P)[:, None], np.arange(P)[None, :]
    arrays["masks"] = np.concatenate([np.full((P, P), MASKED), np.where(key > query, MASKED, 0.0),
                                      np.where(query > key, MASKED, 0.0)], axis=1).astype(ml_dtypes.bfloat16)
    slopes = (2.0 ** (-8.0 / HEADS * (np.arange(HEADS) + 1.0))).astype(np.float32)
    left = slopes[:, None] * np.arange(SEQ, dtype=np.float32)[None, :]
    alibi = []
    for _ in range(3):
        alibi.append(left.astype(ml_dtypes.bfloat16))
        left = left - alibi[-1].astype(np.float32)
    arrays["alibi"] = np.stack(alibi)
    arrays["ones"] = np.ones((3, SLOTS * SEQ), ml_dtypes.bfloat16)

    nc = bacc.Bacc("TRN2", target_bir_lowering=False, num_devices=1)
    fed = {f"in_{k}": np.ascontiguousarray(v) for k, v in arrays.items()}
    d = {k: nc.dram_tensor(f"in_{k}", v.shape, mybir.dt.from_np(v.dtype), kind="ExternalInput").ap()
         for k, v in ((k, fed[f"in_{k}"]) for k in arrays)}
    out = nc.dram_tensor("out", (B, SEQ, C), F32, kind="ExternalOutput").ap()
    adaln_stack(nc, d["x"], {"wmod": d["wmod"], 0: d["w0"], 1: d["w1"], 2: d["w2"], 3: d["w3"]}, d["columns"], d["rows"],
                d["expert_b"], d["ident"], d["rope"], d["masks"], d["alibi"], d["ones"], out)
    return run_bass_kernel_spmd(nc, [fed], core_ids=[0]).results[0]["out"]
```

```python
from contextlib import ExitStack

import numpy as np

import concourse.bass as bass
from concourse import mybir

F32 = mybir.dt.float32
BF16 = mybir.dt.bfloat16
F16 = mybir.dt.float16
ALU = mybir.AluOpType
ACT = mybir.ActivationFunctionType
AX = mybir.AxisListType

P = 128
B, SEQ, C = 2, 1024, 128
TOK = B * SEQ
NT = TOK // P
CH = 512
NCH = TOK // CH
TPC = CH // P
CPB = SEQ // CH
E = 8
H1 = 512
HE = 2 * C
HEADS, HD = 16, 8
EPS = 1e-5
LOWEST = -1e38
ROUND = 12582912.0
MASKED = -1e30
LIFT = 12 * float(np.log(2.0))
LAMBDA_INIT = 0.8 - 0.6 * float(np.exp(-0.3 * 0))

WEIGHTS = {
    0: [("wmod", 6 * C), ("key", C), ("value", C), ("recept", C), ("out", C), ("w1", H1), ("w2", H1)],
    1: [("wmod", 6 * C), ("q", C), ("v", C), ("g", C), ("out", C), ("router", E), ("expert", E * C)],
    2: [("wmod", 6 * C), ("q", C), ("k", C), ("v", C), ("out", C), ("router", E),
        ("w1", E * HE), ("w2", E * HE), ("w3", E * HE)],
    3: [("wmod", 6 * C), ("q0", C), ("q1", C), ("k0", C), ("k1", C), ("v", 2 * C), ("out", 2 * C),
        ("wr", C), ("wk", C), ("wv", C)],
}
COLUMNS = [("c", 8), ("decay", 1), ("first", 1), ("mix_k", 1), ("mix_v", 1), ("mix_r", 1), ("ln1_g", 1),
           ("ln1_b", 1), ("ln2_g", 4), ("ln2_b", 4), ("b2", 1), ("beta", 1), ("gamma", 1), ("lnb", 1),
           ("mu_r", 1), ("mu_k", 1)]


def places(items):
    at, out = 0, {}
    for name, width in items:
        out[name] = (at, width)
        at += width
    return out, at


PAIRS_Q = [0, 1, 2, 0, 1, 0]
PAIRS_K = [0, 0, 0, 1, 1, 2]
ROWS = HD * len(PAIRS_Q)
HALF = 64
MAX_ROWS = P - 6
SLOTS = 4
SETS = 2 * SLOTS
SPLIT = 2
QT = SEQ // P


class Attention:

    def __init__(self, name, heads, width, causal, groups):
        self.name, self.heads, self.width, self.causal, self.groups = name, heads, width, causal, groups
        self.own_rows = ROWS + (3 if causal else 0)
        self.strip = 32 if 3 * (width + 1) <= 32 else 64
        self.obanks = SLOTS * self.strip // P
        self.out_cols = SLOTS * (width + 1)
        self.batches = []
        for pos in range(2):
            for qc in range(CPB):
                for kt in range(0, TPC * (qc + 1) if causal else QT, 2):
                    self.batches.append((qc, pos, kt, max(0, kt - TPC * qc) * P if causal else 0))
        self.nbatch = len(self.batches)
        self.nsteps = SLOTS * self.nbatch
        self.ends = [b for b in range(self.nbatch)
                     if b + 1 == self.nbatch or self.batches[b + 1][0:2] != self.batches[b][0:2]]
        uses = []
        for b in range(self.nbatch):
            uses += [("step", SLOTS * b + sl, 0) for sl in range(SLOTS)]
            uses += [("turn", j, 0 if e + 2 < self.nbatch else -1) for j, e in enumerate(self.ends)
                     if b == (e + 2) % self.nbatch]
        assert len(uses) % 2 == 0
        self.pair = {use[0:2]: k % 2 for k, use in enumerate(uses)}
        self.before = {use[0:2]: (uses[k - 2][0:2], uses[k - 2][2] - use[2] - (1 if k < 2 else 0)) for k, use in enumerate(uses)}
        self.lead = 7 if causal else 5
        self.pieces = []
        for pos in range(2):
            for qt in range(QT):
                for sl in range(SLOTS):
                    keys = P * (qt + 1) if causal else SEQ
                    for pc in range(-(-keys // CH)):
                        self.pieces.append((pos, sl, qt, pc, min(CH, keys - pc * CH)))
        self.npieces = len(self.pieces)
        length = [(1, 1, 1, 1), (1, 1, 2, 0), (1, 1, 2, 0), (1, 1, 1, 1)]
        room = [0 if k < (6 if causal else 6) else x * (0.9 if any(k // SLOTS == (e + 3) % self.nbatch for e in self.ends) else 1.0)
                for k in range(self.nsteps - self.lead) for x in length[k % SLOTS]]
        price = [CH // 8 + keys for _, _, _, _, keys in self.pieces]
        self.at = [sum(1 for m in range(self.npieces)
                       if sum(price[:m + 1]) <= sum(price) * sum(room[:k]) / sum(room) + 1) for k in range(4 * self.nsteps + 1)]
        self.turn_at = self.nsteps - self.lead
        self.loads = 2 * len(PAIRS_Q) + (1 if causal else 0)


def half_of(u, pos):
    return pos if u == 0 else 1 - pos


A2 = Attention("a2", 8, HD, True, 4)
A3 = Attention("a3", 4, 2 * HD, False, 8)


def adaln_stack(nc, x_in, w_in, columns_in, rows_in, expertb_in, ident_in, rope_in, masks_in, alibi_in,
                ones_in, heads_in, out):
    wplace = {layer: places(items)[0] for layer, items in WEIGHTS.items()}
    wwidth = {layer: places(items)[1] - 6 * C for layer, items in WEIGHTS.items()}
    col_at, ncols = places(COLUMNS)

    with ExitStack() as ctx:
        def sb(name, shape, dt=F32):
            return ctx.enter_context(nc.sbuf_tensor(name, shape, dt))

        def sem(name):
            return ctx.enter_context(nc.semaphore(name))

        x_tok = sb("x_tok", [P, NT, C])
        xn = sb("xn", [P, NT, C])
        hT = sb("hT", [P, B, SEQ + 1])
        hF = hT[:].rearrange("p b s -> p (b s)")[:, 0:TOK]
        work = sb("work", [P, 12 * TOK])
        w02 = sb("w02", [P, wwidth[2]])
        w13 = sb("w13", [P, wwidth[1] + wwidth[3]])
        cols = sb("cols", [P, ncols])
        rowc = sb("rowc", [P, H1 + 2 * E + 4 * HD])
        expertb = sb("expertb", [E, C])
        ident = sb("ident", [P, P])
        ident16 = sb("ident16", [P, P], BF16)
        mask16 = sb("mask16", [P, 3 * P], BF16)
        ones = sb("ones", [P, P])
        mod = sb("mod", [P, 4, 6, B])
        modx = sb("modx", [P, 4, 2, B])
        silc = sb("silc", [P, 8])
        stats = sb("stats", [P, NT, 6])
        mv = sb("mv", [P, NT, 2])
        var = sb("var", [P, NT])
        rstd = sb("rstd", [P, NT])
        mhalf = sb("mhalf", [P, NT])
        lift = sb("lift", [P, 1])
        small = sb("small", [P, 64])
        route = sb("route", [P, 8, NT * E])
        rone = sb("rone", [P, 6, NT])
        mcol = sb("mcol", [P, SETS * QT, 2])
        negm = sb("negm", [P, P])
        mrest = sb("mrest", [SETS * QT, P])
        mpart = sb("mpart", [SETS * QT, 3, P], BF16)
        rz = sb("rz", [P, TPC, SLOTS, 1])
        heads = sb("heads", [P, A2.out_cols + A3.obanks * A3.out_cols])
        ohalf = sb("ohalf", [P, 3, TPC * SLOTS * 2 * HD])
        qs = sb("qs", [P, 2, SLOTS, SEQ], BF16)
        ks0 = sb("ks0", [P, 2, SLOTS, SEQ], BF16)
        ps = ctx.enter_context(nc.psum_tensor("ps", [P, 8, CH], F32))

        def arr(n):
            return work[:, n * TOK:(n + 1) * TOK]

        def w(layer, name):
            at, width = wplace[layer][name]
            at -= 6 * C
            if layer in (0, 2):
                return w02[:, at:at + width]
            at += wwidth[1] if layer == 3 else 0
            return w13[:, at:at + width]

        def col(name, j=0):
            at = col_at[name][0] + j
            return cols[:, at:at + 1]

        k1_at = wplace[2]["w1"][0] - 6 * C
        ks1 = w02[:, k1_at:k1_at + SLOTS * SEQ].bitcast(BF16).rearrange("p (u n t) -> p u n t", u=2, n=SLOTS)
        ks = (ks0, ks1)

        b1_row = rowc[:, 0:H1]
        routerb_row = rowc[:, H1:H1 + E]
        tie_row = rowc[:, H1 + E:H1 + 2 * E]
        lam_rows = rowc[:, H1 + 2 * E:]

        def dram(name, shape, dt=F32):
            return nc.dram_tensor(name, shape, dt, kind="Internal").ap()

        gates1 = dram("gates1", [NT, E, P])
        gates2 = dram("gates2", [NT, E, P])
        qd2 = dram("qd2", [1, A2.groups, 3, A2.heads * HD, SEQ], BF16)
        kd2 = dram("kd2", [1, A2.groups, 3, A2.heads * HD, SEQ], BF16)
        qd3 = dram("qd3", [2, A3.groups, 3, A3.heads * HD, SEQ], BF16)
        kd3 = dram("kd3", [2, A3.groups, 3, A3.heads * HD, SEQ], BF16)

        S = {}

        def s(name):
            if name not in S:
                S[name] = sem(name)
            return S[name]

        wmod = work[:, 0:4 * 6 * C].rearrange("p (l n) -> p l n", l=4)
        pslots = work[:, 0:8 * 2 * CH].rearrange("p (n k q) -> p n k q", n=8, k=2)
        phigh = work[:, 0:8 * 2 * CH].bitcast(BF16).rearrange("p (n k q two) -> p n k q two", n=8, k=2, two=2)[:, :, :, :, 1]
        plow = arr(9).bitcast(F16).rearrange("p (n k q) -> p n k q", n=4, k=2)
        vall = work[:, 4 * TOK:8 * TOK]
        vgrp = arr(8).bitcast(BF16).rearrange("p (u n) -> p u n", u=2)
        otok = work[:, 10 * TOK:12 * TOK]

        def low_slot(k):
            return k // SLOTS % 2 * SPLIT + k % SLOTS

        def group_v(a):
            n = SETS if a.causal else SLOTS
            size = a.groups * QT * n * a.strip
            return (vall.bitcast(BF16)[:, 0:size].rearrange("p (g k n d) -> p g k n d", g=a.groups, k=QT, n=n),
                    [vgrp[:, u].rearrange("p (k n d) -> p k n d", k=QT, n=n) for u in range(2)])

        def group_v32(a):
            n = SETS if a.causal else SLOTS
            return (vall[:, 0:a.groups * QT * n * a.strip // 2].rearrange("p (g k n d) -> p g k n d", g=a.groups, k=QT, n=n),
                    [arr(8)[:, u * SEQ:(u + 1) * SEQ].rearrange("p (k n d) -> p k n d", k=QT, n=n) for u in range(2)])

        LN = {"a0": 0, "b0": 1, "in0": 2, "a1": 3, "y1": 4, "b1": 5, "a2": 6, "b2": 7, "a3": 8, "b3": 9}
        VAR = [n + 1 + (NCH if n > 2 else 0) for n in range(len(LN))]
        OUT = {"a0": 0, "b0": 1, "a1": 2, "b1": 3, "a2": 4, "b2": 5, "a3": 6, "b3": 7}
        OUT_MM = {"a0": 0, "b0": 1, "a1": 2, "b1": 3, "a2": 4, "a3": 5, "b3": 6}

        def hid(n):
            return work[:, TOK + (n % 8) * H1:TOK + (n % 8 + 1) * H1]

        def hid_T(c):
            return arr(3 + c % 2).rearrange("p (j t) -> p j t", j=4)

        def parts_ring(slot):
            return arr(2 + slot // 2)[:, (slot % 2) * 1024:(slot % 2) * 1024 + 768].bitcast(BF16).rearrange(
                "p (n t) -> p n t", n=3)

        def side(k):
            return xn[:].rearrange("p t c -> p (t c)")[:, k * 2 * CH:(k + 1) * 2 * CH]

        def o_tile(a, t, hf):
            at = ((t // QT * halves_of(a) + hf) * QT + t % QT) * P
            return otok[:, at:at + P]

        def halves_of(a):
            return 1 if a.causal else 2

        def wkv_temp(b, k):
            n = 4 * b + k
            if n < 4:
                return work[:, 9 * TOK + n * SEQ:9 * TOK + (n + 1) * SEQ]
            if n < 6:
                return xn[:].rearrange("p t c -> p (t c)")[:, (n - 4) * SEQ:(n - 3) * SEQ]
            return work[:, 768:768 + SEQ] if n == 6 else work[:, 9 * TOK - SEQ:9 * TOK]

        def wkv_state(k):
            at = 5 * TOK + k * B * (SEQ + 1)
            return work[:, at:at + B * (SEQ + 1)].rearrange("p (b s) -> p b s", b=B)

        def roped(unit):
            return arr(1)[:, (unit % 4) * CH:(unit % 4 + 1) * CH]

        def v_pieces(a):
            return range(2)

        def v_place(a, t, h, v, slots, at):
            per_b = a.groups // B
            first = SLOTS * h if a.causal else 0
            return v[:, per_b * (t // QT):per_b * (t // QT + 1), t % QT, first + slots.start:first + slots.stop, at:at + HD]

        def v_part(a, t, part, h):
            at = part * (a.width + 1) + (0 if a.causal else HD * h)
            return v_place(a, t, h, group_v(a)[0], range(0, SPLIT), at)

        def v_whole(a, t, h):
            return v_place(a, t, h, group_v32(a)[0], range(SPLIT, SLOTS), 0 if a.causal else HD * h)

        def v_made(a, t, h, split):
            src = ps[:, 6 + t % 2, 0:halves_of(a) * C]
            first = 0 if split else SPLIT
            if a.causal:
                return src.rearrange("p (g h n d) -> p g h n d", g=a.groups // B, h=2, d=HD)[:, :, h, first:first + SPLIT]
            return src.rearrange("p (h g n d) -> p h g n d", h=2, g=a.groups // B, d=HD)[:, h, :, first:first + SPLIT]

        def v_rest(a, t, h):
            at = SEQ + (t % 2) * 2 * C + h * C
            return arr(11)[:, at:at + a.groups // B * SPLIT * HD].rearrange("p (g n d) -> p g n d", g=a.groups // B, d=HD)

        def rest(unit):
            return arr(11)[:, (unit % 2) * CH:(unit % 2 + 1) * CH]

        block = ctx.enter_context(nc.Block())

        def tok(c):
            return slice(c * CH, (c + 1) * CH)

        def h_chunk(c, shift=0):
            b, o = c // CPB, (c % CPB) * CH
            return hT[:, b, 1 + o - shift:1 + o - shift + CH]

        def attention_transfers(sp, a, qd, kd):
            n = a.name
            narr = 1 if a.causal else 2
            per_b = a.groups // B
            rows = a.heads * HD
            units = [(ar, c) for c in range(NCH) for ar in range(2 * narr)]
            for unit, (ar, c) in enumerate(units):
                b, o = c // CPB, (c % CPB) * CH
                dst = (qd, kd)[ar // narr]
                sp.wait_ge(s(n + "_parts"), unit + 1)
                for hg in range(per_b):
                    sp.dma_start(dst[ar % narr, per_b * b + hg, :, :, o:o + CH].rearrange("p r t -> r p t"),
                                 parts_ring(unit % 4)[rows * hg:rows * (hg + 1)]).then_inc(s(f"{n}_st{unit % 4}"), 16)
            for slot in range(4):
                sp.wait_ge(s(f"{n}_st{slot}"), 16 * per_b * (len(units) // 4))
            sp.wait_ge(s("stacks_clear"), 1 if a.causal else 2)
            for u in range(2):
                for i in range(2):
                    r, m = HALF * i + ROWS, MAX_ROWS + 3 * i
                    if a.causal:
                        sp.dma_start(qs[r:r + 3, u].rearrange("p n t -> p (n t)"), ones_in).then_inc(s(n + "_ones"), 16)
                    sp.dma_start(ks[i][m:m + 3, u].rearrange("p n t -> p (n t)"), ones_in).then_inc(s(n + "_ones"), 16)
            va, vg = group_v32(a)
            vflat = va.rearrange("p g k n d -> p g (k n d)")

            def load(g, u, pos):
                i = half_of(u, pos)
                r = HALF * i
                half, first = (0, SLOTS * HD * i) if a.causal else (i, 0)
                for stack, src, pairs in ((qs, qd, PAIRS_Q), (ks[i], kd, PAIRS_K)):
                    for j, part in enumerate(pairs):
                        sp.dma_start(stack[r + HD * j:r + HD * (j + 1), u],
                                     src[half, bass.ds(g, 1), part, first:first + SLOTS * HD, :].rearrange(
                                         "g (n d) t -> (g d) n t", d=HD)).then_inc(s(f"{n}_ld{u}{i}"), 16)
                if a.causal:
                    head = a.heads * (g % 2) + SLOTS * i
                    sp.dma_start(ks[i][r + ROWS:r + ROWS + 3, u], alibi_in[:, head:head + SLOTS, :]
                                 ).then_inc(s(f"{n}_ld{u}{i}"), 16)

            def load_v(g, u):
                sp.dma_start(vg[u].rearrange("p k n d -> p (k n d)"), vflat[:, bass.ds(g, 1)].rearrange("p g n -> p (g n)")
                             ).then_inc(s(f"{n}_ldv{u}"), 16)

            def load_max(g, u):
                sp.wait_ge(s(n + "_msplit"), g + 1)
                for i in range(2):
                    for p in range(3):
                        sp.dma_start(qs[MAX_ROWS + 3 * i + p:MAX_ROWS + 3 * i + p + 1, u].rearrange("r n (q t) -> r (n q) t", t=P),
                                     mpart[32 * i:32 * i + 32, p, :]).then_inc(s(n + "_mld"), 16)

            for u in range(2):
                for pos in range(2):
                    load(u, u, pos)
            sp.wait_ge(s(n + "_v"), NT)
            for u in range(2):
                load_v(u, u)
            load_max(0, 0)

            def loads_beside(g, u, following, second):
                if following:
                    load_max(g + 1, 1 - u)
                if second:
                    sp.wait_ge(s(n + "_sc"), (g + 1) * a.nsteps)
                    load(g + 2, u, 0)
                    load(g + 2, u, 1)
                    sp.wait_ge(s(n + "_pv"), (g + 1) * a.nbatch + 2)
                    load_v(g + 2, u)

            def pair(g):
                loads_beside(g, 0, True, True)
                loads_beside(g + 1, 1, True, True)

            if a.groups > 4:
                with sp.Fori(0, a.groups // 2 - 1) as it:
                    pair(it * 2)
            else:
                pair(0)
            loads_beside(a.groups - 2, 0, True, False)

        @block.sync
        def _(sp):
            sp.dma_start(cols[:], columns_in).then_inc(s("ld_first"), 16)
            sp.dma_start(wmod[:], w_in["wmod"].rearrange("l p n -> p l n")).then_inc(s("ld_first"), 16)
            sp.dma_start(ident[:], ident_in).then_inc(s("ld_first"), 16)
            for c in range(NCH):
                sp.dma_start(x_tok[:, TPC * c:TPC * c + TPC, :],
                             x_in.rearrange("b s d -> (b s) d")[tok(c), :].rearrange("(t p) d -> p t d", p=P)
                             ).then_inc(s("ld_x"), 16)
            sp.dma_start(w02[:, 0:wwidth[0]], w_in[0]).then_inc(s("ld_w0"), 16)
            sp.dma_start(rowc[:], rows_in.to_broadcast([P, H1 + 2 * E + 4 * HD])).then_inc(s("ld_w0"), 16)
            sp.dma_start(w13[:, 0:wwidth[1]], w_in[1]).then_inc(s("ld_w13"), 16)
            sp.dma_start(w13[:, wwidth[1]:], w_in[3]).then_inc(s("ld_w13"), 16)
            sp.dma_start(expertb[:], expertb_in).then_inc(s("ld_w13"), 16)
            sp.dma_start(mask16[:], masks_in).then_inc(s("ld_const"), 16)
            sp.dma_start(heads[:], heads_in).then_inc(s("ld_const"), 16)
            sp.wait_ge(s("out_mm"), NCH * (OUT_MM["b0"] + 1))
            sp.dma_start(w02[:, 0:k1_at], w_in[2][:, 0:k1_at]).then_inc(s("ld_w2"), 16)
            sp.wait_ge(s("gate_rows"), 1)
            sp.dma_start(gates1.rearrange("t e p -> (t e) p"), route[:, 7, :]).then_inc(s("st_gate"), 16)
            sp.wait_ge(s("st_gate"), 16)
            for e in range(E):
                sp.dma_start(arr(e).rearrange("p (t k) -> p t k", k=P),
                             gates1[:, e, :].rearrange("t (u k) -> u t k", u=1).to_broadcast([P, NT, P])
                             ).then_inc(s("ld_gates"), 16)
            sp.dma_start(arr(9)[0:E, :].rearrange("e (t k) -> e t k", k=P), gates1.rearrange("t e k -> e t k")).then_inc(s("ld_gater"), 16)

            attention_transfers(sp, A2, qd2, kd2)
            sp.wait_ge(s("a2_pv"), A2.groups * A2.nbatch + 2)
            sp.dma_start(w02[:, k1_at:wwidth[2]], w_in[2][:, k1_at:wwidth[2]]).then_inc(s("ld_w2"), 16)
            sp.wait_ge(s("gate_rows"), 2)
            sp.dma_start(gates2.rearrange("t e p -> (t e) p"), route[:, 7, :]).then_inc(s("st_gate"), 16)
            sp.wait_ge(s("st_gate"), 32)
            for e in range(E):
                sp.dma_start(arr(e).rearrange("p (t k) -> p t k", k=P),
                             gates2[:, e, :].rearrange("t (u k) -> u t k", u=1).to_broadcast([P, NT, P])
                             ).then_inc(s("ld_gates"), 16)
            sp.wait_ge(s("x_upd"), NCH * (OUT["b2"] + 1))
            sp.dma_start(arr(10), rope_in).then_inc(s("ld_rope"), 16)
            attention_transfers(sp, A3, qd3, kd3)
            for c in range(NCH):
                sp.wait_ge(s("x_upd"), NCH * OUT["b3"] + c + 1)
                sp.dma_start(out.rearrange("b s d -> (b s) d")[tok(c), :].rearrange("(t p) d -> p t d", p=P),
                             x_tok[:, TPC * c:TPC * c + TPC, :]).then_inc(s("st_out"), 16)
            sp.wait_ge(s("st_out"), 16 * NCH)

        def value_products(pe, a, wv, width):
            if not a.causal:
                pe.wait_ge(s("rope_read"), 2 * NCH)
            for t in range(NT):
                if t >= 2:
                    pe.wait_ge(s(a.name + "_vrest"), t - 1)
                pe.matmul(ps[:, 6 + t % 2, 0:width], hF[:, t * P:(t + 1) * P], wv, start=True,
                          stop=True).then_inc(s(a.name + "_vmm"), 1)

        def attention_products(pe, a):
            n = a.name
            vg, vg32 = group_v(a)[1], group_v32(a)[1]
            nb, ns, np_ = a.nbatch, a.nsteps, a.npieces

            def pair_free(g, use):
                (kind, k), away = a.before[use]
                if kind == "step":
                    pe.wait_ge(s(n + "_exp"), (g + away) * ns + k + 3)
                else:
                    pe.wait_ge(s(n + "_oread"), (g + away) * 4 + k + 2)

            def piece(g, u, m):
                pos, sl, qt, pc, keys = a.pieces[m]
                i = half_of(u, pos)
                lo = HALF * i
                if m == 0:
                    wait_loaded(g, u, half_of(u, 0))
                    if not (isinstance(g, int) and g == 0):
                        pe.wait_ge(s(n + "_msplit"), g)
                if m == np_ // 2:
                    wait_loaded(g, u, half_of(u, 1))
                bank = ps[:, 4 + m % 2, 0:keys]
                pe.wait_ge(s(n + "_mx"), g * np_ + m + 1)
                diag = a.causal and (pc + 1) * CH >= P * (qt + 1)
                rows = slice(lo, lo + a.own_rows) if pos == 0 else slice(0, MAX_ROWS)
                last = pe.matmul(bank, qs[rows, u, sl, qt * P:(qt + 1) * P], ks[i][rows, u, sl, pc * CH:pc * CH + keys],
                                 start=True, stop=not diag)
                if diag:
                    last = pe.matmul(ps[:, 4 + m % 2, keys - P:keys], ident16[:], mask16[:, 2 * P:3 * P],
                                     start=False, stop=True)
                last.then_inc(s(n + "_mxmm"), 1)

            def turn_max(g):
                pe.wait_ge(s(n + "_neg"), g + 1)
                pe.transpose(ps[:, 4, 0:P], negm[:], ident[:]).then_inc(s(n + "_mturn"), 1)

            def scores(g, u, beta, sl, h):
                qc, pos, kt, f = a.batches[beta]
                k = SLOTS * beta + sl
                i = half_of(u, pos)
                if h == 0:
                    pair_free(g, ("step", k))
                bank = 2 * a.pair["step", k] + h
                diag = a.causal and kt >= TPC * qc
                last = pe.matmul(ps[:, bank, f:CH], ks[i][:, u, sl, (kt + h) * P:(kt + h + 1) * P],
                                 qs[:, u, sl, qc * CH + f:(qc + 1) * CH], start=True, stop=not diag)
                if diag and h == 0:
                    last = pe.matmul(ps[:, bank, f:f + P], ident16[:], mask16[:, P:2 * P], start=False, stop=True)
                if diag and h == 1:
                    last = pe.matmul(ps[:, bank, f:f + 2 * P], ident16[:], mask16[:, 0:2 * P], start=False, stop=True)
                if h == 1:
                    last.then_inc(s(n + "_sc"), 1)

            def weighted(g, u, beta, quarter, part):
                qc, pos, kt, f = a.batches[beta]
                first = SLOTS * half_of(u, pos) if a.causal else 0

                def product(stationary, sl, h, moving, start, stop):
                    g0 = f + (P * h if a.causal and kt >= TPC * qc else 0)
                    row = a.strip * sl
                    v = stationary[u][:, kt + h, first + sl, :]
                    return pe.matmul(ps[row % P:row % P + v.shape[-1], 6 + row // P, g0:CH], v, moving[:, h, g0:CH],
                                     start=(kt == 0 and start), stop=(beta in a.ends and stop), skip_group_check=True)

                k = SLOTS * beta
                copied = (g * 4 + 2 * pos + qc) * a.obanks
                if quarter == 0:
                    if part == 0:
                        pe.wait_ge(s(n + "_exp"), g * ns + SLOTS * (beta + 1) + 2)
                        if kt == 0:
                            pe.wait_ge(s(n + "_ocopy"), copied + 1)
                    for sl in range(SPLIT):
                        product(vg, sl, part, phigh[:, (k + sl) % 8], part == 0, False)
                if quarter in (1, 2) and part == 0:
                    if kt == 0 and quarter == 1:
                        pe.wait_ge(s(n + "_ocopy"), copied + a.obanks)
                    for sl in range(SPLIT, SLOTS):
                        product(vg32, sl, quarter - 1, pslots[:, (k + sl) % 8], quarter == 1, quarter == 2)
                if quarter == 3:
                    if part == 0:
                        pe.wait_ge(s(n + "_low"), (g * nb + beta + 1) * SPLIT)
                    for sl in range(SPLIT):
                        last = product(vg, sl, part, plow[:, low_slot(k + sl)], False, part == 1)
                    if part == 1:
                        last.then_inc(s(n + "_pv"), 1)

            def turn_out(g, j):
                pe.wait_ge(s(n + "_ocopy"), (g * 4 + j + 2) * a.obanks)
                if isinstance(g, int) and g == a.groups - 1 and a.ends[j] == nb - 1:
                    pe.wait_ge(s(n + "_exp"), a.groups * ns + 2)
                else:
                    pair_free(g, ("turn", j))
                at = 0 if a.causal else A2.out_cols
                for t in range(TPC):
                    for b2 in range(a.obanks):
                        last = pe.matmul(ps[:, 2 * a.pair["turn", j], t * a.out_cols:(t + 1) * a.out_cols],
                                         side(j % 2)[:, b2 * CH + t * P:b2 * CH + (t + 1) * P],
                                         heads[:, at + b2 * a.out_cols:at + (b2 + 1) * a.out_cols],
                                         start=(b2 == 0), stop=(b2 == a.obanks - 1))
                last.then_inc(s(n + "_oturn"), 1)

            def batch(g, u, beta, following, product):
                if beta == 0:
                    pe.wait_ge(s(n + "_mld"), 96 * (g + 1))
                    wait_loaded(g, u, 0)
                    wait_loaded(g, u, 1)
                for sl in range(SLOTS):
                    k = SLOTS * beta + sl
                    for x in range(4):
                        if x < 2:
                            scores(g, u, beta, sl, x)
                        elif product:
                            weighted(*product, sl, x - 2)
                        if following:
                            for m in range(a.at[4 * k + x], a.at[4 * k + x + 1]):
                                piece(g + 1, 1 - u, m)
                    if following and k == a.turn_at:
                        turn_max(g + 1)

            def main(g, u, following, after):
                for beta in range(2, nb + 2):
                    if beta == 2:
                        wait_loaded_v(g, u)
                    if beta == nb + 1 and following:
                        wait_loaded_v(g + 1, 1 - u)
                    product = (g, u, beta - 1) if beta <= nb else (g + 1, 1 - u, 0) if following else None
                    if beta < nb:
                        batch(g, u, beta, following, product)
                    elif following:
                        batch(g + 1, 1 - u, beta - nb, after, product)
                    elif product:
                        for x in range(8):
                            weighted(*product, x // 2, x % 2)
                    for j, e in enumerate(a.ends):
                        if beta == e + 2:
                            turn_out(g, j)

            def wait_loaded_v(g, u):
                if isinstance(g, int):
                    pe.wait_ge(s(f"{n}_ldv{u}"), 16 * (g // 2 + 1))
                else:
                    pe.wait_ge(s(f"{n}_ldv{u}"), g * 8 + (16 - 8 * u))

            def wait_loaded(g, u, i):
                if isinstance(g, int):
                    pe.wait_ge(s(f"{n}_ld{u}{i}"), 16 * a.loads * (g // 2 + 1))
                else:
                    pe.wait_ge(s(f"{n}_ld{u}{i}"), g * (8 * a.loads) + (16 - 8 * u) * a.loads)

            pe.sem_inc(s(n + "_pv"), 2)
            pe.sem_inc(s(n + "_oturn"), 2)
            pe.wait_ge(s(n + "_ones"), 16 * (8 if a.causal else 4))
            for m in range(np_):
                piece(0, 0, m)
            turn_max(0)

            wait_loaded_v(0, 0)
            batch(0, 0, 0, True, None)
            batch(0, 0, 1, True, (0, 0, 0))

            if a.groups > 4:
                with pe.Fori(0, a.groups // 2 - 1) as it:
                    main(it * 2, 0, True, True)
                    main(it * 2 + 1, 1, True, True)
            else:
                main(0, 0, True, True)
                main(1, 1, True, True)
            main(a.groups - 2, 0, True, False)
            main(a.groups - 1, 1, False, False)

        def attention_turns(pe, a):
            n = a.name
            halves = 1 if a.causal else 2
            if a.causal:
                pe.wait_ge(s(n + "_oread"), 4 * a.groups + 1)
            else:
                pe.wait_ge(s(n + "_odone"), 2 * a.groups)
            for c in range(NCH):
                for hf in range(halves):
                    k = halves * c + hf
                    if k >= 2:
                        pe.wait_ge(s(n + "_ctx"), k - 1)
                    for t in range(TPC):
                        last = pe.transpose(ps[:, 4 + k % 2, t * P:(t + 1) * P], o_tile(a, TPC * c + t, hf), ident[:])
                    last.then_inc(s(n + "_cturn"), 1)

        @block.tensor
        def _(pe):
            def layernorm(name):
                n = LN[name]
                for c in range(NCH):
                    pe.wait_ge(s("ln_normed"), NCH * n + c + 1)
                    for t in range(TPC):
                        last = pe.transpose(ps[:, c, t * P:(t + 1) * P], xn[:, TPC * c + t, :], ident[:])
                    last.then_inc(s("ln_turned"), 1)

            def to_tokens(src, name, ready, base):
                for c in range(NCH):
                    pe.wait_ge(ready, base + c + 1)
                    for t in range(TPC):
                        last = pe.transpose(ps[:, 4 + c, t * P:(t + 1) * P], src(c)[:, t * P:(t + 1) * P], ident[:])
                    last.then_inc(s("tok_turned"), 1)

            def block_out(name, c):
                n = OUT[name]
                pe.wait_ge(s("out_scaled"), NCH * n + c + 1)
                if c >= 2:
                    pe.wait_ge(s("x_upd"), NCH * n + c - 1)
                for t in range(TPC):
                    last = pe.transpose(ps[:, 2 + c % 2, t * P:(t + 1) * P],
                                        arr(11)[:, c * CH + t * P:c * CH + (t + 1) * P], ident[:])
                last.then_inc(s("out_turned"), 1)

            def outputs(name, products):
                for c in range(NCH):
                    if c >= 2:
                        pe.wait_ge(s("out_scaled"), NCH * OUT[name] + c - 1)
                    products(c, ps[:, c % 2, :]).then_inc(s("out_mm"), 1)
                    if c >= 1:
                        block_out(name, c - 1)
                block_out(name, NCH - 1)

            pe.wait_ge(s("ld_first"), 48)
            pe.wait_ge(s("start_made"), 1)
            for layer in range(4):
                for j in range(6):
                    at = (layer * 6 + j) * B
                    last = pe.matmul(ps[:, 7, at:at + B], wmod[:, layer, j * C:(j + 1) * C],
                                     silc[:, B * layer:B * layer + B], start=True, stop=True)
            last.then_inc(s("mod_mm"), 1)

            layernorm("a0")
            pe.wait_ge(s("abs_sum"), 2)
            pe.matmul(ps[:, 6, 0:2], ones[:], small[:, 0:2], start=True, stop=True).then_inc(s("abs_mm"), 1)
            pe.wait_ge(s("mixed"), 6)
            for c in range(NCH):
                pe.wait_ge(s("hT"), NCH * LN["a0"] + c + 1)
                for j, name in enumerate(("key", "value", "recept")):
                    n = 3 * c + j
                    pe.wait_ge(s("mod_ready"), 1)
                    pe.wait_ge(s("abs_read"), 1)
                    if n >= 4:
                        pe.wait_ge(s("kvr_read"), n - 3)
                    bank = ps[:, 4 + n % 4, :]
                    pe.matmul(bank, arr(0)[:, (2 * j) * C:(2 * j + 1) * C], h_chunk(c), start=True, stop=False)
                    pe.matmul(bank, arr(0)[:, (2 * j + 1) * C:(2 * j + 2) * C], h_chunk(c, 1), start=False,
                              stop=True).then_inc(s("kvr_mm"), 1)

            def out_a0(c, bank):
                pe.wait_ge(s("wkv"), c // CPB + 1)
                return pe.matmul(bank, w(0, "out"), arr(1)[:, tok(c)], start=True, stop=True)
            outputs("a0", out_a0)

            layernorm("b0")
            to_tokens(h_chunk, "in0", s("hT"), NCH * LN["b0"])
            layernorm("in0")
            pe.wait_ge(s("ternary"), 2)
            pe.wait_ge(s("hT"), NCH * (LN["in0"] + 1))
            for j in range(4):
                last = pe.matmul(ps[:, 3, 0:1], w(0, "w2")[:, j * C:(j + 1) * C], col("ln2_b", j),
                                 start=(j == 0), stop=(j == 3))
            last.then_inc(s("b2_mm"), 1)
            pe.wait_ge(s("w2_scaled"), 1)

            def hidden(c):
                for t in range(TPC):
                    n = TPC * c + t
                    if n >= 2:
                        pe.wait_ge(s("hid_read"), n - 1)
                    pe.matmul(ps[:, 4 + n % 2, :], hT[:, c // CPB, 1 + (c % CPB) * CH + t * P:1 + (c % CPB) * CH + (t + 1) * P],
                              w(0, "w1"), start=True, stop=True).then_inc(s("hid_mm"), 1)

            def out_b0(c, bank):
                hidden(c + 1) if c + 1 < NCH else None
                for t in range(TPC):
                    n = TPC * c + t
                    pe.wait_ge(s("hid_normed"), n + 1)
                    if n >= 2:
                        pe.wait_ge(s("hidT"), n - 1)
                    for j in range(4):
                        last = pe.transpose(ps[:, 6 + n % 2, j * P:(j + 1) * P], hid(n)[:, j * P:(j + 1) * P], ident[:])
                    last.then_inc(s("hid_turned"), 1)
                pe.wait_ge(s("hidT"), TPC * (c + 1))
                for j in range(4):
                    last = pe.matmul(bank, arr(0)[:, j * C:(j + 1) * C], hid_T(c)[:, j, :], start=(j == 0), stop=(j == 3))
                return last
            hidden(0)
            outputs("b0", out_b0)

            layernorm("a1")
            for c in range(NCH):
                pe.wait_ge(s("hT"), NCH * LN["a1"] + c + 1)
                if c == 0:
                    pe.wait_ge(s("ld_w13"), 48)
                for j, name in enumerate(("v", "q", "g")):
                    n = 3 * c + j
                    if n >= 4:
                        for which in range(3):
                            if (n - 4) % 3 == which:
                                pe.wait_ge(s(("l1_state", "l1_y", "l1_gate")[which]), (n - 4) // 3 + 1)
                    pe.matmul(ps[:, 4 + n % 4, :], w(1, name), hF[:, tok(c)], start=True, stop=True).then_inc(s("vqg_mm"), 1)
            pe.wait_ge(s("l1_gate"), NCH)
            pe.wait_ge(s("l1_y"), NCH)
            to_tokens(lambda c: arr(2)[:, tok(c)], "y1", s("l1_y"), 0)
            layernorm("y1")

            def out_a1(c, bank):
                pe.wait_ge(s("l1_gated"), c + 1)
                return pe.matmul(bank, w(1, "out"), arr(4)[:, tok(c)], start=True, stop=True)
            outputs("a1", out_a1)

            def router(layer, n):
                for t in range(NT):
                    pe.wait_ge(s("hT"), NCH * LN[f"b{layer}"] + t // TPC + 1)
                    last = pe.matmul(ps[:, 4, t * E:(t + 1) * E], hF[:, t * P:(t + 1) * P], w(layer, "router"),
                                     start=True, stop=True)
                last.then_inc(s("router_mm"), 1)
                pe.wait_ge(s("gates"), n + 1)
                pe.transpose(ps[:, 5, 0:P], route[:, 6, :], ident[:]).then_inc(s("gates_turned"), 1)

            layernorm("b1")
            router(1, 0)

            def out_b1(c, bank):
                for e in range(E):
                    n = E * c + e
                    pe.wait_ge(s("picked"), n + 1)
                    pe.matmul(bank, w(1, "expert")[:, e * C:(e + 1) * C], arr(8)[:, (n % 4) * CH:(n % 4 + 1) * CH],
                              start=(e == 0), stop=False).then_inc(s("expert_mm"), 1)
                if c == 0:
                    pe.wait_ge(s("ld_gater"), 16)
                return pe.matmul(bank, expertb[:], arr(9)[0:E, tok(c)], start=False, stop=True)
            outputs("b1", out_b1)

            layernorm("a2")
            pe.wait_ge(s("ld_w2"), 16)
            pe.wait_ge(s("hT"), NCH * (LN["a2"] + 1))
            for c in range(NCH):
                for j, name in enumerate(("q", "k")):
                    n = 2 * c + j
                    if n >= 2:
                        pe.wait_ge(s("a2_rest"), n - 1)
                    pe.matmul(ps[:, 4 + n % 2, :], w(2, name), hF[:, tok(c)], start=True, stop=True).then_inc(s("qk2_mm"), 1)
            value_products(pe, A2, w(2, "v"), C)
            pe.wait_ge(s("ident16"), 1)
            attention_products(pe, A2)
            attention_turns(pe, A2)

            def out_a2(c, bank):
                pe.wait_ge(s("a2_ctx"), c + 1)
                return pe.matmul(bank, w(2, "out"), arr(0)[:, tok(c)], start=True, stop=True)
            outputs("a2", out_a2)

            layernorm("b2")
            router(2, 1)
            pe.wait_ge(s("ld_w2"), 32)

            pe.wait_ge(s("gate_rows"), 2)

            def expert_hidden(cc, m):
                k = cc * 2 * E + m
                pe.wait_ge(s("silu2"), k + 1)
                pe.wait_ge(s("swiglu"), k + 1)
                rhs = hF[:, bass.ds(cc * CH, CH)]
                pe.matmul(ps[:, 4 + 2 * (m % 2), :], w(2, "w1")[:, m * P:(m + 1) * P], rhs, start=True,
                          stop=True).then_inc(s("h1_mm"), 1)
                pe.matmul(ps[:, 5 + 2 * (m % 2), :], w(2, "w2")[:, m * P:(m + 1) * P], rhs, start=True,
                          stop=True).then_inc(s("h2_mm"), 1)

            pe.sem_inc(s("g_used"), 2)
            with pe.Fori(0, NCH) as cc:
                pe.wait_ge(s("out_scaled"), NCH * OUT["b2"] + cc)
                for m in range(2 * E):
                    expert_hidden(cc, m)
                    if m >= 1:
                        pe.wait_ge(s("gated2"), cc * (2 * E) + m)
                        pe.matmul(ps[:, 0, :], w(2, "w3")[:, (m - 1) * C:m * C], arr(8)[:, ((m - 1) % 2) * CH:((m - 1) % 2 + 1) * CH],
                                  start=(m == 1), stop=False).then_inc(s("g_used"), 1)
                m = 2 * E
                pe.wait_ge(s("gated2"), cc * (2 * E) + m)
                pe.matmul(ps[:, 0, :], w(2, "w3")[:, (m - 1) * C:m * C], arr(8)[:, ((m - 1) % 2) * CH:((m - 1) % 2 + 1) * CH],
                          start=False, stop=True).then_inc(s("g_used"), 1)
            for c in range(NCH):
                block_out("b2", c)

            layernorm("a3")
            pe.wait_ge(s("hT"), NCH * (LN["a3"] + 1))
            for c in range(NCH):
                for j in range(2):
                    n = 2 * c + j
                    if n >= 2:
                        pe.wait_ge(s("rope_read"), n - 1)
                    for i in range(2):
                        pe.matmul(ps[:, 4 + 2 * (n % 2) + i, :], w(3, "qk"[j] + str(i)), hF[:, tok(c)], start=True,
                                  stop=True).then_inc(s("qk3_mm"), 1)
            value_products(pe, A3, w(3, "v"), 2 * C)
            attention_products(pe, A3)
            attention_turns(pe, A3)

            def out_a3(c, bank):
                pe.wait_ge(s("a3_ctx"), 2 * c + 2)
                pe.matmul(bank, w(3, "out")[:, 0:C], arr(0)[:, tok(c)], start=True, stop=False)
                return pe.matmul(bank, w(3, "out")[:, C:2 * C], arr(1)[:, tok(c)], start=False, stop=True)
            outputs("a3", out_a3)

            layernorm("b3")
            pe.wait_ge(s("mixed"), 10)
            for c in range(NCH):
                pe.wait_ge(s("hT"), NCH * LN["b3"] + c + 1)
                for j in range(2):
                    n = 2 * c + j
                    if n >= 4:
                        pe.wait_ge(s(("cm_k", "cm_r")[j]), c - 1)
                    pe.matmul(ps[:, 4 + n % 4, :], arr(4)[:, 2 * j * C:(2 * j + 1) * C], h_chunk(c), start=True, stop=False)
                    pe.matmul(ps[:, 4 + n % 4, :], arr(4)[:, (2 * j + 1) * C:(2 * j + 2) * C], h_chunk(c, 1), start=False,
                              stop=True).then_inc(s("cm_mm"), 1)

            def out_b3(c, bank):
                pe.wait_ge(s("cm_sq"), c + 1)
                return pe.matmul(bank, w(3, "wv"), arr(2)[:, tok(c)], start=True, stop=True)
            outputs("b3", out_b3)

        def first_part(act, a, unit, src, scale):
            n = a.name
            if unit >= 4:
                act.wait_ge(s(f"{n}_st{unit % 4}"), 16 * (a.groups // B) * (unit // 4))
            act.activation(parts_ring(unit % 4)[:, 0, :], src, ACT.Copy, scale=scale).then_inc(s(n + "_p1"), 1)

        def values(act, a):
            n = a.name
            act.wait_ge(s(n + "_vzero"), 2)
            for t in range(NT):
                act.wait_ge(s(n + "_vmm"), t + 1)
                for h in v_pieces(a):
                    act.activation(v_whole(a, t, h), v_made(a, t, h, False), ACT.Copy)
                    last = act.activation(v_part(a, t, 0, h), v_made(a, t, h, True), ACT.Copy)
                last.then_inc(s(n + "_v1"), 1)


        def exponentials(act, a):
            n = a.name
            nb, ns = a.nbatch, a.nsteps

            def copy_out(g, j):
                act.wait_ge(s(n + "_pv"), g * nb + a.ends[j] + 3)
                act.wait_ge(s(n + "_oturn"), g * 4 + j + 1)
                for b2 in range(a.obanks):
                    act.activation(side(j % 2)[:, b2 * CH:(b2 + 1) * CH], ps[:, 6 + b2, :], ACT.Copy).then_inc(s(n + "_ocopy"), 1)

            def batch(g, beta):
                f = a.batches[beta][3]
                for sl in range(SLOTS):
                    k = SLOTS * beta + sl
                    act.wait_ge(s(n + "_sc"), g * ns + k + 1)
                    act.wait_ge(s(n + "_pv"), g * nb + beta + 1)
                    bank = 2 * a.pair["step", k]
                    act.activation(pslots[:, k % 8, :, f:CH], ps[:, bank:bank + 2, f:CH], ACT.Exp, bias=lift[:]
                                   ).then_inc(s(n + "_exp"), 1)

            def main(g, following):
                for beta in range(2, nb + 2):
                    if beta < nb:
                        batch(g, beta)
                    elif following:
                        batch(g + 1, beta - nb)
                    if beta - 1 in a.ends:
                        copy_out(g, a.ends.index(beta - 1))

            act.sem_inc(s(n + "_exp"), 2)
            act.sem_inc(s(n + "_ocopy"), a.obanks)
            for slot in range(4):
                act.wait_ge(s(f"{n}_st{slot}"), 16 * (a.groups // B) * halves_of(a) * 2)
            batch(0, 0)
            batch(0, 1)
            if a.groups > 4:
                with act.Fori(0, a.groups // 2 - 1) as it:
                    main(it * 2, True)
                    main(it * 2 + 1, True)
            else:
                main(0, True)
                main(1, True)
            main(a.groups - 2, True)
            main(a.groups - 1, False)

        def contexts(act, a):
            n = a.name
            for k in range(halves_of(a) * NCH):
                c, hf = k // halves_of(a), k % halves_of(a)
                act.wait_ge(s(n + "_cturn"), k + 1)
                act.activation(arr(hf)[:, tok(c)], ps[:, 4 + k % 2, :], ACT.Copy).then_inc(s(n + "_ctx"), 1)

        @block.scalar
        def _(act):
            def features(name, scale, bias, dst):
                n = LN[name]
                for c in range(NCH):
                    act.wait_ge(s("ln_turned"), NCH * n + c + 1)
                    act.activation(dst(c), ps[:, c, :], ACT.Identity, bias=bias(c // CPB), scale=scale(c // CPB)
                                   ).then_inc(s("hT"), 1)

            def modulated(layer, which, dst):
                j = 0 if which == "a" else 3
                features(f"{which}{layer}", lambda b: mod[:, layer, j + 1, b:b + 1], lambda b: mod[:, layer, j, b:b + 1], dst)

            def flat(c):
                return hF[:, tok(c)]

            def scaled(name, c, bias=0.0):
                layer, j = int(name[1]), 2 if name[0] == "a" else 5
                act.wait_ge(s("out_mm"), NCH * OUT_MM[name] + c + 1)
                b = c // CPB
                act.activation(arr(11)[:, tok(c)], ps[:, c % 2, :], ACT.Identity, bias=bias,
                               scale=mod[:, layer, j, b:b + 1]).then_inc(s("out_scaled"), 1)

            act.wait_ge(s("ld_first"), 48)
            act.activation(silc[:], cols[:, 0:8], ACT.Silu).then_inc(s("start_made"), 1)
            act.activation(small[:, 18:19], col("beta"), ACT.Sigmoid).then_inc(s("start_made"), 1)
            act.activation(small[:, 16:17], col("decay"), ACT.Exp).then_inc(s("start_made"), 1)

            act.wait_ge(s("mod_ready"), 1)
            modulated(0, "a", h_chunk)
            for n in range(3 * NCH):
                c, j = n // 3, n % 3
                act.wait_ge(s("kvr_mm"), n + 1)
                act.activation(arr(2 + j)[:, tok(c)], ps[:, 4 + n % 4, :], (ACT.Copy, ACT.Copy, ACT.Sigmoid)[j]
                               ).then_inc(s("kvr_read"), 1)
            for b in range(B):
                for k in range(4):
                    act.wait_ge(s("wkv_in"), 4 * b + k + 1)
                    x = wkv_temp(b, (0, 1, 3, 2)[k])
                    act.activation(x, x, ACT.Exp).then_inc(s("wkv_exp"), 1)
            for c in range(NCH):
                scaled("a0", c)

            modulated(0, "b", h_chunk)
            features("in0", lambda b: col("ln1_g"), lambda b: col("ln1_b"), h_chunk)

            def gelus(c):
                for n in range(TPC * c, TPC * c + TPC):
                    act.wait_ge(s("hid_read"), n + 1)
                    act.activation(hid(n), hid(n), ACT.Gelu).then_inc(s("gelu"), 1)
            gelus(0)
            for c in range(NCH):
                if c + 1 < NCH:
                    gelus(c + 1)
                for t in range(TPC):
                    n = TPC * c + t
                    act.wait_ge(s("hid_turned"), n + 1)
                    if c >= 2 and t == 0:
                        act.wait_ge(s("out_mm"), NCH * OUT_MM["b0"] + c - 1)
                    act.activation(hid_T(c)[:, :, t * P:(t + 1) * P],
                                   ps[:, 6 + n % 2, :].rearrange("p (j t) -> p j t", j=4), ACT.Copy
                                   ).then_inc(s("hidT"), 1)
                if c == 0:
                    act.wait_ge(s("b2_ready"), 1)
                scaled("b0", c, bias=small[:, 9 + c // CPB:10 + c // CPB])

            modulated(1, "a", flat)
            for c in range(NCH):
                act.wait_ge(s("vqg_mm"), 3 * c + 3)
                act.activation(arr(3)[:, tok(c)], ps[:, 4 + (3 * c + 2) % 4, :], ACT.Silu).then_inc(s("l1_gate"), 1)
            features("y1", lambda b: col("gamma"), lambda b: col("lnb"), flat)
            for c in range(NCH):
                scaled("a1", c)

            modulated(1, "b", flat)
            act.wait_ge(s("route_in"), 1)
            act.activation(route[:, 3, :], route[:, 3, :], ACT.Exp).then_inc(s("route_exp"), 1)
            for c in range(NCH):
                scaled("b1", c)

            modulated(2, "a", flat)
            for n in range(2 * NCH):
                act.wait_ge(s("qk2_mm"), n + 1)
                first_part(act, A2, n, ps[:, 4 + n % 2, :], HD ** -0.5 if n % 2 == 0 else 1.0)
            values(act, A2)
            exponentials(act, A2)
            contexts(act, A2)
            for c in range(NCH):
                scaled("a2", c)

            modulated(2, "b", flat)
            act.wait_ge(s("route_in"), 2)
            act.activation(rone[:, 3, :], rone[:, 3, :], ACT.Exp).then_inc(s("route_exp"), 1)
            act.sem_inc(s("silu2"), 2)
            with act.Fori(0, NCH) as cc:
                for m in range(2 * E):
                    k = cc * (2 * E) + m
                    act.wait_ge(s("h1_mm"), k + 1)
                    act.wait_ge(s("swiglu"), k + 1)
                    act.activation(arr(9)[:, (m % 2) * CH:(m % 2 + 1) * CH], ps[:, 4 + 2 * (m % 2), :], ACT.Silu
                                   ).then_inc(s("silu2"), 1)
                act.wait_ge(s("g_used"), (cc + 1) * (2 * E) + 2)
                act.activation(arr(11)[:, bass.ds(cc * CH, CH)], ps[:, 0, :], ACT.Copy, scale=small[:, bass.ds(cc + 28, 1)]
                               ).then_inc(s("out_scaled"), 1)

            modulated(3, "a", flat)
            act.wait_ge(s("lam_sum"), 1)
            act.activation(small[:, 22:24], small[:, 20:22], ACT.Exp).then_inc(s("lam_exp"), 1)
            for n in range(2 * NCH):
                for i in range(2):
                    act.wait_ge(s("roped"), 2 * n + i + 1)
                    first_part(act, A3, 2 * n + i, roped(2 * n + i), HD ** -0.5 if n % 2 == 0 else 1.0)
            values(act, A3)
            exponentials(act, A3)
            contexts(act, A3)
            for c in range(NCH):
                scaled("a3", c)

            modulated(3, "b", h_chunk)
            for c in range(NCH):
                act.wait_ge(s("cm_mm"), 2 * c + 1)
                act.activation(arr(1)[:, tok(c)], ps[:, 4 + (2 * c) % 4, :], ACT.Relu).then_inc(s("cm_k"), 1)
                act.wait_ge(s("cm_mm"), 2 * c + 2)
                act.activation(arr(0)[:, tok(c)], ps[:, 4 + (2 * c + 1) % 4, :], ACT.Sigmoid).then_inc(s("cm_r"), 1)

        def gate_out(dve, c):
            dve.wait_ge(s("out_mm"), NCH * OUT_MM["b3"] + c + 1)
            dve.wait_ge(s("cm_r"), c + 1)
            dve.scalar_tensor_tensor(out=arr(11)[:, tok(c)], in0=ps[:, c % 2, :], scalar=mod[:, 3, 5, c // CPB:c // CPB + 1],
                                     in1=arr(0)[:, tok(c)], op0=ALU.mult, op1=ALU.mult).then_inc(s("out_scaled"), 1)

        def other_parts(dve, a, unit, src, scale):
            n = a.name
            ring = parts_ring(unit % 4)
            dve.wait_ge(s(n + "_p1"), unit + 1)
            dve.scalar_tensor_tensor(out=rest(unit), in0=src, scalar=scale, in1=ring[:, 0, :], op0=ALU.mult, op1=ALU.subtract
                                     ).then_inc(s(n + "_rest"), 1)
            dve.wait_ge(s(n + "_rest"), unit + 1)
            dve.tensor_copy(ring[:, 1, :], rest(unit)).then_inc(s(n + "_p2"), 1)
            dve.wait_ge(s(n + "_p2"), unit + 1)
            dve.tensor_tensor(ring[:, 2, :], rest(unit), ring[:, 1, :], ALU.subtract).then_inc(s(n + "_parts"), 1)

        def maxima(dve, a):
            n = a.name
            nb, ns, np_ = a.nbatch, a.nsteps, a.npieces
            for t in range(NT):
                dve.wait_ge(s(n + "_v1"), t + 1)
                if t >= 2:
                    dve.wait_ge(s(n + "_v"), t - 1)
                for i in v_pieces(a):
                    last = dve.tensor_tensor(v_rest(a, t, i), v_made(a, t, i, True), v_part(a, t, 0, i), ALU.subtract)
                last.then_inc(s(n + "_vrest"), 1)
                dve.wait_ge(s(n + "_vrest"), t + 1)
                for i in v_pieces(a):
                    last = dve.tensor_copy(v_part(a, t, 1, i), v_rest(a, t, i))
                last.then_inc(s(n + "_v2"), 1)

            def piece(g, u, m):
                pos, sl, qt, pc, keys = a.pieces[m]
                dve.wait_ge(s(n + "_mxmm"), g * np_ + m + 1)
                row = (half_of(u, pos) * SLOTS + sl) * QT + qt
                dve.tensor_reduce(mcol[:, row, pc:pc + 1], ps[:, 4 + m % 2, 0:keys], AX.X, ALU.max).then_inc(s(n + "_mx"), 1)
                if m == np_ - 1:
                    dve.wait_ge(s(n + "_mx"), (g + 1) * np_ + 2)
                    dve.tensor_reduce(negm[:, 0:SETS * QT], mcol[:], AX.X, ALU.max, negate=True).then_inc(s(n + "_neg"), 1)

            def split_max(g):
                dve.wait_ge(s(n + "_mturn"), g + 1)
                if not (isinstance(g, int) and g == 0):
                    dve.wait_ge(s(n + "_mld"), g * 96)
                src = ps[0:SETS * QT, 4, 0:P]
                dve.tensor_copy(mpart[:, 0, :], src).then_inc(s(n + "_mstep"), 1)
                dve.wait_ge(s(n + "_mstep"), g * 3 + 1)
                dve.tensor_tensor(mrest[:], src, mpart[:, 0, :], ALU.subtract).then_inc(s(n + "_mstep"), 1)
                dve.wait_ge(s(n + "_mstep"), g * 3 + 2)
                dve.tensor_copy(mpart[:, 1, :], mrest[:]).then_inc(s(n + "_mstep"), 1)
                dve.wait_ge(s(n + "_mstep"), g * 3 + 3)
                dve.tensor_tensor(mpart[:, 2, :], mrest[:], mpart[:, 1, :], ALU.subtract).then_inc(s(n + "_msplit"), 1)

            placed = otok[:, 0:a.groups // 2 * QT * P].rearrange("p (g q u f) -> p g q u f", q=QT, u=2, f=P // 2)

            def output(pair, u, j):
                g, (pos, qc), w_ = pair * 2 + u, divmod(j, 2), a.width
                i = half_of(u, pos)
                src = ps[:, 2 * a.pair["turn", j], 0:TPC * a.out_cols].rearrange("p (t n d) -> p t n d", t=TPC, n=SLOTS)
                dve.wait_ge(s(n + "_oturn"), g * 4 + j + 3)
                dve.wait_ge(s(n + "_oread"), g * 4 + j + 1)
                dve.reciprocal(rz[:], src[:, :, :, w_:w_ + 1]).then_inc(s(n + "_ostep"), 1)
                dve.wait_ge(s(n + "_ostep"), g * 4 + j + 1)
                if a.causal:
                    dst = placed[:, bass.ds(pair, 1), TPC * qc:TPC * (qc + 1), u, 32 * i:32 * i + 32].rearrange(
                        "p g q (n d) -> p (g q) n d", d=w_)
                else:
                    dst = ohalf[:, qc if pos == 0 else 2, :].rearrange("p (t n d) -> p t n d", t=TPC, d=w_)
                dve.tensor_tensor(dst, src[:, :, :, 0:w_], rz[:].to_broadcast([P, TPC, SLOTS, w_]), ALU.mult
                                  ).then_inc(s(n + "_oread"), 1)
                if a.causal:
                    return
                half = ohalf[:, qc if pos == 0 else 2, :]
                if pos == 1:
                    dst = placed[:, bass.ds(pair, 1), TPC * qc:TPC * (qc + 1), u, :].rearrange("p g q f -> p (g q) f")
                    first, second = (ohalf[:, qc, :], half) if u == 0 else (half, ohalf[:, qc, :])
                    dve.wait_ge(s(n + "_oread"), g * 4 + j + 2)
                    dve.scalar_tensor_tensor(out=dst, in0=second.rearrange("p (q f) -> p q f", q=TPC), scalar=small[:, 25:26],
                                             in1=first.rearrange("p (q f) -> p q f", q=TPC), op0=ALU.mult, op1=ALU.add
                                             ).then_inc(s(n + "_odone"), 1)

            def batch(g, u, beta, following):
                for k in range(SLOTS * beta, SLOTS * (beta + 1)):
                    if following:
                        for m in range(a.at[4 * k], a.at[4 * k + 4]):
                            piece(g + 1, 1 - u, m)
                        if k == a.turn_at:
                            split_max(g + 1)

            def main(pair, u, following, after):
                g = pair * 2 + u
                for beta in range(2, nb + 2):
                    if beta < nb:
                        batch(g, u, beta, following)
                    elif following:
                        batch(g + 1, 1 - u, beta - nb, after)
                    for j, e in enumerate(a.ends):
                        if beta == e + 2:
                            output(pair, u, j)

            dve.sem_inc(s(n + "_mx"), 2)
            dve.sem_inc(s(n + "_oread"), 1)
            for m in range(np_):
                piece(0, 0, m)
            split_max(0)
            batch(0, 0, 0, True)
            batch(0, 0, 1, True)
            if a.groups > 4:
                with dve.Fori(0, a.groups // 2 - 1) as it:
                    main(it, 0, True, True)
                    main(it, 1, True, True)
            else:
                main(0, 0, True, True)
                main(0, 1, True, True)
            main(a.groups // 2 - 1, 0, True, False)
            main(a.groups // 2 - 1, 1, False, False)


        def third_parts(pool, a):
            n = a.name
            for t in range(NT):
                pool.wait_ge(s(n + "_v2"), t + 1)
                for i in v_pieces(a):
                    last = pool.tensor_tensor(v_part(a, t, 2, i), v_rest(a, t, i), v_part(a, t, 1, i), ALU.subtract)
                last.then_inc(s(n + "_v"), 1)

        def lows(pool, a):
            def main(g):
                for beta, (_, _, _, f) in enumerate(a.batches):
                    for sl in range(SPLIT):
                        k = SLOTS * beta + sl
                        pool.wait_ge(s(a.name + "_exp"), g * a.nsteps + k + 3)
                        pool.tensor_tensor(plow[:, low_slot(k), :, f:CH], pslots[:, k % 8, :, f:CH], phigh[:, k % 8, :, f:CH],
                                           ALU.subtract).then_inc(s(a.name + "_low"), 1)
            if a.groups > 4:
                with pool.Fori(0, a.groups // 2) as it:
                    main(it * 2)
                    main(it * 2 + 1)
            else:
                for g in range(a.groups):
                    main(g)

        @block.vector
        def _(dve):
            chain = [0]

            def link(ins):
                chain[0] += 1
                ins.then_inc(s("dve_chain"), 1)
                dve.wait_ge(s("dve_chain"), chain[0])

            def bc(ap, n):
                return ap.unsqueeze(2).to_broadcast([P, NT, n])

            def layernorm(name, feature_major=False):
                n = LN[name]
                if name != "a0" and not feature_major:
                    dve.wait_ge(s("x_upd"), NCH * (n - {"b0": 0, "a1": 1, "b1": 2, "a2": 2, "b2": 2, "a3": 2, "b3": 2}[name]))

                def src(t):
                    if feature_major:
                        return ps[:, 4 + t // TPC, (t % TPC) * P:(t % TPC + 1) * P]
                    return x_tok[:, t, :]
                for t in range(NT):
                    if t % TPC == 0:
                        if feature_major:
                            dve.wait_ge(s("tok_turned"), NCH * (0 if name == "in0" else 1) + t // TPC + 1)
                        elif name == "a0":
                            if t == 0:
                                dve.wait_ge(s("ld_x"), 16 * NCH)
                    dve.bn_stats(stats[:, t, :], src(t)).then_inc(s("ln_step"), 1)
                for t in range(NT):
                    dve.wait_ge(s("ln_step"), 2 * NT * n + t + 1)
                    dve.bn_aggr(mv[:, t, :], stats[:, t, :]).then_inc(s("ln_step"), 1)
                dve.wait_ge(s("ln_step"), 2 * NT * (n + 1))
                dve.tensor_scalar(var[:], mv[:, :, 1], EPS, None, ALU.add).then_inc(s("var"), 1)
                dve.wait_ge(s("rstd"), VAR[n])
                for t in range(NT):
                    last = dve.tensor_scalar(xn[:, t, :], src(t), mv[:, t, 0:1], rstd[:, t:t + 1], ALU.subtract, ALU.mult)
                    if t % TPC == TPC - 1:
                        last.then_inc(s("ln_normed"), 1)

            def add_to_x(name, c):
                dve.wait_ge(s("out_turned"), NCH * OUT[name] + c + 1)
                xs = x_tok[:, TPC * c:TPC * (c + 1), :].rearrange("p t c -> p (t c)")
                dve.tensor_tensor(xs, xs, ps[:, 2 + c % 2, :], ALU.add).then_inc(s("x_upd"), 1)

            dve.memset(hT[:, :, 0:1], 0.0)
            dve.memset(lift[:], LIFT)
            dve.memset(mhalf[:], -0.5)
            dve.memset(mcol[:], LOWEST)
            dve.memset(negm[:], 0.0)
            link(dve.memset(ones[:], 1.0))
            dve.wait_ge(s("mod_mm"), 1)
            link(dve.tensor_copy(mod[:].rearrange("p l j b -> p (l j b)"), ps[:, 7, 0:8 * 6]))
            for k, j in enumerate((2, 5)):
                dve.tensor_scalar(modx[:, :, k, :], mod[:, :, j, :], 0.0, 2.0, ALU.is_ge, ALU.mult)
            for j in (1, 4):
                dve.tensor_scalar(mod[:, :, j, :], mod[:, :, j, :], 1.0, None, ALU.add)
            for j in (2, 5):
                last = dve.scalar_tensor_tensor(out=mod[:, :, j, :], in0=mod[:, :, j, :], scalar=-1.0, in1=mod[:, :, j, :],
                                                op0=ALU.mult, op1=ALU.max)
            link(last)
            for j in (2, 5):
                last = dve.tensor_scalar(mod[:, :, j, :], mod[:, :, j, :], 0.25, None, ALU.max)
            link(last)
            for k, j in enumerate((2, 5)):
                last = dve.scalar_tensor_tensor(out=mod[:, :, j, :], in0=modx[:, :, k, :], scalar=-1.0, in1=mod[:, :, j, :],
                                                op0=ALU.add, op1=ALU.mult)
            last.then_inc(s("mod_ready"), 1)
            layernorm("a0")

            dve.wait_ge(s("ld_w0"), 32)
            for j, name in enumerate(("mix_k", "mix_v", "mix_r")):
                last = dve.tensor_scalar(small[:, 12 + j:13 + j], col(name), -1.0, 1.0, ALU.mult, ALU.add)
            link(last)
            for j, (name, mix) in enumerate((("key", "mix_k"), ("value", "mix_v"), ("recept", "mix_r"))):
                dve.tensor_scalar(arr(0)[:, 2 * j * C:(2 * j + 1) * C], w(0, name), col(mix), None, ALU.mult).then_inc(s("mixed"), 1)
                dve.tensor_scalar(arr(0)[:, (2 * j + 1) * C:(2 * j + 2) * C], w(0, name), small[:, 12 + j:13 + j], None,
                                  ALU.mult).then_inc(s("mixed"), 1)
            for k, name in enumerate(("w1", "w2")):
                dve.tensor_reduce(small[:, k:k + 1], w(0, name), AX.X, ALU.add, apply_absolute_value=True).then_inc(s("abs_sum"), 1)
            dve.wait_ge(s("start_made"), 3)
            dve.tensor_scalar(small[:, 17:18], small[:, 16:17], -1.0, None, ALU.mult)
            dve.wait_ge(s("abs_mm"), 1)
            dve.tensor_scalar(small[:, 2:4], ps[:, 6, 0:2], 1.0 / (H1 * C), 1e-5, ALU.mult, ALU.max).then_inc(s("abs_read"), 1)

            o_, p_, q_ = wkv_state(0), wkv_state(1), wkv_state(2)
            dve.memset(o_[:, :, 0:1], LOWEST)
            dve.memset(p_[:, :, 0:1], 0.0)
            link(dve.memset(q_[:, :, 0:1], 0.0))
            wdecay, u = small[:, 17:18], col("first")
            for b in range(B):
                bt = slice(b * SEQ, (b + 1) * SEQ)
                k, v = arr(2)[:, bt], arr(3)[:, bt]
                dve.wait_ge(s("kvr_read"), 6 * b + 6)
                link(dve.tensor_tensor_scan(o_[:, b, 1:], wdecay.to_broadcast([P, SEQ]), k, LOWEST, ALU.add, ALU.max))
                before = o_[:, b, 0:SEQ]
                dve.scalar_tensor_tensor(out=wkv_temp(b, 0), in0=before, scalar=wdecay, in1=o_[:, b, 1:], op0=ALU.add,
                                         op1=ALU.subtract).then_inc(s("wkv_in"), 1)
                dve.tensor_tensor(wkv_temp(b, 1), k, o_[:, b, 1:], ALU.subtract).then_inc(s("wkv_in"), 1)
                link(dve.scalar_tensor_tensor(out=wkv_temp(b, 2), in0=k, scalar=u, in1=before, op0=ALU.add, op1=ALU.max))
                link(dve.scalar_tensor_tensor(out=wkv_temp(b, 3), in0=k, scalar=u, in1=wkv_temp(b, 2), op0=ALU.add,
                                              op1=ALU.subtract))
                dve.nop().then_inc(s("wkv_in"), 1)
                dve.tensor_tensor(wkv_temp(b, 2), before, wkv_temp(b, 2), ALU.subtract).then_inc(s("wkv_in"), 1)
            for b in range(B):
                bt = slice(b * SEQ, (b + 1) * SEQ)
                v, y = arr(3)[:, bt], arr(1)[:, bt]
                t0, t1, t2, t3 = (wkv_temp(b, k) for k in range(4))
                dve.wait_ge(s("wkv_exp"), 4 * b + 4)
                link(dve.tensor_tensor(y, t1, v, ALU.mult))
                dve.tensor_tensor_scan(p_[:, b, 1:], t0, y, 0.0, ALU.mult, ALU.add)
                link(dve.tensor_tensor_scan(q_[:, b, 1:], t0, t1, 0.0, ALU.mult, ALU.add))
                dve.tensor_tensor(t0, t2, p_[:, b, 0:SEQ], ALU.mult)
                dve.tensor_tensor(t1, t3, v, ALU.mult)
                link(dve.tensor_tensor(t2, t2, q_[:, b, 0:SEQ], ALU.mult))
                dve.tensor_tensor(t0, t0, t1, ALU.add)
                link(dve.tensor_tensor(t2, t2, t3, ALU.add))
                link(dve.reciprocal(t1, t2))
                link(dve.tensor_tensor(t0, t0, t1, ALU.mult))
                dve.tensor_tensor(y, t0, arr(4)[:, bt], ALU.mult).then_inc(s("wkv"), 1)

            dve.wait_ge(s("abs_read"), 1)
            link(dve.reciprocal(small[:, 4:6], small[:, 2:4]))
            link(dve.reciprocal(small[:, 6:8], small[:, 4:6]))
            for k, name in enumerate(("w1", "w2")):
                x = w(0, name)
                link(dve.tensor_scalar(x, x, small[:, 4 + k:5 + k], ROUND, ALU.mult, ALU.add))
                link(dve.tensor_scalar(x, x, -ROUND, 1.0, ALU.add, ALU.min))
                dve.tensor_scalar(x, x, -1.0, small[:, 6 + k:7 + k], ALU.max, ALU.mult).then_inc(s("ternary"), 1)
            for c in range(NCH):
                add_to_x("a0", c)

            dve.wait_ge(s("ternary"), 2)
            for j in range(4):
                last = dve.tensor_scalar(arr(0)[:, j * C:(j + 1) * C], w(0, "w2")[:, j * C:(j + 1) * C], col("ln2_g", j), None, ALU.mult)
            last.then_inc(s("w2_scaled"), 1)
            layernorm("b0")
            layernorm("in0", True)
            dve.wait_ge(s("b2_mm"), 1)
            link(dve.tensor_scalar(small[:, 8:9], ps[:, 3, 0:1], col("b2"), None, ALU.add))
            for b in range(B):
                last = dve.tensor_scalar(small[:, 9 + b:10 + b], small[:, 8:9], mod[:, 0, 5, b:b + 1], None, ALU.mult)
            last.then_inc(s("b2_ready"), 1)

            def hidden(c):
                for t in range(TPC):
                    n = TPC * c + t
                    dve.wait_ge(s("hid_mm"), n + 1)
                    if c >= 2 and t == 0:
                        dve.wait_ge(s("hid_turned"), TPC * (c - 1))
                    dve.tensor_tensor(hid(n), ps[:, 4 + n % 2, :], b1_row, ALU.add).then_inc(s("hid_read"), 1)
                for t in range(TPC):
                    dve.wait_ge(s("gelu"), TPC * c + t + 1)
                    last = dve.bn_stats(stats[:, t, :], hid(TPC * c + t))
                link(last)
                for t in range(TPC):
                    last = dve.bn_aggr(mv[:, t, :], stats[:, t, :])
                link(last)
                dve.tensor_scalar(var[:, 0:TPC], mv[:, 0:TPC, 1], EPS, None, ALU.add).then_inc(s("var"), 1)
                dve.wait_ge(s("rstd"), VAR[2] + c + 1)
                for t in range(TPC):
                    x = hid(TPC * c + t)
                    dve.tensor_scalar(x, x, mv[:, t, 0:1], rstd[:, t:t + 1], ALU.subtract, ALU.mult).then_inc(s("hid_normed"), 1)
            hidden(0)
            for c in range(NCH):
                if c + 1 < NCH:
                    hidden(c + 1)
                if c >= 1:
                    add_to_x("b0", c - 1)
            add_to_x("b0", NCH - 1)

            layernorm("a1")
            dve.wait_ge(s("start_made"), 2)
            lam = small[:, 18:19].to_broadcast([P, CH])
            for c in range(NCH):
                dve.wait_ge(s("vqg_mm"), 3 * c + 1)
                x = arr(1)[:, tok(c)]
                if c % CPB:
                    dve.wait_ge(s("l1_state"), c)
                dve.tensor_tensor_scan(x, lam, ps[:, 4 + (3 * c) % 4, :], arr(1)[:, c * CH - 1:c * CH] if c % CPB else 0.0,
                                       ALU.mult, ALU.add).then_inc(s("l1_state"), 1)
                dve.wait_ge(s("vqg_mm"), 3 * c + 2)
                dve.wait_ge(s("l1_state"), c + 1)
                dve.tensor_tensor(arr(2)[:, tok(c)], x, ps[:, 4 + (3 * c + 1) % 4, :], ALU.mult).then_inc(s("l1_y"), 1)
            layernorm("y1", True)
            dve.wait_ge(s("l1_gate"), NCH)
            for c in range(NCH):
                dve.wait_ge(s("hT"), NCH * LN["y1"] + c + 1)
                dve.tensor_tensor(arr(4)[:, tok(c)], hF[:, tok(c)], arr(3)[:, tok(c)], ALU.mult).then_inc(s("l1_gated"), 1)
            for c in range(NCH):
                add_to_x("a1", c)

            def r3(k):
                return route[:, k, :].rearrange("p (t e) -> p t e", e=E)

            def rf(k):
                return rone[:, k, :]
            ties = tie_row.unsqueeze(1).to_broadcast([P, NT, E])

            def first_max(logits, biggest, pick, tmp):
                link(dve.tensor_reduce(biggest, logits, AX.X, ALU.max))
                link(dve.tensor_tensor(tmp, logits, bc(biggest, E), ALU.is_equal))
                link(dve.tensor_tensor(tmp, tmp, ties, ALU.mult))
                link(dve.tensor_reduce(rf(5), tmp, AX.X, ALU.max))
                link(dve.tensor_tensor(pick, tmp, bc(rf(5), E), ALU.is_equal))

            def rows_of_gates(n):
                dve.wait_ge(s("gates_turned"), n + 1)
                dve.tensor_copy(route[:, 7, :], ps[:, 5, 0:P]).then_inc(s("gate_rows"), 1)

            layernorm("b1")
            dve.wait_ge(s("router_mm"), 1)
            link(dve.tensor_tensor(r3(0), ps[:, 4, 0:P].rearrange("p (t e) -> p t e", e=E),
                                   routerb_row.unsqueeze(1).to_broadcast([P, NT, E]), ALU.add))
            first_max(r3(0), rf(0), r3(2), r3(1))
            dve.tensor_tensor(r3(3), r3(0), bc(rf(0), E), ALU.subtract).then_inc(s("route_in"), 1)
            dve.wait_ge(s("route_exp"), 1)
            link(dve.tensor_reduce(rf(1), r3(3), AX.X, ALU.add))
            link(dve.reciprocal(rf(2), rf(1)))
            dve.tensor_tensor(r3(6), r3(2), bc(rf(2), E), ALU.mult).then_inc(s("gates"), 1)
            rows_of_gates(0)
            for c in range(NCH):
                for e in range(E):
                    n = E * c + e
                    if n == 0:
                        dve.wait_ge(s("ld_gates"), 16 * E)
                    if n >= 4:
                        dve.wait_ge(s("expert_mm"), n - 3)
                    dve.tensor_tensor(arr(8)[:, (n % 4) * CH:(n % 4 + 1) * CH], hF[:, tok(c)], arr(e)[:, tok(c)],
                                      ALU.mult).then_inc(s("picked"), 1)
                if c >= 1:
                    add_to_x("b1", c - 1)
            add_to_x("b1", NCH - 1)

            layernorm("a2")
            dve.wait_ge(s("ld_const"), 32)
            dve.wait_ge(s("ld_first"), 48)
            dve.tensor_copy(ident16[:], ident[:]).then_inc(s("ident16"), 1)
            for n in range(2 * NCH):
                other_parts(dve, A2, n, ps[:, 4 + n % 2, :], HD ** -0.5 if n % 2 == 0 else 1.0)
            maxima(dve, A2)
            for c in range(NCH):
                add_to_x("a2", c)

            for c in range(NCH):
                dve.tensor_copy(small[:, 28 + c:29 + c], mod[:, 2, 5, c // CPB:c // CPB + 1])
            layernorm("b2")
            dve.wait_ge(s("router_mm"), 2)
            link(dve.tensor_copy(r3(0), ps[:, 4, 0:P].rearrange("p (t e) -> p t e", e=E)))
            first_max(r3(0), rf(0), r3(2), r3(1))
            link(dve.scalar_tensor_tensor(out=route[:, 3, :], in0=route[:, 2, :], scalar=MASKED, in1=route[:, 0, :],
                                          op0=ALU.mult, op1=ALU.add))
            first_max(r3(3), rf(1), r3(4), r3(1))
            dve.tensor_tensor(rf(3), rf(1), rf(0), ALU.subtract).then_inc(s("route_in"), 1)
            dve.wait_ge(s("route_exp"), 2)
            link(dve.tensor_scalar(rf(2), rf(3), 1.0, None, ALU.add))
            link(dve.reciprocal(rf(4), rf(2)))
            link(dve.tensor_tensor(rf(3), rf(3), rf(4), ALU.mult))
            dve.tensor_tensor(r3(5), r3(2), bc(rf(4), E), ALU.mult)
            link(dve.tensor_tensor(r3(1), r3(4), bc(rf(3), E), ALU.mult))
            dve.tensor_tensor(r3(6), r3(5), r3(1), ALU.add).then_inc(s("gates"), 1)
            rows_of_gates(1)
            dve.sem_inc(s("swiglu"), 2)
            dve.wait_ge(s("ld_gates"), 32 * E)
            with dve.Fori(0, NCH) as cc:
                for m in range(2 * E):
                    k = cc * (2 * E) + m
                    dve.wait_ge(s("h2_mm"), k + 1)
                    dve.wait_ge(s("silu2"), k + 3)
                    dve.tensor_tensor(arr(9)[:, (2 + m % 2) * CH:(3 + m % 2) * CH], arr(9)[:, (m % 2) * CH:(m % 2 + 1) * CH],
                                      ps[:, 5 + 2 * (m % 2), :], ALU.mult).then_inc(s("swiglu"), 1)
                    dve.wait_ge(s("g_used"), k + 1)
                    dve.wait_ge(s("swiglu"), k + 3)
                    dve.tensor_tensor(arr(8)[:, (m % 2) * CH:(m % 2 + 1) * CH], arr(9)[:, (2 + m % 2) * CH:(3 + m % 2) * CH],
                                      arr(m // 2)[:, bass.ds(cc * CH, CH)], ALU.mult).then_inc(s("gated2"), 1)
            for c in range(NCH):
                add_to_x("b2", c)

            link(dve.tensor_tensor(small[:, 32:48], lam_rows[:, 0:16], lam_rows[:, 16:32], ALU.mult))
            dve.tensor_reduce(small[:, 20:22], small[:, 32:48].rearrange("p (a d) -> p a d", a=2), AX.X, ALU.add
                              ).then_inc(s("lam_sum"), 1)
            layernorm("a3")
            dve.wait_ge(s("ld_rope"), 16)
            for n in range(2 * NCH + 1):
                if n < 2 * NCH:
                    o = (n // 2 % CPB) * CH
                    cos, sin = arr(10)[:, o:o + CH], arr(10)[:, SEQ + o:SEQ + o + CH]
                    x0, x1 = ps[:, 4 + 2 * (n % 2), :], ps[:, 5 + 2 * (n % 2), :]
                    dve.wait_ge(s("qk3_mm"), 2 * n + 2)
                    if n >= 1:
                        dve.wait_ge(s("roped"), 2 * n)
                    for k, (x, y) in enumerate(((x0, cos), (x1, sin), (x1, cos), (x0, sin))):
                        last = dve.tensor_tensor(arr(0)[:, k * CH:(k + 1) * CH], y, x, ALU.mult)
                    last.then_inc(s("rope_read"), 1)
                if n >= 1:
                    for i in range(2):
                        unit = 2 * (n - 1) + i
                        dve.wait_ge(s("roped"), unit + 1)
                        other_parts(dve, A3, unit, roped(unit), HD ** -0.5 if (n - 1) % 2 == 0 else 1.0)
            dve.wait_ge(s("lam_exp"), 1)
            link(dve.tensor_tensor(small[:, 24:25], small[:, 23:24], small[:, 22:23], ALU.subtract))
            link(dve.tensor_scalar(small[:, 25:26], small[:, 24:25], -LAMBDA_INIT, None, ALU.add))
            maxima(dve, A3)
            for c in range(NCH):
                add_to_x("a3", c)

            dve.memset(hT[:, :, 0:1], 0.0)
            for j, name in enumerate(("mu_k", "mu_r")):
                last = dve.tensor_scalar(small[:, 26 + j:27 + j], col(name), -1.0, 1.0, ALU.mult, ALU.add)
            link(last)
            for j, (name, mu) in enumerate((("wk", "mu_k"), ("wr", "mu_r"))):
                dve.tensor_scalar(arr(4)[:, 2 * j * C:(2 * j + 1) * C], w(3, name), col(mu), None, ALU.mult).then_inc(s("mixed"), 1)
                dve.tensor_scalar(arr(4)[:, (2 * j + 1) * C:(2 * j + 2) * C], w(3, name), small[:, 26 + j:27 + j], None,
                                  ALU.mult).then_inc(s("mixed"), 1)
            layernorm("b3")
            for c in range(NCH):
                dve.wait_ge(s("cm_k"), c + 1)
                dve.tensor_tensor(arr(2)[:, tok(c)], arr(1)[:, tok(c)], arr(1)[:, tok(c)], ALU.mult).then_inc(s("cm_sq"), 1)
                if c >= 1:
                    gate_out(dve, c - 1)
                    if c >= 2:
                        add_to_x("b3", c - 2)
            gate_out(dve, NCH - 1)
            add_to_x("b3", NCH - 2)
            add_to_x("b3", NCH - 1)

        @block.gpsimd
        def _(pool):
            def rsqrt(n):
                pool.wait_ge(s("var"), VAR[n])
                pool.tensor_tensor(rstd[:], var[:], mhalf[:], ALU.pow).then_inc(s("rstd"), 1)

            def zero_v(a):
                def stacks(v, dt):
                    x = v[0].rearrange("p g k n d -> p (g k n) d").rearrange("p (x n) d -> p x n d", n=SLOTS)
                    return x[:, :, :SPLIT] if dt == BF16 else x[:, :, SPLIT:]
                pool.memset(vall[:, 0:a.groups * SEQ], 0.0).then_inc(s(a.name + "_vzero"), 1)
                pool.wait_ge(s(a.name + "_vzero"), 1)
                pool.memset(stacks(group_v(a), BF16)[:, :, :, a.width:a.width + 1], 1.0)
                pool.memset(stacks(group_v32(a), F32)[:, :, :, a.width:a.width + 1], 1.0).then_inc(s(a.name + "_vzero"), 1)

            for n in range(3):
                rsqrt(n)
            for c in range(NCH):
                pool.wait_ge(s("var"), VAR[2] + c + 1)
                pool.tensor_tensor(rstd[:, 0:TPC], var[:, 0:TPC], mhalf[:, 0:TPC], ALU.pow).then_inc(s("rstd"), 1)
            pool.memset(qs[:].rearrange("p u n t -> p (u n t)"), 0.0)
            pool.memset(ks0[:].rearrange("p u n t -> p (u n t)"), 0.0)
            for n in range(3, 6):
                rsqrt(n)
            pool.wait_ge(s("out_mm"), NCH * (OUT_MM["b0"] + 1))
            pool.memset(w02[:, k1_at:k1_at + SLOTS * SEQ], 0.0).then_inc(s("stacks_clear"), 1)
            rsqrt(6)
            zero_v(A2)
            third_parts(pool, A2)
            lows(pool, A2)
            rsqrt(7)
            pool.wait_ge(s("g_used"), NCH * 2 * E + 2)
            pool.memset(w02[:, k1_at:k1_at + SLOTS * SEQ], 0.0)
            pool.memset(ks0[:].rearrange("p u n t -> p (u n t)"), 0.0).then_inc(s("stacks_clear"), 1)
            rsqrt(8)
            zero_v(A3)
            for n in range(2 * NCH):
                pool.wait_ge(s("rope_read"), n + 1)
                for i, op in enumerate((ALU.subtract, ALU.add)):
                    if n >= 2:
                        pool.wait_ge(s("a3_rest"), 2 * n + i - 3)
                    pool.tensor_tensor(roped(2 * n + i), arr(0)[:, 2 * i * CH:(2 * i + 1) * CH],
                                       arr(0)[:, (2 * i + 1) * CH:(2 * i + 2) * CH], op).then_inc(s("roped"), 1)
            third_parts(pool, A3)
            lows(pool, A3)
            rsqrt(9)


def kernel(**inputs):
    import ml_dtypes
    import concourse.bacc as bacc
    from concourse.bass_utils import run_bass_kernel_spmd

    def a(name):
        return np.asarray(inputs[name])

    def cat(parts):
        return np.ascontiguousarray(np.concatenate(parts, axis=1))

    def down(m):
        return m.reshape(-1, P, m.shape[1]).transpose(1, 0, 2).reshape(P, -1)

    arrays = {
        "x": a("L0_attn_x"),
        "wmod": np.ascontiguousarray(np.stack([a(f"L{i}_wmod") for i in range(4)])),
        "w0": cat([a("L0_attn_W_key").T, a("L0_attn_W_value").T, a("L0_attn_W_receptance").T, a("L0_attn_W_output").T,
                   a("L0_ffn_w1").T, down(a("L0_ffn_w2").T)]),
        "w1": cat([a("L1_attn_Wq").T, a("L1_attn_Wv").T, a("L1_attn_Wg").T, a("L1_attn_Wo").T, a("L1_ffn_router_w").T,
                   a("L1_ffn_expert_w").transpose(2, 0, 1).reshape(C, -1)]),
        "w2": cat([a("L2_attn_w_in").T, a("L2_attn_w_out").T, a("L2_ffn_Wg").T, a("L2_ffn_W1").transpose(2, 0, 1).reshape(C, -1),
                   a("L2_ffn_W2").transpose(2, 0, 1).reshape(C, -1), down(a("L2_ffn_W3").transpose(0, 2, 1).reshape(-1, C))]),
        "w3": cat([a("L3_attn_W_qkv").T, down(a("L3_attn_W_proj").T), a("L3_ffn_W_r").T, a("L3_ffn_W_k").T, a("L3_ffn_W_v").T]),
    }
    vectors = {
        "c": np.concatenate([a(f"L{i}_c").T for i in range(4)], axis=1), "decay": a("L0_attn_time_decay"),
        "first": a("L0_attn_time_first"), "mix_k": a("L0_attn_time_mix_k"), "mix_v": a("L0_attn_time_mix_v"),
        "mix_r": a("L0_attn_time_mix_r"), "ln1_g": a("L0_ffn_ln1_g"), "ln1_b": a("L0_ffn_ln1_b"),
        "ln2_g": a("L0_ffn_ln2_g").reshape(4, P).T, "ln2_b": a("L0_ffn_ln2_b").reshape(4, P).T, "b2": a("L0_ffn_b2"),
        "beta": np.repeat(a("L1_attn_beta"), HD), "gamma": a("L1_attn_ln_gamma"), "lnb": a("L1_attn_ln_beta"),
        "mu_r": a("L3_ffn_mu_r"), "mu_k": a("L3_ffn_mu_k"),
    }
    arrays["columns"] = cat([vectors[name].reshape(P, width) for name, width in COLUMNS])
    arrays["rows"] = cat([v.reshape(1, -1) for v in (
        a("L0_ffn_b1"), a("L1_ffn_router_b"), np.arange(E, 0, -1, dtype=np.float32), a("L3_attn_lambda_q1"),
        a("L3_attn_lambda_q2"), a("L3_attn_lambda_k1"), a("L3_attn_lambda_k2"))])
    arrays["expert_b"] = a("L1_ffn_expert_b")

    arrays["ident"] = np.eye(P, dtype=np.float32)
    inv = (1.0 / np.float32(10000.0) ** (np.arange(0, 2 * HD, 2, dtype=np.float32) / np.float32(2 * HD))).astype(np.float32)
    angle = np.tile(np.arange(SEQ, dtype=np.float32)[None, :] * inv[:, None], (HEADS, 1))
    arrays["rope"] = np.concatenate([np.cos(angle), np.sin(angle)], axis=1).astype(np.float32)
    key, query = np.arange(P)[:, None], np.arange(P)[None, :]
    arrays["masks"] = np.concatenate([np.full((P, P), MASKED), np.where(key > query, MASKED, 0.0),
                                      np.where(query > key, MASKED, 0.0)], axis=1).astype(ml_dtypes.bfloat16)
    slopes = (2.0 ** (-8.0 / HEADS * (np.arange(HEADS) + 1.0))).astype(np.float32)
    left = slopes[:, None] * np.arange(SEQ, dtype=np.float32)[None, :]
    alibi = []
    for _ in range(3):
        alibi.append(left.astype(ml_dtypes.bfloat16))
        left = left - alibi[-1].astype(np.float32)
    arrays["alibi"] = np.stack(alibi)
    heads = []
    for att in (A2, A3):
        m = np.zeros((SLOTS * att.strip, att.out_cols), np.float32)
        for sl in range(SLOTS):
            for part in range(3 if sl < SPLIT else 1):
                for d in range(att.width + 1):
                    m[sl * att.strip + part * (att.width + 1) + d, sl * (att.width + 1) + d] = 1.0
        heads += list(m.reshape(-1, P, att.out_cols))
    arrays["heads"] = np.concatenate(heads, axis=1)
    arrays["ones"] = np.ones((3, SLOTS * SEQ), ml_dtypes.bfloat16)

    nc = bacc.Bacc("TRN2", target_bir_lowering=False, num_devices=1)
    fed = {f"in_{k}": np.ascontiguousarray(v) for k, v in arrays.items()}
    d = {k: nc.dram_tensor(f"in_{k}", v.shape, mybir.dt.from_np(v.dtype), kind="ExternalInput").ap()
         for k, v in ((k, fed[f"in_{k}"]) for k in arrays)}
    out = nc.dram_tensor("out", (B, SEQ, C), F32, kind="ExternalOutput").ap()
    adaln_stack(nc, d["x"], {"wmod": d["wmod"], 0: d["w0"], 1: d["w1"], 2: d["w2"], 3: d["w3"]}, d["columns"], d["rows"],
                d["expert_b"], d["ident"], d["rope"], d["masks"], d["alibi"], d["ones"], d["heads"], out)
    return run_bass_kernel_spmd(nc, [fed], core_ids=[0]).results[0]["out"]
```
